# Optimizing a Trainium2 kernel written in Bass

```python
import numpy as np
import jax
import jax.numpy as jnp

def _softmax(x, axis=-1):
    return jax.nn.softmax(x, axis=axis)

def _gelu(x):
    return jax.nn.gelu(x, approximate=True)

def _silu(x):
    return jax.nn.silu(x)

def _sigmoid(x):
    return jax.nn.sigmoid(x)

def _layernorm(x, axis=-1, eps=1e-05):
    m = jnp.mean(x, axis=axis, keepdims=True)
    v = jnp.var(x, axis=axis, keepdims=True)
    return (x - m) / jnp.sqrt(v + eps)

def _scatter_add(tgt, idx, src, axis=0):
    return tgt.at[idx].add(src)

def _segment_sum(src, seg, n):
    return jax.ops.segment_sum(src, seg, n)
kernel_name = 'mk_flamingo_gated_d2_seqx_r8_f34046'

def setup_inputs(seed: int=0):
    np.random.seed(seed)
    _w = jnp.asarray

    def _rec_inputs():
        import jax
        import jax.numpy as jnp
        _rk = jax.random.key(seed)
        x = 7.22e-05 + 1 * jax.random.normal(jax.random.fold_in(_rk, 1), (2, 512, 128), jnp.float32)
        _lenS = 512 - jax.random.randint(jax.random.fold_in(_rk, 7), (2,), 0, max(1, 512 // 4) + 1, jnp.int32)
        _lenS2 = 77 - jax.random.randint(jax.random.fold_in(_rk, 8), (2,), 0, max(1, 77 // 4) + 1, jnp.int32)
        _ctx_1024P = jax.random.normal(jax.random.fold_in(_rk, 11), (2, 16, 128), jnp.float32)
        _ctx_1024c = jax.random.dirichlet(jax.random.fold_in(_rk, 511), 0.3 * jnp.ones((16,), jnp.float32), (2, 77))
        _ctx_1024t = jnp.einsum('bsk,bkd->bsd', _ctx_1024c, _ctx_1024P)
        _ctx_1024t = _ctx_1024t * jax.lax.rsqrt(jnp.mean(jnp.square(_ctx_1024t)) + 1e-12) * 0.953939
        ctx_1024 = -0.000514642 + 1.00011 * (_ctx_1024t + 0.3 * jax.random.normal(jax.random.fold_in(_rk, 611), (2, 77, 128), jnp.float32))
        _g = jax.random.normal(jax.random.fold_in(_rk, 9001), (2, 2), jnp.float32)
        _g = jnp.sign(_g) * jnp.maximum(jnp.abs(_g), 1.0) + (_g == 0) * 1.0
        g_xattn = _g[0]
        g_ffn = _g[1]
        return (x, ctx_1024, g_xattn, g_ffn)
    x, ctx_1024, g_xattn, g_ffn = _rec_inputs()

    def _L0_xattn_setup():
        import jax, jax.numpy as jnp
        import numpy as np
        B, L_ENC, L_DEC, D = (16, 64, 128, 128)
        key = jax.random.key(seed)
        k1, k2, k3, k4, k5, k6 = jax.random.split(key, 6)
        encoder_hc = jax.random.normal(k1, (B, L_ENC, D), dtype=jnp.float32)
        decoder_hq = jax.random.normal(k2, (B, L_DEC, D), dtype=jnp.float32)
        w_sim = jax.random.normal(k3, (3 * D,), dtype=jnp.float32) * 0.02
        b_sim = jax.random.normal(k4, (1,), dtype=jnp.float32) * 0.02
        W_qv = jax.random.normal(k5, (4 * D, D), dtype=jnp.float32) * 0.02
        b_qv = jax.random.normal(k6, (D,), dtype=jnp.float32) * 0.02
        return {'encoder_hc': encoder_hc, 'decoder_hq': decoder_hq, 'w_sim': w_sim, 'b_sim': b_sim, 'W_qv': W_qv, 'b_qv': b_qv}
    _L0_xattn_all = _L0_xattn_setup()
    _L0_xattn_in = {k: v for k, v in _L0_xattn_all.items() if k in ('w_sim', 'b_sim', 'W_qv', 'b_qv')}
    del _L0_xattn_all

    def _L0_ffn_setup():
        import jax, jax.numpy as jnp
        import numpy as np
        E = 8
        K = 2
        CAP_FACTOR = 1.0
        key = jax.random.key(seed)
        k0, k1, k2, k3 = jax.random.split(key, 4)
        B, S, M, H = (4, 256, 128, 512)
        x = jax.random.normal(k0, (B, S, M), jnp.float32)
        wg = jax.random.normal(k1, (M, E), jnp.float32) * 0.02
        w1 = jax.random.normal(k2, (E, M, H), jnp.float32) * 0.02
        b1 = jnp.zeros((E, H), jnp.float32)
        w2 = jax.random.normal(k3, (E, H, M), jnp.float32) * 0.02
        b2 = jnp.zeros((E, M), jnp.float32)
        return {'x': x, 'wg': wg, 'w1': w1, 'b1': b1, 'w2': w2, 'b2': b2}
    _L0_ffn_all = _L0_ffn_setup()
    _L0_ffn_in = {k: v for k, v in _L0_ffn_all.items() if k in ('wg', 'w1', 'b1', 'w2', 'b2')}
    del _L0_ffn_all

    def _L1_xattn_setup():
        import jax, jax.numpy as jnp
        import numpy as np
        H = 128
        NH = 16
        HD = H // NH
        DFF = 4 * H
        SCALE = HD ** (-0.5)
        EPS = 1e-05

        def _ln(x, g, b):
            m = jnp.mean(x, axis=-1, keepdims=True)
            v = jnp.var(x, axis=-1, keepdims=True)
            return (x - m) * jax.lax.rsqrt(v + EPS) * g + b

        def _heads(t, B):
            return t.reshape(B, -1, NH, HD).transpose(0, 2, 1, 3)

        def _merge(t, B):
            return t.transpose(0, 2, 1, 3).reshape(B, -1, H)

        def _attn(q, k, v):
            s = jnp.einsum('bhqd,bhkd->bhqk', q, k) * SCALE
            p = jax.nn.softmax(s, axis=-1)
            p = jnp.nan_to_num(p, nan=0.0)
            return jnp.einsum('bhqk,bhkd->bhqd', p, v)
        key = jax.random.key(seed)
        ks = jax.random.split(key, 16)
        std = (2.0 / (5 * H)) ** 0.5
        B, S, SI = (2, 256, 32)
        d = {'x': jax.random.normal(ks[0], (B, S, H), jnp.float32), 'image_features': jax.random.normal(ks[1], (B, SI, H), jnp.float32)}
        names = ['sq', 'sk', 'sv', 'so', 'cq', 'ck', 'cv', 'co']
        for i, n in enumerate(names):
            d['W_' + n] = std * jax.random.normal(ks[2 + i], (H, H), jnp.float32)
            d['b_' + n] = jnp.zeros((H,), jnp.float32)
        d['W_ff1'] = std * jax.random.normal(ks[10], (H, DFF), jnp.float32)
        d['b_ff1'] = jnp.zeros((DFF,), jnp.float32)
        d['W_ff2'] = std * jax.random.normal(ks[11], (DFF, H), jnp.float32)
        d['b_ff2'] = jnp.zeros((H,), jnp.float32)
        for n in ['ln1', 'ln2', 'ln3']:
            d['g_' + n] = jnp.ones((H,), jnp.float32)
            d['b_' + n] = jnp.zeros((H,), jnp.float32)
        return d
    _L1_xattn_all = _L1_xattn_setup()
    _L1_xattn_in = {k: v for k, v in _L1_xattn_all.items() if k in ('W_sq', 'b_sq', 'W_sk', 'b_sk', 'W_sv', 'b_sv', 'W_so', 'b_so', 'W_cq', 'b_cq', 'W_ck', 'b_ck', 'W_cv', 'b_cv', 'W_co', 'b_co', 'W_ff1', 'b_ff1', 'W_ff2', 'b_ff2', 'g_ln1', 'b_ln1', 'g_ln2', 'b_ln2', 'g_ln3', 'b_ln3')}
    del _L1_xattn_all

    def _L1_ffn_setup():
        import math
        import jax, jax.numpy as jnp
        import numpy as np
        E = 24

        def layer_norm(x, w, b, eps=1e-06):
            m = x.mean(-1, keepdims=True)
            v = x.var(-1, keepdims=True)
            return (x - m) / jnp.sqrt(v + eps) * w + b

        def top2_dispatch(x, Wg, C):
            logits = x @ Wg
            gates = jax.nn.softmax(logits, axis=-1)
            idx1 = jnp.argmax(gates, axis=-1)
            m1 = jax.nn.one_hot(idx1, E, dtype=x.dtype)
            masked = jnp.where(m1 > 0, -jnp.inf, logits)
            idx2 = jnp.argmax(masked, axis=-1)
            m2 = jax.nn.one_hot(idx2, E, dtype=x.dtype)
            loc1 = jnp.cumsum(m1, axis=0) - m1
            loc2 = jnp.cumsum(m2, axis=0) - m2 + jnp.sum(m1, axis=0, keepdims=True)
            m1 = m1 * (loc1 < C)
            m2 = m2 * (loc2 < C)
            g1 = jnp.sum(gates * m1, axis=-1)
            g2 = jnp.sum(gates * m2, axis=-1)
            denom = jnp.maximum(g1 + g2, 1e-09)
            g1, g2 = (g1 / denom, g2 / denom)
            p1 = jnp.sum(loc1 * m1, axis=-1).astype(jnp.int32)
            p2 = jnp.sum(loc2 * m2, axis=-1).astype(jnp.int32)
            c1 = g1[:, None, None] * m1[:, :, None] * jax.nn.one_hot(p1, C, dtype=x.dtype)[:, None, :]
            c2 = g2[:, None, None] * m2[:, :, None] * jax.nn.one_hot(p2, C, dtype=x.dtype)[:, None, :]
            combine = c1 + c2
            dispatch = (combine > 0).astype(x.dtype)
            return (combine, dispatch)

        def moe_apply(x, combine, dispatch, W, b):
            disp = jnp.einsum('sec,sd->ecd', dispatch, x)
            h = jnp.einsum('ecd,edf->ecf', disp, W) + b[:, None, :]
            return jnp.einsum('sec,ecf->sf', combine, h)
        b, seq, d_in, d_hid = (4, 256, 128, 512)
        ks = jax.random.split(jax.random.key(seed), 6)
        s = 0.02
        return {'x': jax.random.normal(ks[0], (b, seq, d_in), dtype=jnp.float32), 'Wg': jax.random.normal(ks[1], (d_in, E), dtype=jnp.float32) * s, 'W1': jax.random.normal(ks[2], (E, d_in, d_hid), dtype=jnp.float32) * s, 'b1': jnp.zeros((E, d_hid), dtype=jnp.float32), 'W2': jax.random.normal(ks[3], (E, d_hid, d_in), dtype=jnp.float32) * s, 'b2': jnp.zeros((E, d_in), dtype=jnp.float32), 'ln_hid_w': jnp.ones((4, d_hid), dtype=jnp.float32), 'ln_hid_b': jnp.zeros((4, d_hid), dtype=jnp.float32), 'ln_out_w': jnp.ones((d_in,), dtype=jnp.float32), 'ln_out_b': jnp.zeros((d_in,), dtype=jnp.float32)}
    _L1_ffn_all = _L1_ffn_setup()
    _L1_ffn_in = {k: v for k, v in _L1_ffn_all.items() if k in ('Wg', 'W1', 'b1', 'W2', 'b2', 'ln_hid_w', 'ln_hid_b', 'ln_out_w', 'ln_out_b')}
    del _L1_ffn_all
    return {'x': x, 'ctx_1024': ctx_1024, 'g_xattn': g_xattn, 'g_ffn': g_ffn, 'L0_xattn_w_sim': _L0_xattn_in['w_sim'], 'L0_xattn_b_sim': _L0_xattn_in['b_sim'], 'L0_xattn_W_qv': _L0_xattn_in['W_qv'], 'L0_xattn_b_qv': _L0_xattn_in['b_qv'], 'L0_ffn_wg': _L0_ffn_in['wg'], 'L0_ffn_w1': _L0_ffn_in['w1'], 'L0_ffn_b1': _L0_ffn_in['b1'], 'L0_ffn_w2': _L0_ffn_in['w2'], 'L0_ffn_b2': _L0_ffn_in['b2'], 'L1_xattn_W_sq': _L1_xattn_in['W_sq'], 'L1_xattn_b_sq': _L1_xattn_in['b_sq'], 'L1_xattn_W_sk': _L1_xattn_in['W_sk'], 'L1_xattn_b_sk': _L1_xattn_in['b_sk'], 'L1_xattn_W_sv': _L1_xattn_in['W_sv'], 'L1_xattn_b_sv': _L1_xattn_in['b_sv'], 'L1_xattn_W_so': _L1_xattn_in['W_so'], 'L1_xattn_b_so': _L1_xattn_in['b_so'], 'L1_xattn_W_cq': _L1_xattn_in['W_cq'], 'L1_xattn_b_cq': _L1_xattn_in['b_cq'], 'L1_xattn_W_ck': _L1_xattn_in['W_ck'], 'L1_xattn_b_ck': _L1_xattn_in['b_ck'], 'L1_xattn_W_cv': _L1_xattn_in['W_cv'], 'L1_xattn_b_cv': _L1_xattn_in['b_cv'], 'L1_xattn_W_co': _L1_xattn_in['W_co'], 'L1_xattn_b_co': _L1_xattn_in['b_co'], 'L1_xattn_W_ff1': _L1_xattn_in['W_ff1'], 'L1_xattn_b_ff1': _L1_xattn_in['b_ff1'], 'L1_xattn_W_ff2': _L1_xattn_in['W_ff2'], 'L1_xattn_b_ff2': _L1_xattn_in['b_ff2'], 'L1_xattn_g_ln1': _L1_xattn_in['g_ln1'], 'L1_xattn_b_ln1': _L1_xattn_in['b_ln1'], 'L1_xattn_g_ln2': _L1_xattn_in['g_ln2'], 'L1_xattn_b_ln2': _L1_xattn_in['b_ln2'], 'L1_xattn_g_ln3': _L1_xattn_in['g_ln3'], 'L1_xattn_b_ln3': _L1_xattn_in['b_ln3'], 'L1_ffn_Wg': _L1_ffn_in['Wg'], 'L1_ffn_W1': _L1_ffn_in['W1'], 'L1_ffn_b1': _L1_ffn_in['b1'], 'L1_ffn_W2': _L1_ffn_in['W2'], 'L1_ffn_b2': _L1_ffn_in['b2'], 'L1_ffn_ln_hid_w': _L1_ffn_in['ln_hid_w'], 'L1_ffn_ln_hid_b': _L1_ffn_in['ln_hid_b'], 'L1_ffn_ln_out_w': _L1_ffn_in['ln_out_w'], 'L1_ffn_ln_out_b': _L1_ffn_in['ln_out_b']}

def reference(x, ctx_1024, g_xattn, g_ffn, L0_xattn_w_sim, L0_xattn_b_sim, L0_xattn_W_qv, L0_xattn_b_qv, L0_ffn_wg, L0_ffn_w1, L0_ffn_b1, L0_ffn_w2, L0_ffn_b2, L1_xattn_W_sq, L1_xattn_b_sq, L1_xattn_W_sk, L1_xattn_b_sk, L1_xattn_W_sv, L1_xattn_b_sv, L1_xattn_W_so, L1_xattn_b_so, L1_xattn_W_cq, L1_xattn_b_cq, L1_xattn_W_ck, L1_xattn_b_ck, L1_xattn_W_cv, L1_xattn_b_cv, L1_xattn_W_co, L1_xattn_b_co, L1_xattn_W_ff1, L1_xattn_b_ff1, L1_xattn_W_ff2, L1_xattn_b_ff2, L1_xattn_g_ln1, L1_xattn_b_ln1, L1_xattn_g_ln2, L1_xattn_b_ln2, L1_xattn_g_ln3, L1_xattn_b_ln3, L1_ffn_Wg, L1_ffn_W1, L1_ffn_b1, L1_ffn_W2, L1_ffn_b2, L1_ffn_ln_hid_w, L1_ffn_ln_hid_b, L1_ffn_ln_out_w, L1_ffn_ln_out_b):
    import jax
    import jax.numpy as jnp

    def _L0_xattn_ref(encoder_hc, decoder_hq, w_sim, b_sim, W_qv, b_qv):
        import jax, jax.numpy as jnp
        import numpy as np
        B, L_ENC, L_DEC, D = (16, 64, 128, 128)
        d = encoder_hc.shape[-1]
        w1, w2, w3 = (w_sim[:d], w_sim[d:2 * d], w_sim[2 * d:])
        Sim = (encoder_hc @ w1)[:, :, None] + (decoder_hq @ w2)[:, None, :] + jnp.einsum('bid,bjd->bij', encoder_hc * w3, decoder_hq) + b_sim[0]
        A = jax.nn.softmax(Sim, axis=2)
        hq_hat = jnp.einsum('bij,bjd->bid', A, decoder_hq)
        Batt = jax.nn.softmax(jnp.max(Sim, axis=2), axis=1)
        hc_bar = jnp.einsum('bi,bid->bd', Batt, encoder_hc)[:, None, :]
        hc_hat = jnp.broadcast_to(hc_bar, encoder_hc.shape)
        feats = jnp.concatenate([encoder_hc, hq_hat, encoder_hc * hq_hat, encoder_hc * hc_hat], axis=-1)
        hcq = feats @ W_qv + b_qv
        return hcq

    def _L0_ffn_ref(x, wg, w1, b1, w2, b2):
        import jax, jax.numpy as jnp
        import numpy as np
        E = 8
        K = 2
        CAP_FACTOR = 1.0
        B, S, M = x.shape
        N = B * S
        capacity = int(CAP_FACTOR * K * N // E)
        xt = x.reshape(N, M)
        logits = xt @ wg
        scores = jax.nn.softmax(logits, axis=-1)
        topv, topi = jax.lax.top_k(scores, K)
        topv = topv / jnp.sum(topv, axis=-1, keepdims=True)
        masks = jax.nn.one_hot(topi.T, E, dtype=jnp.int32)
        flat = masks.reshape(K * N, E)
        locs = jnp.cumsum(flat, axis=0) - 1
        pos = jnp.sum(locs * flat, axis=-1).reshape(K, N).T
        valid = pos < capacity
        gate = topv * valid.astype(topv.dtype)
        pos_c = jnp.where(valid, pos, 0)
        xk = xt[:, None, :] * valid[..., None].astype(xt.dtype)
        disp = jnp.zeros((E, capacity, M), xt.dtype)
        disp = disp.at[topi, pos_c].add(xk)
        h = jax.nn.relu(jnp.einsum('ecm,emh->ech', disp, w1) + b1[:, None, :])
        y = jnp.einsum('ech,ehm->ecm', h, w2) + b2[:, None, :]
        out = jnp.sum(gate[..., None] * y[topi, pos_c], axis=1)
        return out.reshape(B, S, M)

    def _L1_xattn_ref(x, image_features, W_sq, b_sq, W_sk, b_sk, W_sv, b_sv, W_so, b_so, W_cq, b_cq, W_ck, b_ck, W_cv, b_cv, W_co, b_co, W_ff1, b_ff1, W_ff2, b_ff2, g_ln1, b_ln1, g_ln2, b_ln2, g_ln3, b_ln3):
        import jax, jax.numpy as jnp
        import numpy as np
        H = 128
        NH = 16
        HD = H // NH
        DFF = 4 * H
        SCALE = HD ** (-0.5)
        EPS = 1e-05

        def _ln(x, g, b):
            m = jnp.mean(x, axis=-1, keepdims=True)
            v = jnp.var(x, axis=-1, keepdims=True)
            return (x - m) * jax.lax.rsqrt(v + EPS) * g + b

        def _heads(t, B):
            return t.reshape(B, -1, NH, HD).transpose(0, 2, 1, 3)

        def _merge(t, B):
            return t.transpose(0, 2, 1, 3).reshape(B, -1, H)

        def _attn(q, k, v):
            s = jnp.einsum('bhqd,bhkd->bhqk', q, k) * SCALE
            p = jax.nn.softmax(s, axis=-1)
            p = jnp.nan_to_num(p, nan=0.0)
            return jnp.einsum('bhqk,bhkd->bhqd', p, v)
        B = x.shape[0]
        x = x * 0.1
        img = image_features * 0.1
        nx = _ln(x, g_ln1, b_ln1)
        q = _heads(nx @ W_sq + b_sq, B)
        k = _heads(nx @ W_sk + b_sk, B)
        v = _heads(nx @ W_sv + b_sv, B)
        so = _merge(_attn(q, k, v), B) @ W_so + b_so
        x = x + so
        nx = _ln(x, g_ln2, b_ln2)
        q = _heads(nx @ W_cq + b_cq, B)
        k = _heads(img @ W_ck + b_ck, B)
        v = _heads(img @ W_cv + b_cv, B)
        co = _merge(_attn(q, k, v), B) @ W_co + b_co
        x = x + co
        nx = _ln(x, g_ln3, b_ln3)
        ff = jax.nn.gelu(nx @ W_ff1 + b_ff1, approximate=False) @ W_ff2 + b_ff2
        x = x + ff
        return x * 10.0

    def _L1_ffn_ref(x, Wg, W1, b1, W2, b2, ln_hid_w, ln_hid_b, ln_out_w, ln_out_b):
        import math
        import jax, jax.numpy as jnp
        import numpy as np
        E = 24

        def layer_norm(x, w, b, eps=1e-06):
            m = x.mean(-1, keepdims=True)
            v = x.var(-1, keepdims=True)
            return (x - m) / jnp.sqrt(v + eps) * w + b

        def top2_dispatch(x, Wg, C):
            logits = x @ Wg
            gates = jax.nn.softmax(logits, axis=-1)
            idx1 = jnp.argmax(gates, axis=-1)
            m1 = jax.nn.one_hot(idx1, E, dtype=x.dtype)
            masked = jnp.where(m1 > 0, -jnp.inf, logits)
            idx2 = jnp.argmax(masked, axis=-1)
            m2 = jax.nn.one_hot(idx2, E, dtype=x.dtype)
            loc1 = jnp.cumsum(m1, axis=0) - m1
            loc2 = jnp.cumsum(m2, axis=0) - m2 + jnp.sum(m1, axis=0, keepdims=True)
            m1 = m1 * (loc1 < C)
            m2 = m2 * (loc2 < C)
            g1 = jnp.sum(gates * m1, axis=-1)
            g2 = jnp.sum(gates * m2, axis=-1)
            denom = jnp.maximum(g1 + g2, 1e-09)
            g1, g2 = (g1 / denom, g2 / denom)
            p1 = jnp.sum(loc1 * m1, axis=-1).astype(jnp.int32)
            p2 = jnp.sum(loc2 * m2, axis=-1).astype(jnp.int32)
            c1 = g1[:, None, None] * m1[:, :, None] * jax.nn.one_hot(p1, C, dtype=x.dtype)[:, None, :]
            c2 = g2[:, None, None] * m2[:, :, None] * jax.nn.one_hot(p2, C, dtype=x.dtype)[:, None, :]
            combine = c1 + c2
            dispatch = (combine > 0).astype(x.dtype)
            return (combine, dispatch)

        def moe_apply(x, combine, dispatch, W, b):
            disp = jnp.einsum('sec,sd->ecd', dispatch, x)
            h = jnp.einsum('ecd,edf->ecf', disp, W) + b[:, None, :]
            return jnp.einsum('sec,ecf->sf', combine, h)
        bsz, seq, d = x.shape
        H = 4
        n = seq // H
        S = bsz * n
        C = math.ceil(2 * S / E)
        xg = x.reshape(bsz, H, n, d).transpose(1, 0, 2, 3).reshape(H, S, d)

        def per_group(xf, lw, lb):
            combine, dispatch = top2_dispatch(xf, Wg, C)
            h = moe_apply(xf, combine, dispatch, W1, b1)
            h = layer_norm(h, lw, lb)
            h = jax.nn.relu(h)
            return moe_apply(h, combine, dispatch, W2, b2)
        out = jax.vmap(per_group)(xg, ln_hid_w, ln_hid_b)
        out = out.reshape(H, bsz, n, d).transpose(1, 0, 2, 3).reshape(bsz, seq, d)
        return layer_norm(out + x, ln_out_w, ln_out_b)
    x = x + jnp.tanh(g_xattn[0]) * _L0_xattn_ref(_layernorm(x, axis=-1), ctx_1024, L0_xattn_w_sim, L0_xattn_b_sim, L0_xattn_W_qv, L0_xattn_b_qv)
    x = x + jnp.tanh(g_ffn[0]) * _L0_ffn_ref(_layernorm(x, axis=-1), L0_ffn_wg, L0_ffn_w1, L0_ffn_b1, L0_ffn_w2, L0_ffn_b2)
    x = x + jnp.tanh(g_xattn[1]) * _L1_xattn_ref(_layernorm(x, axis=-1), ctx_1024, L1_xattn_W_sq, L1_xattn_b_sq, L1_xattn_W_sk, L1_xattn_b_sk, L1_xattn_W_sv, L1_xattn_b_sv, L1_xattn_W_so, L1_xattn_b_so, L1_xattn_W_cq, L1_xattn_b_cq, L1_xattn_W_ck, L1_xattn_b_ck, L1_xattn_W_cv, L1_xattn_b_cv, L1_xattn_W_co, L1_xattn_b_co, L1_xattn_W_ff1, L1_xattn_b_ff1, L1_xattn_W_ff2, L1_xattn_b_ff2, L1_xattn_g_ln1, L1_xattn_b_ln1, L1_xattn_g_ln2, L1_xattn_b_ln2, L1_xattn_g_ln3, L1_xattn_b_ln3)
    x = x + jnp.tanh(g_ffn[1]) * _L1_ffn_ref(_layernorm(x, axis=-1), L1_ffn_Wg, L1_ffn_W1, L1_ffn_b1, L1_ffn_W2, L1_ffn_b2, L1_ffn_ln_hid_w, L1_ffn_ln_hid_b, L1_ffn_ln_out_w, L1_ffn_ln_out_b)
    return x

_drawn_inputs = setup_inputs


def setup_inputs(seed=0):
    import zlib

    import numpy as np

    out = dict(_drawn_inputs(seed))
    spreads = {'g_ffn': (-1.0, 0.6),
     'L0_ffn_b1': (0.0, 0.443),
     'L0_ffn_b2': (0.0, 0.1),
     'L1_xattn_b_sq': (0.0, 0.366),
     'L1_xattn_b_sk': (0.0, 0.8),
     'L1_xattn_b_sv': (0.0, 0.1),
     'L1_xattn_b_so': (0.0, 0.1),
     'L1_xattn_b_cq': (0.0, 0.8),
     'L1_xattn_b_ck': (0.0, 0.8),
     'L1_xattn_b_cv': (0.0, 0.1),
     'L1_xattn_b_co': (0.0, 0.1),
     'L1_xattn_b_ff1': (0.0, 0.1),
     'L1_xattn_b_ff2': (0.0, 0.1),
     'L1_xattn_g_ln1': (1.0, 0.2),
     'L1_xattn_b_ln1': (0.0, 0.1),
     'L1_xattn_g_ln2': (1.0, 0.6),
     'L1_xattn_b_ln2': (0.0, 0.8),
     'L1_xattn_g_ln3': (1.0, 0.2),
     'L1_xattn_b_ln3': (0.0, 0.1),
     'L1_ffn_b1': (0.0, 0.489),
     'L1_ffn_b2': (0.0, 0.64),
     'L1_ffn_ln_hid_w': (1.0, 0.6),
     'L1_ffn_ln_hid_b': (0.0, 0.8),
     'L1_ffn_ln_out_w': (1.0, 0.2),
     'L1_ffn_ln_out_b': (0.0, 0.425)}
    factors = {'L0_ffn_w1': 3.068, 'L1_xattn_W_cq': 8.0, 'L1_xattn_W_ck': 8.0}
    for name, (base, spread) in spreads.items():
        noise = np.random.default_rng([zlib.crc32(name.encode()), seed]).standard_normal(out[name].shape)
        drawn = base * np.exp(spread * noise) if base else spread * noise
        out[name] = jnp.asarray(drawn.astype(out[name].dtype))
    for name, factor in factors.items():
        out[name] = (out[name] * factor).astype(out[name].dtype)
    return out
```

```python
from contextlib import ExitStack

import concourse.bass as bass
from concourse import mybir

F32 = mybir.dt.float32
BF16 = mybir.dt.bfloat16
U32 = mybir.dt.uint32
ALU = mybir.AluOpType
ACT = mybir.ActivationFunctionType
AX = mybir.AxisListType

P = 128
D = 128
B, SEQ = 2, 512
TB = SEQ // P
T = B * TB
N = B * SEQ
J = 77
NH, HD = 16, 8
HG = NH // 4
QK_SCALE = HD ** -0.5
E0, C0 = 8, 256
F0 = 512
E1, NG, C1 = 24, 4, 22
M1 = NG * C1
F1 = 512
KP = 96
BIG = 1e30
SKIP = 1e6
LN_EPS = 1e-5
MOE_EPS = 1e-6

V_WSIM, V_BSQ, V_BSK, V_BCQ, V_BCK, V_BFF1, V_LN1, V_LN2, V_LN3, V_B1 = 0, 3, 4, 5, 6, 7, 11, 13, 15, 17
NV = V_B1 + E0 * F0 // P
(R_QV, R_SV, R_SO, R_CV, R_CO, R_FF2, R_LNW, R_LNB) = range(8)
(W_SQ, W_SK, W_SV, W_SO, W_CQ, W_CK, W_CV, W_CO) = range(8)
AHEAD = [6, 6, 5, 5, 5, 5, 0, 0]


class Chain:

    def __init__(self, eng, sem):
        self.eng, self.sem, self.n = eng, sem, 0

    def step(self, ins):
        ins.then_inc(self.sem, 1)
        self.n += 1
        return self.n

    def wait(self, n=None):
        self.eng.wait_ge(self.sem, self.n if n is None else n)

    def link(self, ins):
        self.step(ins)
        self.wait()


def flamingo_kernel(nc, a, out):
    ctx = ExitStack()
    with ctx:
        def sb(name, shape, dt=F32):
            return ctx.enter_context(nc.sbuf_tensor(name, shape, dt))

        def sem(name):
            return ctx.enter_context(nc.semaphore(name))

        def sems(name, n):
            return [sem(f"{name}{i}") for i in range(n)]

        R0 = sb("R0", [P, 8192])
        w1_0 = R0[:, 0:4096].rearrange("p (e h) -> p e h", e=E0)
        w2_0 = R0[:, 4096:8192].rearrange("p (e m) -> p e m", e=E0 * 4)
        lnw_h = R0[:, 0:2048].rearrange("p (g f) -> p g f", g=NG)
        lnb_h = R0[:, 2048:4096].rearrange("p (g f) -> p g f", g=NG)
        geluT = R0[:, 4096:8192].rearrange("p (f t) -> p f t", f=4)
        slots1 = R0[0:M1, 4096:4096 + E1 * D].rearrange("p (e d) -> p e d", e=E1)
        yrow1 = slots1

        R1 = sb("R1", [P, 24576])

        def r1(start, n, parts=P):
            return R1[0:parts, start:start + n]

        x0 = r1(0, 1024).rearrange("p (t d) -> p t d", t=T)
        xplus = r1(1024, 1024).rearrange("p (t d) -> p t d", t=T)
        x1 = r1(2048, 1024).rearrange("p (t d) -> p t d", t=T)
        hqT = r1(3072, 1024)
        prodT = r1(4096, 1024)
        simA = r1(5120, T * J).rearrange("p (t j) -> p t j", t=T)
        simT = r1(6144, 1024, J)
        wqv = r1(7168, 512).rearrange("p (k n) -> p k n", k=4)
        w14 = r1(7680, 256).rearrange("p (b n) -> p b n", b=B)
        b2_0 = r1(8192, 1024).rearrange("p (e d) -> p e d", e=E0)
        slots0 = r1(9216, 2048).rearrange("p (a d) -> p a d", a=16)
        slots0T = r1(11264, 2048)
        hid0 = [r1(13312 + 1024 * i, 1024).rearrange("p (f c) -> p f c", f=4) for i in range(2)]
        yrow0 = r1(15360, 2048).rearrange("p (a d) -> p a d", a=16)
        got0 = r1(17408, 2048).rearrange("p (t k d) -> p t k d", t=T, k=2)
        Q9 = r1(0, 8192).bitcast(BF16).rearrange("p (h t) -> p h t", h=NH)
        K9 = r1(8192, 8192).bitcast(BF16).rearrange("p (h t) -> p h t", h=NH)
        probs = [r1(16384 + 1024 * i, 1024) for i in range(4)]
        qparts = r1(20480, 1536).bitcast(BF16).rearrange("p (i t) -> p i t", i=3)
        kparts = r1(22016, 1536).bitcast(BF16).rearrange("p (i t) -> p i t", i=3)
        qcT = r1(12288 + 10240, 1024)
        PT = r1(12288, 8192, J).rearrange("p (h t) -> p h t", h=NH)
        PC = 8 * J
        pc = [r1(12288 + 8192 + PC * i, PC).rearrange("p (h j) -> p h j", h=8) for i in range(3)]
        W1 = r1(0, 12288).rearrange("p (e f) -> p e f", e=E1)
        W2 = r1(12288, 12288).rearrange("p (e m) -> p e m", e=E1 * 4)
        got1 = r1(0, 8192).rearrange("p (t k f) -> p t k f", t=T, k=2)
        hsum = r1(8192, 4096).rearrange("p (t f) -> p t f", t=T)
        got2 = r1(0, 2048).rearrange("p (t k d) -> p t k d", t=T, k=2)

        R2 = sb("R2", [P, 2048])
        oT = [R2[:, 512 * i:512 * i + 512] for i in range(2)]
        ring = [R2[0:M1, 512 * i:512 * i + 512] for i in range(4)]

        R3 = sb("R3", [P, B * NH * J])
        kbd = R3[:, :].rearrange("p (b h j) -> p b h j", b=B, h=NH)
        slots1T = R3[:, 0:E1 * M1]
        hid1T = [R3[:, 4 * M1 * i:4 * M1 * (i + 1)].rearrange("p (f c) -> p f c", f=4) for i in range(4)]

        t1 = sb("t1", [P, T, D])
        t2 = sb("t2", [P, T, D])
        t3 = sb("t3", [P, T, D])
        xn = sb("xn", [P, T, D])
        xT = sb("xT", [P, N])
        attn = sb("attn", [P, T, D])
        attnT = sb("attnT", [P, N])
        flat = lambda tile: tile[:, :, :].rearrange("p t d -> p (t d)")
        x2, xres, xa = t1, t2, t3
        qf, kf = flat(attn), attnT[:, :]
        combT = attnT[0:E1, :]

        ident = sb("ident", [P, P])
        ones_f = sb("ones_f", [P, P])
        ones_b = sb("ones_b", [P, P], BF16)
        before = sb("before", [P, P], BF16)
        rev = sb("rev", [P, E1])
        group_row = sb("group_row", [P, T])
        head_of = sb("head_of", [P, NH])
        zeros = sb("zeros", [P, 528])
        vrow = sb("vrow", [NV, P])
        vcol = sb("vcol", [P, NV])
        bias = sb("bias", [P, 8, D])
        gates = sb("gates", [P, 4])
        tg = sb("tg", [P, 6])
        bsim = sb("bsim", [1, 1])
        wx = sb("wx", [P, 8, D])
        wg0 = sb("wg0", [P, E0])
        wg1 = sb("wg1", [P, E1])
        ff1 = sb("ff1", [P, 512])
        ff2 = sb("ff2", [P, 4, D])
        cx = sb("cx", [J, B, D])
        cxT = sb("cxT", [P, B * J])
        imgT = sb("imgT", [P, B * J])
        rT = sb("rT", [P, B * J])
        simrow = sb("simrow", [1, B * J])
        kcT = sb("kcT", [P, B * J])
        vaug = sb("vaug", [P, T, NH, HD + 1])
        vcaug = sb("vcaug", [J, B, NH, HD + 1])
        st6 = sb("st6", [P, T, 6])
        mv = sb("mv", [P, T, 2])
        var_eps = sb("var_eps", [P, 2, T])
        std = sb("std", [P, 2, T])
        rstds = sb("rstds", [P, 2, T])
        rstd, rstd2 = rstds[:, 0, :], rstds[:, 1, :]
        tmp8 = sb("tmp8", [P, T])
        tmp8b = sb("tmp8b", [P, T])
        small = sb("small", [P, 64])
        rowmax = sb("rowmax", [1, B])
        mcol = sb("mcol", [P, HG, 32])
        mneg = sb("mneg", [32, P])
        mparts = r1(23552, 768, 32).bitcast(BF16).rearrange("p (g i t) -> p g i t", g=HG, i=3)
        rden = sb("rden", [P, NH])
        rdl = sb("rdl", [P, T * E1])
        rkey = sb("rkey", [P, T * E1])
        rtmp = sb("rtmp", [P, T * E1])
        oh = [sb(f"oh{k}", [P, T * E1], BF16) for k in range(2)]
        rs = sb("rs", [P, 16, T])
        srow = [sb(f"srow{k}", [P, 2, T], U32) for k in range(2)]
        grow = [sb(f"grow{k}", [P, 2, T], U32) for k in range(2)]
        gate = [sb(f"gate{k}", [P, 2, T]) for k in range(2)]
        comb = R0[:, 7168:7168 + T * E1].rearrange("p (t e) -> p t e", t=T)
        b1_1 = R0[0:E1, 7424:7424 + F1]
        b2_1 = R0[0:E1, 7936:7936 + D]

        ps = ctx.enter_context(nc.psum_tensor("ps", [P, 8, 512], F32))
        bank = lambda i: ps[:, i, :]

        disp0_d = nc.dram_tensor("disp0_d", (E0 * C0, D), F32).ap()
        y0_d = nc.dram_tensor("y0_d", (E0 * C0, D), F32).ap()
        qk_d = nc.dram_tensor("qk_d", (2, 3, P, N), BF16).ap()
        disp1_d = nc.dram_tensor("disp1_d", (E1 * M1, D), F32).ap()
        h1_d = nc.dram_tensor("h1_d", (E1 * M1, F1), F32).ap()
        disp2_d = nc.dram_tensor("disp2_d", (E1 * M1, F1), F32).ap()
        y1_d = nc.dram_tensor("y1_d", (E1 * M1, D), F32).ap()

        pool_self, dve_self, act_self = sem("pool_self"), sem("dve_self"), sem("act_self")
        consts = sem("consts")
        ld_x, ld_cx, ld_vec, ld_gate = sem("ld_x"), sem("ld_cx"), sem("ld_vec"), sem("ld_gate")
        ld_wqv, ld_bias, ld_wx, ld_w0 = sem("ld_wqv"), sem("ld_bias"), sem("ld_wx"), sem("ld_w0")
        ld_ff, ld_hid, ld_W1, ld_W2 = sem("ld_ff"), sem("ld_hid"), sem("ld_W1"), sem("ld_W2")
        zeroed = sem("zeroed")
        ln_stats, ln_std, ln_out, ln_tp, xT_ready = (
            sem("ln_stats"), sem("ln_std"), sem("ln_out"), sem("ln_tp"), sem("xT_ready"))
        tanh_ready = sem("tanh_ready")
        cx_tp, cxT_ready, rT_ready, simrow_mm, simrow_ready = (
            sem("cx_tp"), sem("cxT_ready"), sem("rT_ready"), sem("simrow_mm"), sem("simrow_ready"))
        sim_mm, simmax, sim_sub, sim_exp, sim_norm = (
            sem("sim_mm"), sem("simmax"), sem("sim_sub"), sem("sim_exp"), sem("sim_norm"))
        mrow_tp, mrow_max, mrow_mm, batt_sub, batt_exp, batt_mm = (
            sem("mrow_tp"), sem("mrow_max"), sem("mrow_mm"), sem("batt_sub"), sem("batt_exp"), sem("batt_mm"))
        simT_tp, simT_ready, hq_mm, hqT_ready, prodT_ready, w14_ready, hcq_mm, x1_ready = (
            sem("simT_tp"), sem("simT_ready"), sem("hq_mm"), sem("hqT_ready"), sem("prodT_ready"),
            sem("w14_ready"), sem("hcq_mm"), sem("x1_ready"))
        logits_mm, route_sub, route_exp, onehot, loc_mm, rows_ready = (
            sem("logits_mm"), sem("route_sub"), sem("route_exp"), sem("onehot"), sem("loc_mm"), sem("rows_ready"))
        kc_mm, kc_ready, kbd_ready, vc_ready = sem("kc_mm"), sem("kc_ready"), sem("kbd_ready"), sem("vc_ready")
        scattered, ld_slots = sem("scattered"), sems("ld_slots", 4)
        slots0_tp, slots0T_ready, h0_mm, h0_act, h0_dve, y0_mm, y0_row, y0_wr = (
            sem("slots0_tp"), sem("slots0T_ready"), sem("h0_mm"), sem("h0_act"), sem("h0_dve"),
            sem("y0_mm"), sem("y0_row"), sem("y0_wr"))
        gathered = sems("gathered", T)
        x2_ready = sem("x2_ready")
        qk_mm, v_mm, qk_ready, qk_parts, v_ready, qk_wr = (
            sem("qk_mm"), sem("v_mm"), sem("qk_ready"), sem("qk_parts"), sem("v_ready"), sem("qk_wr"))
        ld_qk, ld_max = sems("ld_qk", HG), sems("ld_max", HG)
        s1_mm, s1_max, max_tp, max_neg, max_parts = (
            sem("s1_mm"), sem("s1_max"), sem("max_tp"), sem("max_neg"), sem("max_parts"))
        s2_mm, s2_exp, pv_mm, oT_ready, o_tp, o_norm = (
            sem("s2_mm"), sem("s2_exp"), sem("pv_mm"), sem("oT_ready"), sem("o_tp"), sem("o_norm"))
        attn_tp, attnT_ready, proj_mm, xa_ready = sem("attn_tp"), sem("attnT_ready"), sem("proj_mm"), sem("xa_ready")
        qc_mm, qc_ready, c_mm, c_sub, c_exp, c_tp, c_PT, c_pv = (
            sem("qc_mm"), sem("qc_ready"), sem("c_mm"), sem("c_sub"), sem("c_exp"), sem("c_tp"), sem("c_PT"), sem("c_pv"))
        ff_mm, ff_gelu, ff2_mm, x4_ready = sem("ff_mm"), sem("ff_gelu"), sem("ff2_mm"), sem("x4_ready")
        slots1_tp, slots1T_ready, h1_mm, h1_act, h1_dve = (
            sem("slots1_tp"), sem("slots1T_ready"), sem("h1_mm"), sem("h1_act"), sem("h1_dve"))
        ring_dma = sems("ring_dma", 4)
        comb_ready, comb_tp, combT_ready, hb_mm, hvar, hstd, hid_ready = (
            sem("comb_ready"), sem("comb_tp"), sem("combT_ready"), sem("hb_mm"), sem("hvar"), sem("hstd"),
            sem("hid_ready"))
        hid1_tp, hid1_act, hid1_dve, y1_mm, y1_act, y1_dve, y1_wr = (
            sem("hid1_tp"), sem("hid1_act"), sem("hid1_dve"), sem("y1_mm"),
            sem("y1_act"), sem("y1_dve"), sem("y1_wr"))
        ob_mm, out_ready, out_done = (
            sem("ob_mm"), sem("out_ready"), sem("out_done"))

        N_VEC, N_BIAS, N_WX = 13, 9, 10
        row = lambda v: v.rearrange("(a d) -> a d", a=1)
        block = ctx.enter_context(nc.Block())

        @block.sync
        def _(sp):
            for b in range(B):
                sp.dma_start(x0[:, b * TB:(b + 1) * TB, :], a["x"][b].rearrange("(s p) d -> p s d", p=P)).then_inc(ld_x, 16)
            sp.dma_start(cx[:, :, :], a["ctx_1024"].rearrange("b j d -> j b d")).then_inc(ld_cx, 16)
            sp.dma_start(vrow[0:3, :], a["L0_xattn_w_sim"].rearrange("(k d) -> k d", k=3)).then_inc(ld_vec, 16)
            for name, r in (("b_sq", V_BSQ), ("b_sk", V_BSK), ("b_cq", V_BCQ), ("b_ck", V_BCK),
                            ("g_ln1", V_LN1), ("b_ln1", V_LN1 + 1), ("g_ln2", V_LN2), ("b_ln2", V_LN2 + 1),
                            ("g_ln3", V_LN3), ("b_ln3", V_LN3 + 1)):
                sp.dma_start(vrow[r:r + 1, :], row(a["L1_xattn_" + name])).then_inc(ld_vec, 16)
            sp.dma_start(vrow[V_BFF1:V_BFF1 + 4, :], a["L1_xattn_b_ff1"].rearrange("(k d) -> k d", k=4)).then_inc(ld_vec, 16)
            sp.dma_start(vrow[V_B1:NV, :], a["L0_ffn_b1"].rearrange("e (k f) -> (e k) f", f=P)).then_inc(ld_vec, 16)
            sp.dma_start(gates[:, 0:2], row(a["g_xattn"]).to_broadcast([P, 2])).then_inc(ld_gate, 16)
            sp.dma_start(gates[:, 2:4], row(a["g_ffn"]).to_broadcast([P, 2])).then_inc(ld_gate, 16)
            sp.dma_start(bsim[:, :], row(a["L0_xattn_b_sim"])).then_inc(ld_gate, 16)
            sp.dma_start(wqv, a["L0_xattn_W_qv"].rearrange("(k p) n -> p k n", p=P)).then_inc(ld_wqv, 16)
            for r, name in enumerate(("L0_xattn_b_qv", "L1_xattn_b_sv", "L1_xattn_b_so", "L1_xattn_b_cv", "L1_xattn_b_co",
                                      "L1_xattn_b_ff2", "L1_ffn_ln_out_w", "L1_ffn_ln_out_b")):
                sp.dma_start(bias[:, r, :], row(a[name]).to_broadcast([P, D])).then_inc(ld_bias, 16)
            sp.dma_start(b2_0.rearrange("p e d -> p (e d)"),
                         row(a["L0_ffn_b2"].rearrange("e d -> (e d)")).to_broadcast([P, E0 * D])).then_inc(ld_bias, 16)
            sp.dma_start(wg0[:, :], a["L0_ffn_wg"]).then_inc(ld_wx, 16)
            sp.dma_start(wg1[:, :], a["L1_ffn_Wg"]).then_inc(ld_wx, 16)
            for w, name in enumerate(("sq", "sk", "sv", "so", "cq", "ck", "cv", "co")):
                sp.dma_start(wx[:, w, :], a["L1_xattn_W_" + name]).then_inc(ld_wx, 16)
            sp.wait_ge(consts, 1)
            sp.dma_start(disp0_d.rearrange("(p a) d -> p (a d)", p=P).rearrange("p (a z) -> p a z", z=512),
                         zeros[:, 0:512].unsqueeze(1).to_broadcast([P, 4, 512])).then_inc(zeroed, 16)
            sp.dma_start(w1_0, a["L0_ffn_w1"].rearrange("e m h -> m e h")).then_inc(ld_w0, 16)
            sp.dma_start(w2_0, a["L0_ffn_w2"].rearrange("e (k f) m -> f (e k) m", f=P)).then_inc(ld_w0, 16)
            sp.dma_start(ff1[:, :], a["L1_xattn_W_ff1"]).then_inc(ld_ff, 16)
            sp.dma_start(ff2[:, :, :], a["L1_xattn_W_ff2"].rearrange("(k f) m -> f k m", f=P)).then_inc(ld_ff, 16)
            z = zeros[:, :].unsqueeze(1)
            sp.dma_start(disp1_d.rearrange("r d -> (r d)").rearrange("(p a z) -> p a z", p=P, z=528),
                         z.to_broadcast([P, 4, 528])).then_inc(zeroed, 16)
            sp.dma_start(disp2_d.rearrange("r d -> (r d)").rearrange("(p a z) -> p a z", p=P, z=528),
                         z.to_broadcast([P, 16, 528])).then_inc(zeroed, 16)

            sp.wait_ge(scattered, 16 * 2 * T)
            for c in range(4):
                sp.dma_start(slots0[:, 4 * c:4 * c + 4, :],
                             disp0_d[512 * c:512 * c + 512, :].rearrange("(a p) d -> p a d", p=P)).then_inc(ld_slots[c], 16)
            for e in range(E0):
                sp.wait_ge(y0_row, e + 1)
                sp.dma_start(y0_d[C0 * e:C0 * e + C0, :].rearrange("(a p) d -> p a d", p=P),
                             yrow0[:, 2 * e:2 * e + 2, :]).then_inc(y0_wr, 16)

            sp.wait_ge(x2_ready, T)
            sp.dma_start(lnw_h, a["L1_ffn_ln_hid_w"].rearrange("g f -> (g f)").rearrange("(a d) -> a d", a=1)
                         .to_broadcast([P, NG * F1]).rearrange("p (g f) -> p g f", g=NG)).then_inc(ld_hid, 16)
            sp.dma_start(lnb_h, a["L1_ffn_ln_hid_b"].rearrange("g f -> (g f)").rearrange("(a d) -> a d", a=1)
                         .to_broadcast([P, NG * F1]).rearrange("p (g f) -> p g f", g=NG)).then_inc(ld_hid, 16)

            ones_src = ones_b[72:75, :].unsqueeze(1)
            zsrc = lambda lo: zeros[lo:KP, 0:512].bitcast(BF16).unsqueeze(1).to_broadcast([KP - lo, NH, N])
            sp.dma_start(Q9[72:KP, :, :], zsrc(72)).then_inc(ld_qk[0], 16)
            sp.dma_start(K9[75:KP, :, :], zsrc(75)).then_inc(ld_qk[0], 16)
            sp.dma_start(K9[72:75, :, :].rearrange("p h (u q) -> p (h u) q", q=P),
                         ones_src.to_broadcast([3, NH * T, P])).then_inc(ld_qk[0], 16)
            sp.wait_ge(qk_parts, 1)
            sp.dma_start(qk_d[0].rearrange("i p t -> p i t"), qparts).then_inc(qk_wr, 16)
            sp.wait_ge(qk_parts, 2)
            sp.dma_start(qk_d[1].rearrange("i p t -> p i t"), kparts).then_inc(qk_wr, 16)
            sp.wait_ge(qk_wr, 32)
            for hg in range(HG):
                for c in range(9):
                    for packed, which, part in ((Q9, 0, c // 3), (K9, 1, c % 3)):
                        src = qk_d[which, part].rearrange("(h d) t -> d h t", d=HD)[:, 4 * hg:4 * hg + 4, :]
                        sp.dma_start(packed[8 * c:8 * c + 8, 4 * hg:4 * hg + 4, :], src).then_inc(ld_qk[hg], 16)
            for hg in range(HG):
                sp.wait_ge(max_parts, hg + 1)
                for i in range(3):
                    sp.dma_start(Q9[72 + i:73 + i, 4 * hg:4 * hg + 4, :].rearrange("p h (u q) -> p (h u) q", q=P),
                                 mparts[:, hg, i, :]).then_inc(ld_max[hg], 16)

            sp.wait_ge(o_norm, 2 * HG)
            sp.dma_start(W1, a["L1_ffn_W1"].rearrange("e m h -> m e h")).then_inc(ld_W1, 16)
            sp.wait_ge(o_norm, 4 * HG)
            sp.dma_start(W2, a["L1_ffn_W2"].rearrange("e (k f) m -> f (e k) m", f=P)).then_inc(ld_W2, 16)

            sp.wait_ge(ff2_mm, 2)
            sp.dma_start(b1_1, a["L1_ffn_b1"]).then_inc(ld_hid, 16)
            sp.dma_start(b2_1, a["L1_ffn_b2"]).then_inc(ld_hid, 16)

            sp.wait_ge(scattered, 2 * 16 * 2 * T)
            for c in range(4):
                sp.dma_start(slots1[:, 6 * c:6 * c + 6, :],
                             disp1_d[6 * M1 * c:6 * M1 * (c + 1), :].rearrange("(e p) d -> p e d", p=M1)).then_inc(ld_slots[c], 16)
            for e in range(E1):
                sp.wait_ge(h1_dve if e % 2 else h1_act, e // 2 + 1)
                sp.dma_start(h1_d[M1 * e:M1 * (e + 1), :], ring[e % 4]).then_inc(ring_dma[e % 4], 16)
            sp.wait_ge(scattered, 3 * 16 * 2 * T)
            for i in range(E1 + 4):
                if i < E1:
                    if i >= 4:
                        sp.wait_ge(hid1_tp, i - 3)
                    sp.dma_start(ring[i % 4], disp2_d[M1 * i:M1 * (i + 1), :]).then_inc(ring_dma[i % 4], 16)
                if i >= 4:
                    e = i - 4
                    sp.wait_ge(y1_act if e % 2 else y1_dve, e // 2 + 1)
                    sp.dma_start(y1_d[M1 * e:M1 * (e + 1), :], yrow1[:, e, :]).then_inc(y1_wr, 16)
            for b in range(B):
                sp.wait_ge(out_ready, TB * (b + 1))
                sp.dma_start(out[b].rearrange("(s p) d -> p s d", p=P), t3[:, b * TB:(b + 1) * TB, :]).then_inc(out_done, 16)
            sp.wait_ge(out_done, 16 * B)

        @block.gpsimd
        def _(pool):
            me = Chain(pool, pool_self)
            g = nc.gpsimd
            g.memset(zeros[:, :], 0.0).then_inc(consts, 1)
            me.step(g.memset(ident[:, :], 0.0))
            me.step(g.memset(ones_f[:, :], 1.0))
            me.step(g.memset(ones_b[:, :], 1.0))
            me.step(g.memset(head_of[:, :], 1.0))
            me.link(g.memset(before[:, :], 1.0))
            me.step(g.affine_select(out=ident[:, :], in_=ident[:, :], compare_op=ALU.not_equal, fill=1.0, base=0,
                                    pattern=[[-1, P]], channel_multiplier=1))
            me.step(g.affine_select(out=before[:, :], in_=before[:, :], compare_op=ALU.is_gt, fill=0.0, base=0,
                                    pattern=[[1, P]], channel_multiplier=-1))
            me.link(g.affine_select(out=head_of[:, :], in_=head_of[:, :], compare_op=ALU.is_ge, fill=0.0, base=0,
                                    pattern=[[-HD, NH]], channel_multiplier=1))
            me.step(g.affine_select(out=head_of[:, :], in_=head_of[:, :], compare_op=ALU.is_ge, fill=0.0, base=HD - 1,
                                    pattern=[[HD, NH]], channel_multiplier=-1))
            me.step(g.iota(rev[:, :], [[-1, E1]], base=32, channel_multiplier=0, allow_small_or_imprecise_dtypes=True))
            me.step(g.iota(group_row[:, :].rearrange("p (b s) -> p b s", b=B), [[0, B], [C1, TB]], base=0,
                           channel_multiplier=0, allow_small_or_imprecise_dtypes=True))
            me.step(g.memset(vaug[:, :, :, HD], 1.0))
            g.memset(vcaug[:, :, :, HD], 1.0).then_inc(consts, 1)

            def scatter(rows, index, dst, last_row):
                for t in range(T):
                    for k in range(2):
                        g.indirect_dma_start(dst, bass.IndirectOffsetOnAxis(ap=index[:, k, t:t + 1], axis=0), rows[:, t, :],
                                             None, bounds_check=last_row, oob_is_err=False).then_inc(scattered, 16)

            def gather(into, index, src, t):
                for k in range(2):
                    g.indirect_dma_start(into[:, t, k, :], None, src,
                                         bass.IndirectOffsetOnAxis(ap=index[:, k, t:t + 1], axis=0)).then_inc(gathered[t], 16)

            pool.wait_ge(rows_ready, 1)
            pool.wait_ge(zeroed, 48)
            scatter(xn, srow[0], disp0_d, E0 * C0 - 1)
            pool.wait_ge(kc_ready, 1)
            for b in range(B):
                ins = g.tensor_tensor(kbd[:, b], kcT[:, b * J:(b + 1) * J].unsqueeze(1).to_broadcast([P, NH, J]),
                                      head_of[:, :].unsqueeze(2).to_broadcast([P, NH, J]), ALU.mult)
            ins.then_inc(kbd_ready, 1)
            pool.wait_ge(y0_wr, 16 * E0)
            for t in range(T):
                gather(got0, grow[0], y0_d, t)
            pool.wait_ge(rows_ready, 2)
            scatter(xn, srow[1], disp1_d, E1 * M1 - 1)
            for r in range(4):
                pool.wait_ge(ring_dma[r], 16 * (E1 // 4))
            for t in range(T + 3):
                if t < T:
                    gather(got1, grow[1], h1_d, t)
                if t >= 3:
                    pool.wait_ge(hid_ready, t - 2)
                    for k in range(2):
                        g.indirect_dma_start(disp2_d, bass.IndirectOffsetOnAxis(ap=srow[1][:, k, t - 3:t - 2], axis=0),
                                             hsum[:, t - 3, :], None, bounds_check=E1 * M1 - 1,
                                             oob_is_err=False).then_inc(scattered, 16)
            pool.wait_ge(y1_wr, 16 * E1)
            for t in range(T):
                gather(got2, grow[1], y1_d, t)

        @block.scalar
        def _(act):
            s = nc.scalar

            def evac_xT(i, v):
                for b in range(B):
                    act.wait_ge(ln_tp, 2 * i + b + 1)
                    dst = xT[:, b * SEQ:(b + 1) * SEQ]
                    if v is None:
                        s.copy(dst, bank(b)).then_inc(xT_ready, 1)
                    else:
                        s.activation(dst, bank(b), ACT.Identity, bias=vcol[:, v + 1:v + 2],
                                     scale=vcol[:, v:v + 1]).then_inc(xT_ready, 1)

            def std_of(i, k=1):
                act.wait_ge(ln_stats, i + 1)
                s.activation(std[:, 0:k, :], var_eps[:, 0:k, :], ACT.Sqrt).then_inc(ln_std, 1)

            act.wait_ge(ld_gate, 48)
            s.activation(tg[:, 0:4], gates[:, :], ACT.Tanh).then_inc(tanh_ready, 1)
            std_of(0)
            evac_xT(0, None)
            act.wait_ge(sim_sub, 1)
            s.activation(simA, simA, ACT.Exp).then_inc(sim_exp, 1)
            act.wait_ge(batt_sub, 1)
            s.activation(small[:, 16:24], small[:, 8:16], ACT.Exp).then_inc(batt_exp, 1)
            for b in range(B):
                act.wait_ge(simT_tp, b + 1)
                s.copy(simT[:, b * SEQ:(b + 1) * SEQ], ps[0:J, 6 + b, :]).then_inc(simT_ready, 1)
            for b in range(B):
                act.wait_ge(hq_mm, b + 1)
                s.copy(hqT[:, b * SEQ:(b + 1) * SEQ], bank(b)).then_inc(hqT_ready, 1)

            def route_exps(i, E):
                act.wait_ge(route_sub, i + 1)
                s.activation(rtmp[:, 0:T * E], rdl[:, 0:T * E], ACT.Exp)
                s.activation(rs[:, 1, :], rs[:, 0, :], ACT.Exp).then_inc(route_exp, 1)

            std_of(1)
            evac_xT(1, None)
            route_exps(0, E0)
            act.wait_ge(kc_mm, 1)
            s.activation(kcT[:, :], ps[:, 0, 0:B * J], ACT.Identity, bias=vcol[:, V_BCK:V_BCK + 1]).then_inc(kc_ready, 1)

            def evac_slots0(c):
                act.wait_ge(slots0_tp, c + 1)
                s.copy(slots0T[:, 512 * c:512 * c + 512], bank(c % 2)).then_inc(slots0T_ready, 1)

            evac_slots0(0)
            for e in range(E0):
                if e % 2 == 0 and e // 2 + 1 < 4:
                    evac_slots0(e // 2 + 1)
                act.wait_ge(h0_mm, 2 * e + 1)
                if e >= 2:
                    act.wait_ge(y0_mm, e - 1)
                for f in range(2):
                    ins = s.activation(hid0[e % 2][:, f, :], ps[:, 2 + 2 * (e % 2), f * C0:(f + 1) * C0], ACT.Relu,
                                       bias=vcol[:, V_B1 + 4 * e + f:V_B1 + 4 * e + f + 1])
                ins.then_inc(h0_act, 1)

            std_of(2, 2)
            evac_xT(2, V_LN1)
            for mm, full, parts, v, bk in ((2, qf, qparts, V_BSQ, 2), (4, kf, kparts, V_BSK, 4)):
                act.wait_ge(qk_mm, mm)
                src = ps[:, bk:bk + 2, :].rearrange("p b t -> p (b t)")
                s.activation(full, src, ACT.Identity, bias=vcol[:, v:v + 1])
                s.activation(parts[:, 0, :], src, ACT.Identity, bias=vcol[:, v:v + 1]).then_inc(qk_ready, 1)

            def evac_oT(u, produced, count):
                act.wait_ge(produced, count)
                if u >= 2:
                    act.wait_ge(o_tp, u - 1)
                s.copy(oT[u % 2], bank(6)).then_inc(oT_ready, 1)

            for st in range(8 * HG + 1):
                if st < 8 * HG:
                    for idx in (2 * st, 2 * st + 1):
                        act.wait_ge(s2_mm, idx + 1)
                        if idx >= 4:
                            act.wait_ge(pv_mm, (idx - 4) // 2 + 1)
                        s.activation(probs[idx % 4], ps[:, 2 * (idx % 2):2 * (idx % 2) + 2, :].rearrange("p b t -> p (b t)"),
                                     ACT.Exp, scale=QK_SCALE).then_inc(s2_exp, 1)
                if st >= 4 and st % 4 == 0:
                    evac_oT(st // 4 - 1, pv_mm, st)

            def evac_attnT(i):
                for b in range(B):
                    act.wait_ge(attn_tp, 2 * i + b + 1)
                    s.copy(attnT[:, b * SEQ:(b + 1) * SEQ], bank(b)).then_inc(attnT_ready, 1)

            evac_attnT(0)
            std_of(3)
            evac_xT(3, V_LN2)
            act.wait_ge(qc_mm, 2)
            s.activation(qcT, ps[:, 2:4, :].rearrange("p b t -> p (b t)"), ACT.Identity,
                         bias=vcol[:, V_BCQ:V_BCQ + 1]).then_inc(qc_ready, 1)

            def cross_exp(un):
                act.wait_ge(c_sub, un + 1)
                s.activation(pc[un % 3], pc[un % 3], ACT.Exp, scale=QK_SCALE).then_inc(c_exp, 1)

            cross_exp(0)
            for un in range(2 * T):
                if un + 1 < 2 * T:
                    cross_exp(un + 1)
                t, half = un // 2, un % 2
                for j in range(2):
                    act.wait_ge(c_tp, 2 * un + j + 1)
                    h = 8 * half + 4 * j
                    if t >= TB:
                        act.wait_ge(c_pv, h // 4 + 1)
                    s.copy(PT[:, h:h + 4, (t % TB) * P:(t % TB + 1) * P],
                           ps[0:J, 4 + j, :].rearrange("p (h q) -> p h q", h=4)).then_inc(c_PT, 1)
                if un % 8 == 7:
                    for hg in range(HG):
                        n = HG * (un // 8) + hg
                        evac_oT(2 * HG + n, c_pv, n + 1)
            evac_attnT(1)
            std_of(4)
            evac_xT(4, V_LN3)
            for b in range(B):
                for f in range(4):
                    act.wait_ge(ff_mm, 4 * b + f + 1)
                    s.activation(geluT[:, f, b * SEQ:(b + 1) * SEQ], bank(4 * b + f), ACT.Gelu,
                                 bias=vcol[:, V_BFF1 + f:V_BFF1 + f + 1]).then_inc(ff_gelu, 1)
            std_of(5)
            evac_xT(5, None)
            route_exps(1, E1)

            def evac_slots1(c):
                act.wait_ge(slots1_tp, c + 1)
                s.copy(slots1T[:, 4 * M1 * c:4 * M1 * (c + 1)], ps[:, c % 2, 0:4 * M1]).then_inc(slots1T_ready, 1)

            evac_slots1(0)
            for e in range(E1):
                if e % 4 == 0 and e // 4 + 1 < E1 // 4:
                    evac_slots1(e // 4 + 1)
                if e % 2 == 0:
                    act.wait_ge(h1_mm, e + 1)
                    if e >= 4:
                        act.wait_ge(ring_dma[e % 4], 16 * (e // 4))
                    s.copy(ring[e % 4], ps[0:M1, 2 + e % 4, :]).then_inc(h1_act, 1)
            for b in range(B):
                act.wait_ge(comb_tp, b + 1)
                s.copy(combT[:, b * SEQ:(b + 1) * SEQ], ps[0:E1, b, :]).then_inc(combT_ready, 1)
            for t in range(T):
                act.wait_ge(hvar, t + 1)
                s.activation(tmp8[:, t:t + 1], tmp8b[:, t:t + 1], ACT.Sqrt).then_inc(hstd, 1)
            for e in range(E1 + 1):
                if e < E1 and e % 2 == 0:
                    act.wait_ge(hid1_tp, e + 1)
                    if e >= 4:
                        act.wait_ge(y1_mm, e - 3)
                    s.activation(hid1T[e % 4].rearrange("p f c -> p (f c)"), ps[:, 0, 0:4 * M1],
                                 ACT.Relu).then_inc(hid1_act, 1)
                if e >= 1 and (e - 1) % 2 == 1:
                    act.wait_ge(y1_mm, e)
                    s.copy(yrow1[:, e - 1, :], ps[0:M1, 2 + (e - 1) % 4, 0:D]).then_inc(y1_act, 1)
            for b in range(B):
                half = slice(b * TB, (b + 1) * TB)
                act.wait_ge(ln_stats, 6 + b + 1)
                s.activation(std[:, 0, half], var_eps[:, 0, half], ACT.Sqrt).then_inc(ln_std, 1)

        @block.vector
        def _(dve):
            me = Chain(dve, dve_self)
            v = nc.vector

            def stats(src, count, again=False):
                for t in range(T):
                    me.step(v.bn_stats(st6[:, t, :], src[:, t, :]))
                me.wait()
                for t in range(T):
                    me.step(v.bn_aggr(mv[:, t, :], st6[:, t, :]))
                me.wait()
                k = 1
                if again:
                    k = 2
                    me.step(v.tensor_scalar(var_eps[:, 1, :], mv[:, :, 1], 0.01 + LN_EPS, LN_EPS * LN_EPS, ALU.mult, ALU.add))
                v.tensor_scalar(var_eps[:, 0, :], mv[:, :, 1], LN_EPS, None, ALU.add).then_inc(ln_stats, 1)
                dve.wait_ge(ln_std, count)
                me.link(v.reciprocal(rstds[:, 0:k, :], std[:, 0:k, :]))
                if again:
                    me.link(v.tensor_scalar(rstds[:, :, :], rstds[:, :, :], 0.1, None, ALU.mult))

            def apply(src, dst, scale, done):
                for t in range(T):
                    ins = v.tensor_scalar(dst[:, t, :], src[:, t, :], mv[:, t, 0:1], scale[:, t:t + 1],
                                          ALU.subtract, ALU.mult)
                    if done is not None:
                        ins.then_inc(done, 1)
                return ins

            dve.wait_ge(cx_tp, 1)
            me.step(v.tensor_copy(cxT[:, :], ps[:, 2, 0:B * J]))
            v.tensor_copy(vcol[:, :], ps[:, 2, B * J:B * J + NV]).then_inc(cxT_ready, 1)
            dve.wait_ge(cxT_ready, 1)
            v.tensor_scalar(rT[:, :], cxT[:, :], vcol[:, 2:3], vcol[:, 0:1], ALU.mult, ALU.add).then_inc(rT_ready, 1)
            v.tensor_scalar(imgT[:, :], cxT[:, :], 0.1, None, ALU.mult).then_inc(rT_ready, 1)
            dve.wait_ge(simrow_mm, 1)
            dve.wait_ge(ld_gate, 48)
            v.tensor_scalar(simrow[:, :], ps[0:1, 3, 0:B * J], bsim[:, 0:1], None, ALU.add).then_inc(simrow_ready, 1)
            dve.wait_ge(ld_x, 32)
            stats(x0, 1)
            apply(x0, xn, rstd, ln_out)
            dve.wait_ge(tanh_ready, 1)
            dve.wait_ge(ld_bias, 16 * N_BIAS)
            me.step(v.tensor_scalar(tg[:, 4:5], tg[:, 1:2], 10.0, None, ALU.mult))
            me.link(v.tensor_scalar(attn[:, 0, :], bias[:, R_QV, :], tg[:, 0:1], None, ALU.mult))
            me.step(v.tensor_tensor(xplus, x0, attn[:, 0:1, :].to_broadcast([P, T, D]), ALU.add))
            dve.wait_ge(sim_mm, 2)
            sim = ps[:, 2:4, 0:TB * J].rearrange("p b (t j) -> p b t j", j=J)
            mx = small[:, 0:T]
            v.tensor_reduce(mx.rearrange("p (b t) -> p b t", b=B), sim, AX.X, ALU.max).then_inc(simmax, 1)
            dve.wait_ge(simmax, 1)
            v.tensor_tensor(simA.rearrange("p (b t) j -> p b t j", b=B), sim,
                            mx.rearrange("p (b t) -> p b t", b=B).unsqueeze(3).to_broadcast([P, B, TB, J]),
                            ALU.subtract).then_inc(sim_sub, 1)
            dve.wait_ge(mrow_tp, 1)
            v.tensor_reduce(rowmax[:, :], ps[0:1, 0:2, :], AX.X, ALU.max).then_inc(mrow_max, 1)
            dve.wait_ge(mrow_mm, 1)
            v.tensor_tensor(small[:, 8:16].rearrange("p (b t) -> p b t", b=B), mx.rearrange("p (b t) -> p b t", b=B),
                            ps[:, 4, 0:B].unsqueeze(2).to_broadcast([P, B, TB]), ALU.subtract).then_inc(batt_sub, 1)
            dve.wait_ge(sim_exp, 1)
            me.link(v.tensor_reduce(small[:, 24:32], simA, AX.X, ALU.add))
            me.link(v.reciprocal(small[:, 32:40], small[:, 24:32]))
            v.tensor_tensor(simA, simA, small[:, 32:40].unsqueeze(2).to_broadcast([P, T, J]), ALU.mult).then_inc(sim_norm, 1)
            dve.wait_ge(batt_mm, 1)
            me.link(v.tensor_reduce(small[:, 40:42], ps[:, 4, 8:16].rearrange("p (b t) -> p b t", b=B), AX.X, ALU.add))
            me.link(v.reciprocal(small[:, 42:44], small[:, 40:42]))
            me.link(v.tensor_tensor(small[:, 44:46], ps[:, 5, 0:B], small[:, 42:44], ALU.mult))
            dve.wait_ge(ld_wqv, 16)
            for b in range(B):
                ins = v.scalar_tensor_tensor(out=w14[:, b, :], in0=wqv[:, 3, :], scalar=small[:, 44 + b:45 + b],
                                             in1=wqv[:, 0, :], op0=ALU.mult, op1=ALU.add)
            ins.then_inc(w14_ready, 1)
            for b in range(B):
                dve.wait_ge(hqT_ready, b + 1)
                half = slice(b * SEQ, (b + 1) * SEQ)
                v.tensor_tensor(prodT[:, half], hqT[:, half], xT[:, half], ALU.mult).then_inc(prodT_ready, 1)
            for b in range(B):
                dve.wait_ge(hcq_mm, b + 1)
                half = slice(b * TB, (b + 1) * TB)
                v.scalar_tensor_tensor(out=x1[:, half, :].rearrange("p t d -> p (t d)"), in0=bank(2 + b), scalar=tg[:, 0:1],
                                       in1=xplus[:, half, :].rearrange("p t d -> p (t d)"), op0=ALU.mult,
                                       op1=ALU.add).then_inc(x1_ready, 1)
            dve.wait_ge(x1_ready, 2)

            def route(i, E, C, logits, loc_of):
                def pte(tile):
                    return tile[:, 0:T * E].rearrange("p (t e) -> p t e", e=E)
                def over(x):
                    return x.unsqueeze(2).to_broadcast([P, T, E])
                revb = rev[:, 0:E].unsqueeze(1).to_broadcast([P, T, E])
                m2, e2, m1, km = rs[:, 0, :], rs[:, 1, :], rs[:, 2, :], rs[:, 3:5, :]
                dve.wait_ge(logits_mm, i + 1)
                me.link(v.tensor_reduce(m1, logits, AX.X, ALU.max))
                me.link(v.tensor_tensor(pte(rdl), logits, over(m1), ALU.subtract))
                me.link(v.scalar_tensor_tensor(out=pte(rkey), in0=pte(rdl), scalar=0.0, in1=revb,
                                               op0=ALU.is_equal, op1=ALU.mult))
                me.link(v.tensor_reduce(km[:, 0, :], pte(rkey), AX.X, ALU.max))
                me.link(v.tensor_tensor(pte(oh[0]), pte(rkey), over(km[:, 0, :]), ALU.is_equal))
                me.link(v.scalar_tensor_tensor(out=pte(rkey), in0=pte(oh[0]), scalar=-BIG, in1=pte(rdl),
                                               op0=ALU.mult, op1=ALU.add))
                v.tensor_reduce(m2, pte(rkey), AX.X, ALU.max).then_inc(route_sub, 1)
                dve.wait_ge(route_sub, i + 1)
                me.link(v.tensor_tensor(pte(rkey), pte(rkey), over(m2), ALU.is_equal))
                me.link(v.tensor_tensor(pte(rkey), pte(rkey), revb, ALU.mult))
                me.link(v.tensor_reduce(km[:, 1, :], pte(rkey), AX.X, ALU.max))
                v.tensor_tensor(pte(oh[1]), pte(rkey), over(km[:, 1, :]), ALU.is_equal).then_inc(onehot, 1)
                score, valid, pos, base = rs[:, 5:7, :], rs[:, 7:9, :], rs[:, 9:11, :], rs[:, 11:13, :]
                dve.wait_ge(route_exp, i + 1)
                me.link(v.tensor_reduce(rs[:, 13, :], pte(rtmp), AX.X, ALU.add))
                me.link(v.reciprocal(score[:, 0, :], rs[:, 13, :]))
                me.link(v.tensor_tensor(score[:, 1, :], score[:, 0, :], e2, ALU.mult))
                me.step(v.tensor_scalar(base, km, -float(C if i == 0 else M1), 32.0 * (C if i == 0 else M1), ALU.mult, ALU.add))
                dve.wait_ge(loc_mm, i + 1)
                for k in range(2):
                    me.link(v.tensor_tensor(pte(rkey), loc_of(k), pte(oh[k]), ALU.mult))
                    me.link(v.tensor_reduce(pos[:, k, :], pte(rkey), AX.X, ALU.add))
                me.link(v.tensor_scalar(valid, pos, float(C), None, ALU.is_lt))
                if i == 1:
                    me.link(v.tensor_tensor(base, base, group_row[:, :].unsqueeze(1).to_broadcast([P, 2, T]), ALU.add))
                else:
                    me.wait()
                skip = rs[:, 14:16, :]
                me.step(v.tensor_scalar(skip, valid, -SKIP, SKIP, ALU.mult, ALU.add))
                me.link(v.tensor_tensor(rkey[:, 0:16].rearrange("p (k t) -> p k t", k=2), pos, valid, ALU.mult))
                me.step(v.tensor_tensor(grow[i][:, :, :], rkey[:, 0:16].rearrange("p (k t) -> p k t", k=2), base, ALU.add))
                me.link(v.tensor_tensor(pos, pos, base, ALU.add))
                v.tensor_tensor(srow[i][:, :, :], pos, skip, ALU.add).then_inc(rows_ready, 1)
                g = gate[i][:, :, :]
                if i == 0:
                    me.link(v.tensor_tensor(rs[:, 13, :], score[:, 0, :], score[:, 1, :], ALU.add))
                    me.link(v.tensor_tensor(score, score, valid, ALU.mult))
                else:
                    me.link(v.tensor_tensor(score, score, valid, ALU.mult))
                    me.link(v.tensor_tensor(rs[:, 13, :], score[:, 0, :], score[:, 1, :], ALU.add))
                    me.link(v.tensor_scalar(rs[:, 13, :], rs[:, 13, :], 1e-9, None, ALU.max))
                me.link(v.reciprocal(rs[:, 2, :], rs[:, 13, :]))
                me.link(v.tensor_tensor(g, score, rs[:, 2:3, :].to_broadcast([P, 2, T]), ALU.mult))

            stats(x1, 2)
            apply(x1, xn, rstd, ln_out)
            route(0, E0, C0, ps[:, 2, 0:T * E0].rearrange("p (t e) -> p t e", e=E0),
                  lambda k: ps[:, 3 + k, 0:T * E0].rearrange("p (t e) -> p t e", e=E0))
            me.link(v.tensor_scalar(gate[0][:, :, :], gate[0][:, :, :], tg[:, 2:3], None, ALU.mult))
            dve.wait_ge(kc_mm, 2)
            v.tensor_tensor(vcaug[:, :, :, 0:HD], ps[0:J, 1, 0:B * D].rearrange("p (b h d) -> p b h d", b=B, h=NH),
                            bias[0:J, R_CV, :].rearrange("p (h d) -> p h d", h=NH).unsqueeze(1).to_broadcast([J, B, NH, HD]),
                            ALU.add).then_inc(vc_ready, 1)
            for e in range(E0 + 1):
                if e < E0:
                    dve.wait_ge(h0_mm, 2 * e + 2)
                    if e >= 2:
                        dve.wait_ge(y0_mm, e - 1)
                    for f in (2, 3):
                        ins = v.tensor_scalar(hid0[e % 2][:, f, :], ps[:, 3 + 2 * (e % 2), (f - 2) * C0:(f - 1) * C0],
                                              vcol[:, V_B1 + 4 * e + f:V_B1 + 4 * e + f + 1], 0.0, ALU.add, ALU.max)
                    ins.then_inc(h0_dve, 1)
                if e >= 1:
                    dve.wait_ge(y0_mm, e)
                    v.tensor_tensor(yrow0[:, 2 * e - 2:2 * e, :], ps[:, 6 + (e - 1) % 2, 0:2 * D].rearrange("p (a d) -> p a d", a=2),
                                    b2_0[:, e - 1:e, :].to_broadcast([P, 2, D]), ALU.add).then_inc(y0_row, 1)
            for t in range(T):
                dve.wait_ge(gathered[t], 32)
                me.step(v.scalar_tensor_tensor(out=x1[:, t, :], in0=got0[:, t, 0, :], scalar=gate[0][:, 0, t:t + 1],
                                               in1=x1[:, t, :], op0=ALU.mult, op1=ALU.add))
                me.wait()
                v.scalar_tensor_tensor(out=x2[:, t, :], in0=got0[:, t, 1, :], scalar=gate[0][:, 1, t:t + 1],
                                       in1=x1[:, t, :], op0=ALU.mult, op1=ALU.add).then_inc(x2_ready, 1)
            dve.wait_ge(x2_ready, T)

            stats(x2, 3, again=True)
            apply(x2, xn, rstd2, ln_out)
            me.link(apply(x2, xres, rstd, None))
            me.step(v.tensor_tensor(xres[:, :, :], xres[:, :, :], bias[:, R_SO:R_SO + 1, :].to_broadcast([P, T, D]), ALU.add))
            for n, full, parts in ((1, qf, qparts), (2, kf, kparts)):
                dve.wait_ge(qk_ready, n)
                me.link(v.tensor_tensor(full, full, parts[:, 0, :], ALU.subtract))
                me.link(v.tensor_copy(parts[:, 1, :], full))
                v.tensor_tensor(parts[:, 2, :], full, parts[:, 1, :], ALU.subtract).then_inc(qk_parts, 1)
            for b in range(B):
                dve.wait_ge(v_mm, b + 1)
                v.tensor_tensor(vaug[:, b * TB:(b + 1) * TB, :, 0:HD],
                                bank(6 + b).rearrange("p (t h d) -> p t h d", t=TB, h=NH),
                                bias[:, R_SV, :].rearrange("p (h d) -> p h d", h=NH).unsqueeze(1).to_broadcast([P, TB, NH, HD]),
                                ALU.add).then_inc(v_ready, 1)

            def row_max(n):
                hg, r = n // 32, n % 32
                dve.wait_ge(s1_mm, n + 1)
                col = 8 * (r % 4) + r // 4
                v.tensor_reduce(mcol[:, hg, col:col + 1], bank(4 + n % 2), AX.X, ALU.max).then_inc(s1_max, 1)

            def max_split(hg):
                dve.wait_ge(max_tp, hg + 1)
                v.tensor_scalar(mneg[:, :], ps[0:32, 7, 0:P], -1.0, None, ALU.mult).then_inc(max_neg, 1)
                dve.wait_ge(max_neg, hg + 1)
                me.link(v.tensor_copy(mparts[:, hg, 0, :], mneg[:, :]))
                me.link(v.tensor_tensor(mneg[:, :], mneg[:, :], mparts[:, hg, 0, :], ALU.subtract))
                me.link(v.tensor_copy(mparts[:, hg, 1, :], mneg[:, :]))
                v.tensor_tensor(mparts[:, hg, 2, :], mneg[:, :], mparts[:, hg, 1, :], ALU.subtract).then_inc(max_parts, 1)

            def normalize(u, hg, b):
                dve.wait_ge(o_tp, u + 1)
                o = bank(7).rearrange("p (t h c) -> p t h c", t=TB, h=4)
                me.link(v.reciprocal(rden[:, :].rearrange("p (t h) -> p t h", h=4), o[:, :, :, HD]))
                v.tensor_tensor(attn[:, b * TB:(b + 1) * TB, 32 * hg:32 * hg + 32].rearrange("p t (h d) -> p t h d", h=4),
                                o[:, :, :, 0:HD],
                                rden[:, :].rearrange("p (t h) -> p t h", h=4).unsqueeze(3).to_broadcast([P, TB, 4, HD]),
                                ALU.mult).then_inc(o_norm, 1)

            n = 0
            for n in range(32):
                row_max(n)
            max_split(0)
            n = 32
            for st in range(8 * HG + 1):
                hg, r = st // 8, st % 8
                if hg + 1 < HG:
                    if r == 6:
                        max_split(hg + 1)
                    for _ in range(AHEAD[r]):
                        row_max(n)
                        n += 1
                if st % 4 == 1 and st >= 5:
                    u = st // 4 - 1
                    normalize(u, u // 2, u % 2)
            normalize(2 * HG - 1, HG - 1, 1)
            for b in range(B):
                dve.wait_ge(proj_mm, b + 1)
                v.tensor_tensor(xa[:, b * TB:(b + 1) * TB, :].rearrange("p t d -> p (t d)"), bank(2 + b),
                                xres[:, b * TB:(b + 1) * TB, :].rearrange("p t d -> p (t d)"), ALU.add).then_inc(xa_ready, 1)
            dve.wait_ge(xa_ready, 2)

            stats(xa, 4)
            apply(xa, xn, rstd, ln_out)
            me.step(v.tensor_tensor(xres[:, :, :], xa[:, :, :], bias[:, R_CO:R_CO + 1, :].to_broadcast([P, T, D]), ALU.add))

            for un in range(2 * T):
                dve.wait_ge(c_mm, un + 1)
                bk = 2 * (un % 2)
                sc = ps[:, bk:bk + 2, 0:4 * J].rearrange("p b (h j) -> p b h j", h=4)
                m = small[:, 0:8].rearrange("p (b h) -> p b h", b=2)
                me.link(v.tensor_reduce(m, sc, AX.X, ALU.max))
                if un >= 3:
                    dve.wait_ge(c_tp, 2 * un - 4)
                v.tensor_tensor(pc[un % 3].rearrange("p (b h) j -> p b h j", b=2), sc,
                                m.unsqueeze(3).to_broadcast([P, 2, 4, J]), ALU.subtract).then_inc(c_sub, 1)
                dve.wait_ge(c_sub, un + 1)
                if un == 9:
                    for hg in range(HG):
                        normalize(2 * HG + hg, hg, 0)
            for hg in range(HG):
                normalize(3 * HG + hg, hg, 1)
            for b in range(B):
                dve.wait_ge(proj_mm, 2 + b + 1)
                v.tensor_tensor(xa[:, b * TB:(b + 1) * TB, :].rearrange("p t d -> p (t d)"), bank(2 + b),
                                xres[:, b * TB:(b + 1) * TB, :].rearrange("p t d -> p (t d)"), ALU.add).then_inc(xa_ready, 1)
            dve.wait_ge(xa_ready, 4)

            stats(xa, 5)
            apply(xa, xn, rstd, ln_out)
            me.link(v.tensor_tensor(xres[:, :, :], xa[:, :, :], bias[:, R_FF2:R_FF2 + 1, :].to_broadcast([P, T, D]), ALU.add))
            me.link(v.scalar_tensor_tensor(out=flat(t1), in0=flat(xres), scalar=tg[:, 4:5], in1=flat(x2), op0=ALU.mult, op1=ALU.add))
            x4 = t3
            for b in range(B):
                half = slice(b * TB, (b + 1) * TB)
                dve.wait_ge(ff2_mm, b + 1)
                v.scalar_tensor_tensor(out=x4[:, half, :].rearrange("p t d -> p (t d)"), in0=bank(4 * b), scalar=tg[:, 4:5],
                                       in1=t1[:, half, :].rearrange("p t d -> p (t d)"), op0=ALU.mult,
                                       op1=ALU.add).then_inc(x4_ready, 1)
            dve.wait_ge(x4_ready, 2)

            stats(x4, 6)
            apply(x4, xn, rstd, ln_out)
            lnw = bias[:, R_LNW, :]
            me.step(v.tensor_scalar(lnw, lnw, tg[:, 3:4], None, ALU.mult))
            me.link(v.tensor_scalar(bias[:, R_LNB, :], bias[:, R_LNB, :], tg[:, 3:4], None, ALU.mult))
            me.step(v.tensor_tensor(t1[:, :, :], x4[:, :, :], bias[:, R_LNB:R_LNB + 1, :].to_broadcast([P, T, D]), ALU.add))
            route(1, E1, C1, ps[:, 2, 0:T * E1].rearrange("p (t e) -> p t e", e=E1),
                  lambda k: ps[:, 3 + k, 0:T * E1].rearrange("p (t e) -> p t e", e=E1))
            ohe = [oh[k][:, :].rearrange("p (t e) -> p t e", e=E1) for k in range(2)]
            g1 = gate[1]
            me.step(v.tensor_tensor(comb[:, :, :], ohe[0], g1[:, 0, :].unsqueeze(2).to_broadcast([P, T, E1]), ALU.mult))
            kk = rkey[:, :].rearrange("p (t e) -> p t e", e=E1)
            me.link(v.tensor_tensor(kk, ohe[1], g1[:, 1, :].unsqueeze(2).to_broadcast([P, T, E1]), ALU.mult))
            v.tensor_tensor(comb[:, :, :], comb[:, :, :], kk, ALU.add).then_inc(comb_ready, 1)
            for e in range(1, E1, 2):
                dve.wait_ge(h1_mm, e + 1)
                if e >= 4:
                    dve.wait_ge(ring_dma[e % 4], 16 * (e // 4))
                v.tensor_copy(ring[e % 4], ps[0:M1, 2 + e % 4, :]).then_inc(h1_dve, 1)
            dve.wait_ge(ld_hid, 64)
            for t in range(T + 1):
                if t < T:
                    dve.wait_ge(gathered[t], 64)
                    dve.wait_ge(hb_mm, t + 1)
                    me.link(v.scalar_tensor_tensor(out=hsum[:, t, :], in0=got1[:, t, 0, :], scalar=g1[:, 0, t:t + 1],
                                                   in1=bank(2 + t % 4), op0=ALU.mult, op1=ALU.add))
                    me.link(v.scalar_tensor_tensor(out=hsum[:, t, :], in0=got1[:, t, 1, :], scalar=g1[:, 1, t:t + 1],
                                                   in1=hsum[:, t, :], op0=ALU.mult, op1=ALU.add))
                    me.link(v.bn_stats(st6[:, t, :], hsum[:, t, :]))
                    me.link(v.bn_aggr(mv[:, t, :], st6[:, t, :]))
                    v.tensor_scalar(tmp8b[:, t:t + 1], mv[:, t, 1:2], MOE_EPS, None, ALU.add).then_inc(hvar, 1)
                if t >= 1:
                    u = t - 1
                    gi = u % TB
                    dve.wait_ge(hstd, u + 1)
                    me.link(v.reciprocal(rstd[:, u:u + 1], tmp8[:, u:u + 1]))
                    me.link(v.scalar_tensor_tensor(out=got1[:, u, 0, :], in0=hsum[:, u, :], scalar=mv[:, u, 0:1],
                                                   in1=lnw_h[:, gi, :], op0=ALU.subtract, op1=ALU.mult))
                    v.scalar_tensor_tensor(out=hsum[:, u, :], in0=got1[:, u, 0, :], scalar=rstd[:, u:u + 1],
                                           in1=lnb_h[:, gi, :], op0=ALU.mult, op1=ALU.add).then_inc(hid_ready, 1)
            for e in range(E1 + 1):
                if e < E1 and e % 2 == 1:
                    dve.wait_ge(hid1_tp, e + 1)
                    if e >= 4:
                        dve.wait_ge(y1_mm, e - 3)
                    v.tensor_scalar(hid1T[e % 4].rearrange("p f c -> p (f c)"), ps[:, 1, 0:4 * M1], 0.0, None,
                                    ALU.max).then_inc(hid1_dve, 1)
                if e >= 1 and (e - 1) % 2 == 0:
                    dve.wait_ge(y1_mm, e)
                    v.tensor_copy(yrow1[:, e - 1, :], ps[0:M1, 2 + (e - 1) % 4, 0:D]).then_inc(y1_dve, 1)
            z = t2
            for t in range(T):
                dve.wait_ge(gathered[t], 96)
                if t % TB == 0:
                    dve.wait_ge(ob_mm, t // TB + 1)
                me.link(v.scalar_tensor_tensor(out=z[:, t, :], in0=got2[:, t, 0, :], scalar=g1[:, 0, t:t + 1],
                                               in1=ps[:, 6 + t // TB, (t % TB) * D:(t % TB + 1) * D], op0=ALU.mult, op1=ALU.add))
                me.link(v.scalar_tensor_tensor(out=z[:, t, :], in0=got2[:, t, 1, :], scalar=g1[:, 1, t:t + 1],
                                               in1=z[:, t, :], op0=ALU.mult, op1=ALU.add))
                me.link(v.tensor_tensor(z[:, t, :], z[:, t, :], xn[:, t, :], ALU.add))
                me.link(v.bn_stats(st6[:, t, :], z[:, t, :]))
                me.link(v.bn_aggr(mv[:, t, :], st6[:, t, :]))
                if t % TB == TB - 1:
                    half = slice(t - TB + 1, t + 1)
                    v.tensor_scalar(var_eps[:, 0, half], mv[:, half, 1], MOE_EPS, None, ALU.add).then_inc(ln_stats, 1)
            for t in range(T):
                if t % TB == 0:
                    dve.wait_ge(ln_std, 6 + t // TB + 1)
                    me.link(v.reciprocal(rstds[:, 0, t:t + TB], std[:, 0, t:t + TB]))
                me.link(v.scalar_tensor_tensor(out=z[:, t, :], in0=z[:, t, :], scalar=mv[:, t, 0:1], in1=lnw,
                                               op0=ALU.subtract, op1=ALU.mult))
                v.scalar_tensor_tensor(out=t3[:, t, :], in0=z[:, t, :], scalar=rstd[:, t:t + 1], in1=t1[:, t, :],
                                       op0=ALU.mult, op1=ALU.add).then_inc(out_ready, 1)

        @block.tensor
        def _(pe):
            m = nc.tensor

            def tp(dst, src, k):
                return m.transpose(dst, src, ident[0:k, 0:k])

            def transpose_tiles(src, ready, first, done):
                for b in range(B):
                    for s in range(TB):
                        if ready is not None:
                            pe.wait_ge(ready, first + b * TB + s + 1)
                        ins = tp(ps[:, b, s * P:(s + 1) * P], src[:, b * TB + s, :], P)
                    ins.then_inc(done, 1)

            pe.wait_ge(consts, 2)
            pe.wait_ge(ld_cx, 16)
            pe.wait_ge(ld_vec, 16 * N_VEC)
            for b in range(B):
                tp(ps[:, 2, b * J:(b + 1) * J], cx[:, b, :], J)
            tp(ps[:, 2, B * J:B * J + NV], vrow[:, :], NV).then_inc(cx_tp, 1)
            pe.wait_ge(cxT_ready, 1)
            m.matmul(ps[0:1, 3, 0:B * J], vcol[:, 1:2], cxT[:, :], start=True, stop=True).then_inc(simrow_mm, 1)
            transpose_tiles(xn, ln_out, 0, ln_tp)
            pe.wait_ge(rT_ready, 2)
            pe.wait_ge(simrow_ready, 1)
            for b in range(B):
                pe.wait_ge(xT_ready, b + 1)
                for s in range(TB):
                    o = ps[:, 2 + b, s * J:(s + 1) * J]
                    m.matmul(o, xT[:, (b * TB + s) * P:(b * TB + s + 1) * P], rT[:, b * J:(b + 1) * J], start=True, stop=False)
                    ins = m.matmul(o, ones_f[0:1, :], simrow[0:1, b * J:(b + 1) * J], start=False, stop=True)
                ins.then_inc(sim_mm, 1)
            pe.wait_ge(simmax, 1)
            for t in range(T):
                ins = tp(ps[0:1, t // TB, (t % TB) * P:(t % TB + 1) * P], small[:, t:t + 1], P)
            ins.then_inc(mrow_tp, 1)
            pe.wait_ge(mrow_max, 1)
            m.matmul(ps[:, 4, 0:B], ones_f[0:1, :], rowmax[0:1, :], start=True, stop=True).then_inc(mrow_mm, 1)
            pe.wait_ge(batt_exp, 1)
            m.matmul(ps[:, 4, 8:16], ones_f[:, :], small[:, 16:24], start=True, stop=True)
            for t in range(T):
                ins = m.matmul(ps[:, 5, t // TB:t // TB + 1], xn[:, t, :], small[:, 16 + t:17 + t],
                               start=(t % TB == 0), stop=(t % TB == TB - 1))
            ins.then_inc(batt_mm, 1)
            pe.wait_ge(sim_norm, 1)
            for t in range(T):
                ins = tp(ps[0:J, 6 + t // TB, (t % TB) * P:(t % TB + 1) * P], simA[:, t, :], P)
                if t % TB == TB - 1:
                    ins.then_inc(simT_tp, 1)
            for b in range(B):
                pe.wait_ge(simT_ready, b + 1)
                m.matmul(bank(b), cx[:, b, :], simT[:, b * SEQ:(b + 1) * SEQ], start=True, stop=True).then_inc(hq_mm, 1)
            pe.wait_ge(w14_ready, 1)
            for b in range(B):
                pe.wait_ge(prodT_ready, b + 1)
                for s in range(TB):
                    o = ps[:, 2 + b, s * P:(s + 1) * P]
                    c = slice((b * TB + s) * P, (b * TB + s + 1) * P)
                    m.matmul(o, xT[:, c], w14[:, b, :], start=True, stop=False)
                    m.matmul(o, hqT[:, c], wqv[:, 1, :], start=False, stop=False)
                    ins = m.matmul(o, prodT[:, c], wqv[:, 2, :], start=False, stop=True)
                ins.then_inc(hcq_mm, 1)

            transpose_tiles(xn, ln_out, T, ln_tp)
            pe.wait_ge(ld_wx, 16 * N_WX)
            for t in range(T):
                if t % TB == 0:
                    pe.wait_ge(xT_ready, 2 + t // TB + 1)
                ins = m.matmul(ps[:, 2, t * E0:(t + 1) * E0], xT[:, t * P:(t + 1) * P], wg0[:, :], start=True, stop=True)
            ins.then_inc(logits_mm, 1)
            pe.wait_ge(onehot, 1)
            o0 = [oh[k][:, 0:T * E0].rearrange("p (t e) -> p t e", e=E0) for k in range(2)]
            for k in range(2):
                loc = ps[:, 3 + k, 0:T * E0].rearrange("p (t e) -> p t e", e=E0)
                m.matmul(loc, before[:, :], o0[k], start=True, stop=False)
                for t in range(T - 1):
                    m.matmul(loc[:, t + 1:T, :], ones_b[:, :], o0[k][:, t:t + 1, :].to_broadcast([P, T - 1 - t, E0]),
                             start=False, stop=(k == 0 and t == T - 2))
                if k == 1:
                    for t in range(T):
                        ins = m.matmul(loc, ones_b[:, :], o0[0][:, t:t + 1, :].to_broadcast([P, T, E0]),
                                       start=False, stop=(t == T - 1))
            ins.then_inc(loc_mm, 1)
            m.matmul(ps[:, 0, 0:B * J], wx[:, W_CK, :], imgT[:, :], start=True, stop=True).then_inc(kc_mm, 1)
            for b in range(B):
                ins = m.matmul(ps[0:J, 1, b * D:(b + 1) * D], imgT[:, b * J:(b + 1) * J], wx[:, W_CV, :], start=True, stop=True)
            ins.then_inc(kc_mm, 1)

            def slots0_transposes(c):
                pe.wait_ge(ld_slots[c], 16)
                if c == 0:
                    pe.wait_ge(kc_ready, 1)
                elif c == 1:
                    pe.wait_ge(vc_ready, 1)
                else:
                    pe.wait_ge(slots0T_ready, c - 1)
                for i in range(4):
                    ins = tp(ps[:, c % 2, i * P:(i + 1) * P], slots0[:, 4 * c + i, :], P)
                ins.then_inc(slots0_tp, 1)

            slots0_transposes(0)
            pe.wait_ge(ld_w0, 32)
            for e in range(E0 + 1):
                if e < E0:
                    if e % 2 == 0 and e // 2 + 1 < 4:
                        slots0_transposes(e // 2 + 1)
                    pe.wait_ge(slots0T_ready, e // 2 + 1)
                    for f in range(4):
                        if e >= 2 and f % 2 == 0:
                            pe.wait_ge(h0_dve if f else h0_act, e - 1)
                        elif e < 2 and f == 0:
                            pe.wait_ge(rows_ready, 1)
                        ins = m.matmul(ps[:, 2 + 2 * (e % 2) + f // 2, (f % 2) * C0:(f % 2 + 1) * C0],
                                       w1_0[:, e, f * P:(f + 1) * P], slots0T[:, e * C0:(e + 1) * C0], start=True, stop=True)
                        if f % 2:
                            ins.then_inc(h0_mm, 1)
                if e >= 1:
                    q = e - 1
                    pe.wait_ge(h0_act, q + 1)
                    pe.wait_ge(h0_dve, q + 1)
                    if q >= 2:
                        pe.wait_ge(y0_row, q - 1)
                    for r in range(2):
                        for f in range(4):
                            ins = m.matmul(ps[:, 6 + q % 2, r * D:(r + 1) * D], hid0[q % 2][:, f, r * P:(r + 1) * P],
                                           w2_0[:, 4 * q + f, :], start=(f == 0), stop=(f == 3))
                    ins.then_inc(y0_mm, 1)

            transpose_tiles(xn, ln_out, 2 * T, ln_tp)
            for w, bk in ((W_SQ, 2), (W_SK, 4)):
                for b in range(B):
                    pe.wait_ge(xT_ready, 4 + b + 1)
                    m.matmul(bank(bk + b), wx[:, w, :], xT[:, b * SEQ:(b + 1) * SEQ], start=True, stop=True).then_inc(qk_mm, 1)
            for b in range(B):
                for s in range(TB):
                    ins = m.matmul(ps[:, 6 + b, s * D:(s + 1) * D], xT[:, (b * TB + s) * P:(b * TB + s + 1) * P],
                                   wx[:, W_SV, :], start=True, stop=True)
                ins.then_inc(v_mm, 1)

            def score_row_tile(n):
                hg, r = n // 32, n % 32
                b, qt, h = r // 16, r % 16 // 4, 4 * hg + r % 4
                if r == 0:
                    pe.wait_ge(ld_qk[hg], 16 * 18 + (48 if hg == 0 else 0))
                if n >= 2:
                    pe.wait_ge(s1_max, n - 1)
                q0 = b * SEQ + qt * P
                m.matmul(bank(4 + n % 2), Q9[0:KP, h, q0:q0 + P], K9[0:KP, h, b * SEQ:(b + 1) * SEQ],
                         start=True, stop=True).then_inc(s1_mm, 1)

            def max_transpose(hg, units):
                pe.wait_ge(s1_max, 32 * (hg + 1))
                if units:
                    pe.wait_ge(o_norm, units)
                tp(ps[0:32, 7, 0:P], mcol[:, hg, :], P).then_inc(max_tp, 1)

            def score_pair(idx):
                st, pair = idx // 2, idx % 2
                hg, b, kt = st // 8, st % 8 // 4, st % 4
                if idx >= 2:
                    pe.wait_ge(s2_exp, idx - 1)
                for j in range(2):
                    h = 4 * hg + 2 * pair + j
                    k0 = b * SEQ + kt * P
                    ins = m.matmul(bank(2 * (idx % 2) + j), K9[0:KP, h, k0:k0 + P], Q9[0:KP, h, b * SEQ:(b + 1) * SEQ],
                                   start=True, stop=True)
                ins.then_inc(s2_mm, 1)

            def values(st):
                hg, b, kt, u = st // 8, st % 8 // 4, st % 4, st // 4
                pe.wait_ge(s2_exp, 2 * st + 2)
                if kt == 0 and u >= 1:
                    pe.wait_ge(oT_ready, u)
                for hh in range(4):
                    ins = m.matmul(ps[32 * hh:32 * hh + HD + 1, 6, :], vaug[:, b * TB + kt, 4 * hg + hh, :],
                                   probs[(2 * st + hh // 2) % 4][:, (hh % 2) * SEQ:(hh % 2 + 1) * SEQ],
                                   start=(kt == 0), stop=(kt == TB - 1))
                ins.then_inc(pv_mm, 1)

            def out_transposes(u):
                pe.wait_ge(oT_ready, u + 1)
                if u >= 1:
                    pe.wait_ge(o_norm, u)
                for s in range(TB):
                    ins = tp(ps[:, 7, s * P:(s + 1) * P], oT[u % 2][:, s * P:(s + 1) * P], P)
                ins.then_inc(o_tp, 1)

            pe.wait_ge(qk_ready, 2)
            pe.wait_ge(v_ready, 2)
            for n in range(32):
                score_row_tile(n)
            max_transpose(0, 0)
            n = 32
            for st in range(8 * HG + 1):
                hg, r = st // 8, st % 8
                if st < 8 * HG:
                    if r == 0:
                        pe.wait_ge(ld_max[hg], 48)
                    score_pair(2 * st)
                    if hg + 1 < HG:
                        if r == 6:
                            max_transpose(hg + 1, max(0, st // 4 - 0 - 1 + (1 if st % 4 > 1 else 0)) if st >= 5 else 0)
                        for _ in range(AHEAD[r]):
                            score_row_tile(n)
                            n += 1
                    score_pair(2 * st + 1)
                if st >= 1:
                    values(st - 1)
                    if (st - 1) % 4 == 0 and st >= 5:
                        pe.wait_ge(max_neg, min(HG, (st + 1) // 8 + 1))
                        out_transposes((st - 1) // 4 - 1)
            out_transposes(2 * HG - 1)

            def project(i, w):
                pe.wait_ge(o_norm, 2 * HG * (i + 1))
                transpose_tiles(attn, None, 0, attn_tp)
                for b in range(B):
                    pe.wait_ge(attnT_ready, 2 * i + b + 1)
                    for s in range(TB):
                        ins = m.matmul(ps[:, 2 + b, s * D:(s + 1) * D], attnT[:, (b * TB + s) * P:(b * TB + s + 1) * P],
                                       wx[:, w, :], start=True, stop=True)
                    ins.then_inc(proj_mm, 1)

            project(0, W_SO)

            transpose_tiles(xn, ln_out, 3 * T, ln_tp)
            for b in range(B):
                pe.wait_ge(xT_ready, 6 + b + 1)
                m.matmul(bank(2 + b), wx[:, W_CQ, :], xT[:, b * SEQ:(b + 1) * SEQ], start=True, stop=True).then_inc(qc_mm, 1)
            pe.wait_ge(qc_ready, 1)
            pe.wait_ge(kbd_ready, 1)

            def cross_scores(un):
                t, half = un // 2, un % 2
                if un >= 2:
                    pe.wait_ge(c_sub, un - 1)
                for j in range(2):
                    h = 8 * half + 4 * j
                    ins = m.matmul(ps[:, 2 * (un % 2) + j, 0:4 * J], qcT[:, t * P:(t + 1) * P],
                                   kbd[:, t // TB, h:h + 4, :].rearrange("p h j -> p (h j)"), start=True, stop=True)
                ins.then_inc(c_mm, 1)

            cross_scores(0)
            cross_scores(1)
            for un in range(2 * T):
                pe.wait_ge(c_exp, un + 1)
                for j in range(2):
                    if un >= 1:
                        pe.wait_ge(c_PT, 2 * un - 1 + j)
                    for i in range(4):
                        ins = tp(ps[0:J, 4 + j, i * P:(i + 1) * P], pc[un % 3][:, 4 * j + i, :], P)
                    ins.then_inc(c_tp, 1)
                if un + 2 < 2 * T:
                    cross_scores(un + 2)
                if un % 8 == 7:
                    b = un // 8
                    pe.wait_ge(c_PT, 16 * (b + 1))
                    for hg in range(HG):
                        u = 2 * HG + HG * b + hg
                        pe.wait_ge(oT_ready, u)
                        for hh in range(4):
                            ins = m.matmul(ps[32 * hh:32 * hh + HD + 1, 6, :], vcaug[:, b, 4 * hg + hh, :], PT[:, 4 * hg + hh, :],
                                           start=True, stop=True)
                        ins.then_inc(c_pv, 1)
                        out_transposes(u)
            project(1, W_CO)

            transpose_tiles(xn, ln_out, 4 * T, ln_tp)
            pe.wait_ge(ld_ff, 32)
            for b in range(B):
                pe.wait_ge(xT_ready, 8 + b + 1)
                for f in range(4):
                    if b == 0 and f == 1:
                        pe.wait_ge(xT_ready, 10)
                    m.matmul(bank(4 * b + f), ff1[:, f * P:(f + 1) * P], xT[:, b * SEQ:(b + 1) * SEQ],
                             start=True, stop=True).then_inc(ff_mm, 1)
            for b in range(B):
                pe.wait_ge(ff_gelu, 4 * (b + 1))
                for s in range(TB):
                    for f in range(4):
                        ins = m.matmul(ps[:, 4 * b, s * D:(s + 1) * D], geluT[:, f, (b * TB + s) * P:(b * TB + s + 1) * P],
                                       ff2[:, f, :], start=(f == 0), stop=(f == 3))
                ins.then_inc(ff2_mm, 1)

            transpose_tiles(xn, ln_out, 5 * T, ln_tp)
            for t in range(T):
                if t % TB == 0:
                    pe.wait_ge(xT_ready, 10 + t // TB + 1)
                ins = m.matmul(ps[:, 2, t * E1:(t + 1) * E1], xT[:, t * P:(t + 1) * P], wg1[:, :], start=True, stop=True)
            ins.then_inc(logits_mm, 1)
            pe.wait_ge(onehot, 2)
            o1 = [oh[k][:, :].rearrange("p (t e) -> p t e", e=E1) for k in range(2)]
            for k in range(2):
                loc = ps[:, 3 + k, 0:T * E1].rearrange("p (t e) -> p t e", e=E1)
                m.matmul(loc, before[:, :], o1[k], start=True, stop=False)
                m.matmul(loc[:, TB:T, :], ones_b[:, :], o1[k][:, 0:TB, :], start=False, stop=(k == 0))
                if k == 1:
                    for dst in (slice(0, TB), slice(TB, T)):
                        for src in (slice(0, TB), slice(TB, T)):
                            ins = m.matmul(loc[:, dst, :], ones_b[:, :], o1[0][:, src, :], start=False,
                                           stop=(dst.start == TB and src.start == TB))
            ins.then_inc(loc_mm, 1)

            def slots1_transposes(c):
                for q in range((4 * c) // 6, (4 * c + 3) // 6 + 1):
                    pe.wait_ge(ld_slots[q], 32)
                if c >= 2:
                    pe.wait_ge(slots1T_ready, c - 1)
                for i in range(4):
                    ins = tp(ps[:, c % 2, i * M1:(i + 1) * M1], slots1[:, 4 * c + i, :], M1)
                ins.then_inc(slots1_tp, 1)

            slots1_transposes(0)
            pe.wait_ge(rows_ready, 2)
            pe.wait_ge(ld_W1, 16)
            for e in range(E1):
                if e % 4 == 0 and e // 4 + 1 < E1 // 4:
                    slots1_transposes(e // 4 + 1)
                pe.wait_ge(slots1T_ready, e // 4 + 1)
                if e >= 4:
                    pe.wait_ge(h1_dve if e % 2 else h1_act, (e - 4) // 2 + 1)
                m.matmul(ps[0:M1, 2 + e % 4, :], slots1T[:, e * M1:(e + 1) * M1], W1[:, e, :],
                         start=True, stop=True).then_inc(h1_mm, 1)
            pe.wait_ge(comb_ready, 1)
            pe.wait_ge(slots1T_ready, 6)
            for t in range(T):
                ins = tp(ps[0:E1, t // TB, (t % TB) * P:(t % TB + 1) * P], comb[:, t, :], P)
                if t % TB == TB - 1:
                    ins.then_inc(comb_tp, 1)
            pe.wait_ge(ld_hid, 64)
            pe.wait_ge(h1_act, E1 // 2)
            pe.wait_ge(h1_dve, E1 // 2)
            pe.wait_ge(combT_ready, 2)
            for t in range(T):
                ins = m.matmul(ps[:, 6 + t // TB, (t % TB) * D:(t % TB + 1) * D], combT[:, t * P:(t + 1) * P], b2_1[:, :],
                               start=True, stop=True)
                if t % TB == TB - 1:
                    ins.then_inc(ob_mm, 1)
            for t in range(T):
                if t >= 4:
                    pe.wait_ge(hvar, t - 3)
                m.matmul(bank(2 + t % 4), combT[:, t * P:(t + 1) * P], b1_1[:, :], start=True, stop=True).then_inc(hb_mm, 1)
            pe.wait_ge(hid_ready, T)
            pe.wait_ge(ld_W2, 16)
            for e in range(E1 + 1):
                if e < E1:
                    pe.wait_ge(ring_dma[e % 4], 16 * (E1 // 4 + e // 4 + 1))
                    if e >= 2:
                        pe.wait_ge(hid1_dve if e % 2 else hid1_act, (e - 2) // 2 + 1)
                    for f in range(4):
                        ins = tp(ps[:, e % 2, f * M1:(f + 1) * M1], ring[e % 4][:, f * P:(f + 1) * P], M1)
                    ins.then_inc(hid1_tp, 1)
                if e >= 1:
                    q = e - 1
                    pe.wait_ge(hid1_dve if q % 2 else hid1_act, q // 2 + 1)
                    if q >= 4:
                        pe.wait_ge(y1_act if q % 2 else y1_dve, (q - 4) // 2 + 1)
                    for f in range(4):
                        ins = m.matmul(ps[0:M1, 2 + q % 4, 0:D], hid1T[q % 4][:, f, :], W2[:, 4 * q + f, :],
                                       start=(f == 0), stop=(f == 3))
                    ins.then_inc(y1_mm, 1)


def kernel(**inputs):
    import numpy as _np
    import concourse.bacc as _bacc
    from concourse import mybir as _mybir
    from concourse.bass_utils import run_bass_kernel_spmd as _run

    nc = _bacc.Bacc("TRN2", target_bir_lowering=False, num_devices=1)
    arrays, args = {}, {}
    for name, value in inputs.items():
        v = _np.ascontiguousarray(value)
        arrays[f"in_{name}_dram"] = v
        args[name] = nc.dram_tensor(f"in_{name}_dram", v.shape, _mybir.dt.from_np(v.dtype), kind="ExternalInput").ap()
    out = nc.dram_tensor("out_0_dram", (2, 512, 128), _mybir.dt.float32, kind="ExternalOutput").ap()
    flamingo_kernel(nc, args, out)
    r = _run(nc, [arrays], core_ids=[0])
    return r.results[0]["out_0_dram"]
```

```python
from contextlib import ExitStack

import concourse.bass as bass
from concourse import mybir

F32 = mybir.dt.float32
BF16 = mybir.dt.bfloat16
U32 = mybir.dt.uint32
ALU = mybir.AluOpType
ACT = mybir.ActivationFunctionType
AX = mybir.AxisListType

P = 128
D = 128
B, SEQ = 2, 512
TB = SEQ // P
T = B * TB
N = B * SEQ
J = 77
NH, HD = 16, 8
HG = NH // 4
QK_SCALE = HD ** -0.5
E0, C0 = 8, 256
F0 = 512
E1, NG, C1 = 24, 4, 22
M1 = NG * C1
CG = E1 * C1
F1 = 512
KP = 96
BIG = 1e30
SKIP = 1e6
LN_EPS = 1e-5
MOE_EPS = 1e-6

V_BSQ, V_BSK, V_BCQ, V_BCK, V_BFF1, V_LN1, V_LN2, V_LN3, V_B1 = 0, 1, 2, 3, 4, 8, 10, 12, 14
NV = V_B1 + E0 * F0 // P
(R_QV, R_SV, R_SO, R_CV, R_CO, R_FF2, R_LNW, R_LNB) = range(8)
(W_SQ, W_SK, W_SV, W_SO, W_CQ, W_CK, W_CV, W_CO) = range(8)
MU = 4 * 8
LEAD = 44


class Chain:

    def __init__(self, eng, sem):
        self.eng, self.sem, self.n = eng, sem, 0

    def step(self, ins):
        ins.then_inc(self.sem, 1)
        self.n += 1
        return self.n

    def wait(self, n=None):
        self.eng.wait_ge(self.sem, self.n if n is None else n)

    def link(self, ins):
        self.step(ins)
        self.wait()


def flamingo_kernel(nc, a, out):
    ctx = ExitStack()
    with ctx:
        def sb(name, shape, dt=F32):
            return ctx.enter_context(nc.sbuf_tensor(name, shape, dt))

        def sem(name):
            return ctx.enter_context(nc.semaphore(name))

        def sems(name, n):
            return [sem(f"{name}{i}") for i in range(n)]

        R0 = sb("R0", [P, 8192])
        w1_0 = R0[:, 0:4096].rearrange("p (e h) -> p e h", e=E0)
        w2_0 = R0[:, 4096:8192].rearrange("p (e m) -> p e m", e=E0 * 4)
        lnw_h = R0[:, 0:2048].rearrange("p (g f) -> p g f", g=NG)
        lnb_h = R0[:, 2048:4096].rearrange("p (g f) -> p g f", g=NG)
        geluT = R0[:, 4096:8192].rearrange("p (f t) -> p f t", f=4)
        yparts = R0[:, 4096:5632].bitcast(BF16).rearrange("p (i t d) -> p i t d", i=3, t=T)
        slot1h = [R0[:, 5632 + CG // 2 * i:5632 + CG // 2 * (i + 1)].bitcast(BF16) for i in range(4)]
        yrow1 = R0[0:M1, 4096:4096 + E1 * D].rearrange("p (e d) -> p e d", e=E1)

        R1 = sb("R1", [P, 24576])

        def r1(start, n, parts=P):
            return R1[0:parts, start:start + n]

        x0 = r1(0, 1024).rearrange("p (t d) -> p t d", t=T)
        xplus = r1(1024, 1024).rearrange("p (t d) -> p t d", t=T)
        x1 = r1(2048, 1024).rearrange("p (t d) -> p t d", t=T)
        hqT = r1(3072, 1024)
        prodT = r1(4096, 1024)
        simA = r1(5120, T * J).rearrange("p (t j) -> p t j", t=T)
        simT = r1(6144, 1024, J)
        wqv = r1(7168, 512).rearrange("p (k n) -> p k n", k=4)
        w14 = r1(7680, 256).rearrange("p (b n) -> p b n", b=B)
        b2_0 = r1(8192, 1024).rearrange("p (e d) -> p e d", e=E0)
        slots0 = r1(9216, 2048).rearrange("p (a d) -> p a d", a=16)
        slots0T = r1(11264, 2048)
        hid0 = [r1(13312 + 1024 * i, 1024).rearrange("p (f c) -> p f c", f=4) for i in range(2)]
        yrow0 = r1(15360, 2048).rearrange("p (a d) -> p a d", a=16)
        got0 = r1(17408, 2048).rearrange("p (t k d) -> p t k d", t=T, k=2)
        Q9 = r1(0, 8192).bitcast(BF16).rearrange("p (h t) -> p h t", h=NH)
        K9 = r1(8192, 8192).bitcast(BF16).rearrange("p (h t) -> p h t", h=NH)
        probs = [r1(16384 + 1024 * i, 1024) for i in range(4)]
        qparts = r1(20480, 1536).bitcast(BF16).rearrange("p (i t) -> p i t", i=3)
        kparts = r1(22016, 1536).bitcast(BF16).rearrange("p (i t) -> p i t", i=3)
        qcT = r1(16384 + 2048, 1024)
        PT = [r1(8192 * b, 8192, J).rearrange("p (h t) -> p h t", h=NH) for b in range(B)]
        PC = 8 * J
        pc = [r1(16384 + PC * i, PC).rearrange("p (h j) -> p h j", h=8) for i in range(3)]
        W1 = r1(0, 12288).rearrange("p (e f) -> p e f", e=E1)
        W2 = r1(12288, 12288).rearrange("p (e m) -> p e m", e=E1 * 4)
        got1 = r1(0, 8192).rearrange("p (t k f) -> p t k f", t=T, k=2)
        hsum = r1(8192, 4096).rearrange("p (t f) -> p t f", t=T)
        got2 = r1(0, 2048).rearrange("p (t k d) -> p t k d", t=T, k=2)

        R2 = sb("R2", [P, 2048])
        oT = [R2[:, 512 * i:512 * i + 512] for i in range(2)]
        slot_iota = R2[:, 1024:1024 + CG]
        ring = [R2[0:M1, 512 * i:512 * i + 512] for i in range(4)]

        R3 = sb("R3", [P, B * NH * J])
        kbd = R3[:, :].rearrange("p (b h j) -> p b h j", b=B, h=NH)
        slots1T = R3[:, 0:E1 * M1]
        hid1T = [R3[:, 4 * M1 * i:4 * M1 * (i + 1)].rearrange("p (f c) -> p f c", f=4) for i in range(4)]

        t1 = sb("t1", [P, T, D])
        t2 = sb("t2", [P, T, D])
        t3 = sb("t3", [P, T, D])
        xn = sb("xn", [P, T, D])
        xT = sb("xT", [P, N])
        attn = sb("attn", [P, T, D])
        attnT = sb("attnT", [P, N])
        flat = lambda tile: tile[:, :, :].rearrange("p t d -> p (t d)")
        x2, xres, xa = t1, t2, t3
        qf, kf = flat(attn), attnT[:, :]
        combT = attnT[0:E1, :]

        ident = sb("ident", [P, P])
        ones_f = sb("ones_f", [P, P])
        ones_b = sb("ones_b", [P, P], BF16)
        before = sb("before", [P, P], BF16)
        rev = sb("rev", [P, E1])
        group_row = sb("group_row", [P, T])
        head_of = sb("head_of", [P, NH])
        zeros = sb("zeros", [P, 528])
        wsim_row = sb("wsim_row", [3, P])
        wsim = sb("wsim", [P, 3])
        vrow = sb("vrow", [NV, P])
        vrow_qk = sb("vrow_qk", [2, P])
        wx_qk = sb("wx_qk", [P, 2, P])
        vcol = sb("vcol", [P, NV])
        bias = sb("bias", [P, 8, D])
        gates = sb("gates", [P, 4])
        tg = sb("tg", [P, 6])
        bsim = sb("bsim", [1, 1])
        wx = sb("wx", [P, 8, D])
        wg0 = sb("wg0", [P, E0])
        wg1 = sb("wg1", [P, E1])
        ff1 = sb("ff1", [P, 512])
        ff2 = sb("ff2", [P, 4, D])
        cx = sb("cx", [J, B, D])
        cxT = sb("cxT", [P, B * J])
        imgT = sb("imgT", [P, B * J])
        rT = sb("rT", [P, B * J])
        simrow = sb("simrow", [1, B * J])
        kcT = sb("kcT", [P, B * J])
        vaug = sb("vaug", [P, T, NH, HD + 1])
        vcaug = sb("vcaug", [J, B, NH, HD + 1])
        st6 = sb("st6", [P, T, 6])
        mv = sb("mv", [P, T, 2])
        var_eps = sb("var_eps", [P, 2, T])
        std = sb("std", [P, 2, T])
        rstds = sb("rstds", [P, 2, T])
        rstd, rstd2 = rstds[:, 0, :], rstds[:, 1, :]
        tmp8 = sb("tmp8", [P, T])
        tmp8b = sb("tmp8b", [P, T])
        small = sb("small", [P, 64])
        rowmax = sb("rowmax", [1, B])
        mcol = sb("mcol", [P, HG, MU])
        mneg = sb("mneg", [MU, P])
        mparts = R0[0:MU, 4096:4096 + HG * 3 * P // 2].bitcast(BF16).rearrange("p (g i c) -> p g i c", g=HG, i=3)
        rden = sb("rden", [P, NH])
        rdl = sb("rdl", [P, T * E1])
        rkey = sb("rkey", [P, T * E1])
        rtmp = sb("rtmp", [P, T * E1])
        oh = [sb(f"oh{k}", [P, T * E1], BF16) for k in range(2)]
        rs = sb("rs", [P, 16, T])
        srow = [sb(f"srow{k}", [P, 2, T], U32) for k in range(2)]
        grow = [sb(f"grow{k}", [P, 2, T], U32) for k in range(2)]
        gate = [sb(f"gate{k}", [P, 2, T]) for k in range(2)]
        comb = R0[:, 7168:7168 + T * E1].rearrange("p (t e) -> p t e", t=T)
        b1_1 = R0[0:E1, 7424:7424 + F1]
        b2_1 = R0[0:E1, 7936:7936 + D]

        ps = ctx.enter_context(nc.psum_tensor("ps", [P, 8, 512], F32))
        bank = lambda i: ps[:, i, :]

        disp0_d = nc.dram_tensor("disp0_d", (E0 * C0, D), F32).ap()
        y0_d = nc.dram_tensor("y0_d", (E0 * C0, D), F32).ap()
        qk_d = nc.dram_tensor("qk_d", (2, 3, P, N), BF16).ap()
        h1_d = nc.dram_tensor("h1_d", (E1 * M1, F1), F32).ap()
        disp2_d = nc.dram_tensor("disp2_d", (E1 * M1, F1), F32).ap()
        y1_d = nc.dram_tensor("y1_d", (E1 * M1, D), F32).ap()

        pool_self, dve_self, act_self = sem("pool_self"), sem("dve_self"), sem("act_self")
        consts = sem("consts")
        ld_x, ld_cx, ld_vec, ld_gate = sem("ld_x"), sem("ld_cx"), sem("ld_vec"), sem("ld_gate")
        ld_wqv, ld_bias, ld_wx, ld_w0 = sem("ld_wqv"), sem("ld_bias"), sem("ld_wx"), sem("ld_w0")
        ld_ff, ld_hid, ld_W1, ld_W2 = sem("ld_ff"), sem("ld_hid"), sem("ld_W1"), sem("ld_W2")
        zeroed = sem("zeroed")
        ln_stats, ln_std, ln_out, ln_tp, xT_ready = (
            sem("ln_stats"), sem("ln_std"), sem("ln_out"), sem("ln_tp"), sem("xT_ready"))
        tanh_ready, vcol_ready = sem("tanh_ready"), sem("vcol_ready")
        cx_tp, cxT_ready, rT_ready, simrow_mm, simrow_ready = (
            sem("cx_tp"), sem("cxT_ready"), sem("rT_ready"), sem("simrow_mm"), sem("simrow_ready"))
        sim_mm, simmax, sim_sub, sim_exp, sim_norm = (
            sem("sim_mm"), sem("simmax"), sem("sim_sub"), sem("sim_exp"), sem("sim_norm"))
        mrow_tp, mrow_max, mrow_mm, batt_sub, batt_exp, batt_mm = (
            sem("mrow_tp"), sem("mrow_max"), sem("mrow_mm"), sem("batt_sub"), sem("batt_exp"), sem("batt_mm"))
        simT_tp, simT_ready, hq_mm, hqT_ready, prodT_ready, w14_ready, hcq_mm, x1_ready = (
            sem("simT_tp"), sem("simT_ready"), sem("hq_mm"), sem("hqT_ready"), sem("prodT_ready"),
            sem("w14_ready"), sem("hcq_mm"), sem("x1_ready"))
        logits_mm, route_sub, route_exp, onehot, loc_mm, rows_ready = (
            sem("logits_mm"), sem("route_sub"), sem("route_exp"), sem("onehot"), sem("loc_mm"), sem("rows_ready"))
        kc_mm, kc_ready, kbd_ready, vc_ready = sem("kc_mm"), sem("kc_ready"), sem("kbd_ready"), sem("vc_ready")
        scattered, ld_slots = sem("scattered"), sems("ld_slots", 4)
        slots0_tp, slots0T_ready, h0_mm, h0_act, h0_dve, y0_mm, y0_row, y0_wr = (
            sem("slots0_tp"), sem("slots0T_ready"), sem("h0_mm"), sem("h0_act"), sem("h0_dve"),
            sem("y0_mm"), sem("y0_row"), sem("y0_wr"))
        gathered = sems("gathered", T)
        x2_ready = sem("x2_ready")
        qk_mm, v_mm, qk_ready, qk_parts, v_ready = (
            sem("qk_mm"), sem("v_mm"), sem("qk_ready"), sem("qk_parts"), sem("v_ready"))
        part_wr = sems("part_wr", 6)
        ld_qk, ld_max = sems("ld_qk", 2), sems("ld_max", HG)
        qk_order = sem("qk_order")
        s1_mm, s1_max, max_tp, max_neg, max_parts = (
            sem("s1_mm"), sem("s1_max"), sem("max_tp"), sem("max_neg"), sem("max_parts"))
        s2_mm, s2_exp, pv_mm, oT_ready, o_tp, o_norm = (
            sem("s2_mm"), sem("s2_exp"), sem("pv_mm"), sem("oT_ready"), sem("o_tp"), sem("o_norm"))
        attn_tp, attnT_ready, proj_mm, xa_ready = sem("attn_tp"), sem("attnT_ready"), sem("proj_mm"), sem("xa_ready")
        qc_mm, qc_ready, c_mm, c_sub, c_exp, c_tp, c_PT, c_pv = (
            sem("qc_mm"), sem("qc_ready"), sem("c_mm"), sem("c_sub"), sem("c_exp"), sem("c_tp"), sem("c_PT"), sem("c_pv"))
        ff_mm, ff_gelu, ff2_mm, x4_ready = sem("ff_mm"), sem("ff_gelu"), sem("ff2_mm"), sem("x4_ready")
        y_parts, slot_onehot, disp_mm = sem("y_parts"), sem("slot_onehot"), sem("disp_mm")
        slots1T_ready, h1_mm, h1_act, h1_dve = (
            sem("slots1T_ready"), sem("h1_mm"), sem("h1_act"), sem("h1_dve"))
        ring_dma = sems("ring_dma", 4)
        comb_ready, comb_tp, combT_ready, hb_mm, hvar, hstd, hid_ready = (
            sem("comb_ready"), sem("comb_tp"), sem("combT_ready"), sem("hb_mm"), sem("hvar"), sem("hstd"),
            sem("hid_ready"))
        hid1_tp, hid1_act, hid1_dve, y1_mm, y1_act, y1_dve, y1_wr = (
            sem("hid1_tp"), sem("hid1_act"), sem("hid1_dve"), sem("y1_mm"),
            sem("y1_act"), sem("y1_dve"), sem("y1_wr"))
        ob_mm, out_ready, out_done = (
            sem("ob_mm"), sem("out_ready"), sem("out_done"))

        N_VEC, N_BIAS, N_WX = 12, 9, 10
        row = lambda v: v.rearrange("(a d) -> a d", a=1)
        block = ctx.enter_context(nc.Block())

        @block.sync
        def _(sp):
            for b in range(B):
                sp.dma_start(x0[:, b * TB:(b + 1) * TB, :], a["x"][b].rearrange("(s p) d -> p s d", p=P)).then_inc(ld_x, 16)
            sp.dma_start(cx[:, :, :], a["ctx_1024"].rearrange("b j d -> j b d")).then_inc(ld_cx, 16)
            sp.dma_start(wsim_row[:, :], a["L0_xattn_w_sim"].rearrange("(k d) -> k d", k=3)).then_inc(ld_cx, 16)
            sp.dma_start(gates[:, 0:2], row(a["g_xattn"]).to_broadcast([P, 2])).then_inc(ld_gate, 16)
            sp.dma_start(gates[:, 2:4], row(a["g_ffn"]).to_broadcast([P, 2])).then_inc(ld_gate, 16)
            sp.dma_start(bsim[:, :], row(a["L0_xattn_b_sim"])).then_inc(ld_gate, 16)
            sp.dma_start(wqv, a["L0_xattn_W_qv"].rearrange("(k p) n -> p k n", p=P)).then_inc(ld_wqv, 16)
            for r, name in enumerate(("L0_xattn_b_qv", "L1_xattn_b_sv", "L1_xattn_b_so", "L1_xattn_b_cv", "L1_xattn_b_co",
                                      "L1_xattn_b_ff2", "L1_ffn_ln_out_w", "L1_ffn_ln_out_b")):
                sp.dma_start(bias[:, r, :], row(a[name]).to_broadcast([P, D])).then_inc(ld_bias, 16)
            sp.dma_start(b2_0.rearrange("p e d -> p (e d)"),
                         row(a["L0_ffn_b2"].rearrange("e d -> (e d)")).to_broadcast([P, E0 * D])).then_inc(ld_bias, 16)
            sp.dma_start(wg0[:, :], a["L0_ffn_wg"]).then_inc(ld_wx, 16)
            sp.dma_start(wg1[:, :], a["L1_ffn_Wg"]).then_inc(ld_wx, 16)
            for w, name in enumerate(("sq", "sk", "sv", "so", "cq", "ck", "cv", "co")):
                sp.dma_start(wx[:, w, :], a["L1_xattn_W_" + name]).then_inc(ld_wx, 16)
            for name, r in (("b_sq", V_BSQ), ("b_sk", V_BSK), ("b_cq", V_BCQ), ("b_ck", V_BCK),
                            ("g_ln1", V_LN1), ("b_ln1", V_LN1 + 1), ("g_ln2", V_LN2), ("b_ln2", V_LN2 + 1),
                            ("g_ln3", V_LN3), ("b_ln3", V_LN3 + 1)):
                sp.dma_start(vrow[r:r + 1, :], row(a["L1_xattn_" + name])).then_inc(ld_vec, 16)
            sp.dma_start(vrow[V_BFF1:V_BFF1 + 4, :], a["L1_xattn_b_ff1"].rearrange("(k d) -> k d", k=4)).then_inc(ld_vec, 16)
            sp.dma_start(vrow[V_B1:NV, :], a["L0_ffn_b1"].rearrange("e (k f) -> (e k) f", f=P)).then_inc(ld_vec, 16)
            sp.wait_ge(consts, 1)
            sp.dma_start(disp0_d.rearrange("(p a) d -> p (a d)", p=P).rearrange("p (a z) -> p a z", z=512),
                         zeros[:, 0:512].unsqueeze(1).to_broadcast([P, 4, 512])).then_inc(zeroed, 16)
            sp.dma_start(w1_0, a["L0_ffn_w1"].rearrange("e m h -> m e h")).then_inc(ld_w0, 16)
            sp.dma_start(w2_0, a["L0_ffn_w2"].rearrange("e (k f) m -> f (e k) m", f=P)).then_inc(ld_w0, 16)
            sp.dma_start(ff1[:, :], a["L1_xattn_W_ff1"]).then_inc(ld_ff, 16)
            sp.dma_start(ff2[:, :, :], a["L1_xattn_W_ff2"].rearrange("(k f) m -> f k m", f=P)).then_inc(ld_ff, 16)
            z = zeros[:, :].unsqueeze(1)
            sp.dma_start(disp2_d.rearrange("r d -> (r d)").rearrange("(p a z) -> p a z", p=P, z=528),
                         z.to_broadcast([P, 16, 528])).then_inc(zeroed, 16)

            sp.wait_ge(scattered, 16 * 2 * T)
            for c in range(4):
                sp.dma_start(slots0[:, 4 * c:4 * c + 4, :],
                             disp0_d[512 * c:512 * c + 512, :].rearrange("(a p) d -> p a d", p=P)).then_inc(ld_slots[c], 16)
            for e in range(E0):
                sp.wait_ge(y0_row, e + 1)
                sp.dma_start(y0_d[C0 * e:C0 * e + C0, :].rearrange("(a p) d -> p a d", p=P),
                             yrow0[:, 2 * e:2 * e + 2, :]).then_inc(y0_wr, 16)

            sp.wait_ge(x2_ready, T)
            ones_src = ones_b[72:75, :].unsqueeze(1)
            zsrc = lambda lo: zeros[lo:KP, 0:512].bitcast(BF16).unsqueeze(1).to_broadcast([KP - lo, NH, N])
            sp.dma_start(Q9[72:KP, :, :], zsrc(72)).then_inc(ld_qk[0], 16)
            sp.dma_start(K9[75:KP, :, :], zsrc(75)).then_inc(ld_qk[0], 16)
            sp.dma_start(K9[72:75, :, :].rearrange("p h (u q) -> p (h u) q", q=P),
                         ones_src.to_broadcast([3, NH * T, P])).then_inc(ld_qk[0], 16)

            def load_packed(which, c, heads, n):
                src = (qk_d[0, c].unsqueeze(0).to_broadcast([3, P, N]) if which == 0 else qk_d[1])
                src = src.rearrange("i (d h) t -> i d h t", d=HD)[:, :, heads, :].rearrange("i d h t -> i d (h t)")
                sp.dma_start((Q9, K9)[which][24 * c:24 * c + 24, heads, :].rearrange("r h t -> r (h t)"), src).then_inc(ld_qk[n], 16)

            for part in range(3):
                sp.wait_ge(part_wr[part], 16)
                load_packed(0, part, slice(0, 4), 0)
            for part in range(3):
                sp.wait_ge(part_wr[3 + part], 16)
            for part in range(3):
                load_packed(1, part, slice(0, 4), 0)
            for which in range(2):
                for part in range(3):
                    load_packed(which, part, slice(4, NH), 1)
            for hg in range(HG):
                sp.wait_ge(max_parts, hg + 1)
                for i in range(3):
                    sp.dma_start(Q9[72 + i:73 + i, 4 * hg:4 * hg + 4, :].rearrange("p h (t q) -> p (h t) q", q=P),
                                 mparts[:, hg, i, :]).then_inc(ld_max[hg], 16)

            sp.dma_start(lnw_h, a["L1_ffn_ln_hid_w"].rearrange("g f -> (g f)").rearrange("(a d) -> a d", a=1)
                         .to_broadcast([P, NG * F1]).rearrange("p (g f) -> p g f", g=NG)).then_inc(ld_hid, 16)
            sp.dma_start(lnb_h, a["L1_ffn_ln_hid_b"].rearrange("g f -> (g f)").rearrange("(a d) -> a d", a=1)
                         .to_broadcast([P, NG * F1]).rearrange("p (g f) -> p g f", g=NG)).then_inc(ld_hid, 16)

            sp.wait_ge(o_norm, 4 * HG)
            sp.dma_start(W1, a["L1_ffn_W1"].rearrange("e m h -> m e h")).then_inc(ld_W1, 16)
            sp.dma_start(W2, a["L1_ffn_W2"].rearrange("e (k f) m -> f (e k) m", f=P)).then_inc(ld_W2, 16)

            sp.wait_ge(ff2_mm, 2)
            sp.dma_start(b1_1, a["L1_ffn_b1"]).then_inc(ld_hid, 16)
            sp.dma_start(b2_1, a["L1_ffn_b2"]).then_inc(ld_hid, 16)

            for e in range(E1):
                sp.wait_ge(h1_dve if e % 2 else h1_act, e // 2 + 1)
                sp.dma_start(h1_d[M1 * e:M1 * (e + 1), :], ring[e % 4]).then_inc(ring_dma[e % 4], 16)
            sp.wait_ge(scattered, 2 * 16 * 2 * T)
            for i in range(E1 + 4):
                if i < E1:
                    if i >= 4:
                        sp.wait_ge(hid1_tp, i - 3)
                    sp.dma_start(ring[i % 4], disp2_d[M1 * i:M1 * (i + 1), :]).then_inc(ring_dma[i % 4], 16)
                if i >= 4:
                    e = i - 4
                    sp.wait_ge(y1_act if e % 2 else y1_dve, e // 2 + 1)
                    sp.dma_start(y1_d[M1 * e:M1 * (e + 1), :], yrow1[:, e, :]).then_inc(y1_wr, 16)
            for b in range(B):
                sp.wait_ge(out_ready, TB * (b + 1))
                sp.dma_start(out[b].rearrange("(s p) d -> p s d", p=P), t3[:, b * TB:(b + 1) * TB, :]).then_inc(out_done, 16)
            sp.wait_ge(out_done, 16 * B)

        @block.gpsimd
        def _(pool):
            me = Chain(pool, pool_self)
            g = nc.gpsimd
            g.memset(zeros[:, :], 0.0).then_inc(consts, 1)
            me.step(g.memset(ident[:, :], 0.0))
            me.step(g.memset(ones_f[:, :], 1.0))
            me.step(g.memset(ones_b[:, :], 1.0))
            me.step(g.memset(head_of[:, :], 1.0))
            me.link(g.memset(before[:, :], 1.0))
            me.step(g.affine_select(out=ident[:, :], in_=ident[:, :], compare_op=ALU.not_equal, fill=1.0, base=0,
                                    pattern=[[-1, P]], channel_multiplier=1))
            me.step(g.affine_select(out=before[:, :], in_=before[:, :], compare_op=ALU.is_gt, fill=0.0, base=0,
                                    pattern=[[1, P]], channel_multiplier=-1))
            me.link(g.affine_select(out=head_of[:, :], in_=head_of[:, :], compare_op=ALU.is_ge, fill=0.0, base=0,
                                    pattern=[[-HD, NH]], channel_multiplier=1))
            me.step(g.affine_select(out=head_of[:, :], in_=head_of[:, :], compare_op=ALU.is_ge, fill=0.0, base=HD - 1,
                                    pattern=[[HD, NH]], channel_multiplier=-1))
            me.step(g.iota(rev[:, :], [[-1, E1]], base=32, channel_multiplier=0, allow_small_or_imprecise_dtypes=True))
            me.step(g.iota(group_row[:, :].rearrange("p (b s) -> p b s", b=B), [[0, B], [C1, TB]], base=0,
                           channel_multiplier=0, allow_small_or_imprecise_dtypes=True))
            me.step(g.memset(vaug[:, :, :, HD], 1.0))
            g.memset(vcaug[:, :, :, HD], 1.0).then_inc(consts, 1)

            pool.wait_ge(ld_vec, 16 * N_VEC)
            pool.wait_ge(ld_wx, 16 * N_WX)
            by_dim = "p (h d) -> p d h"
            g.tensor_copy(vrow_qk[:, :].rearrange("p (d h) -> p d h", d=HD),
                          vrow[V_BSQ:V_BSK + 1, :].rearrange(by_dim, d=HD)).then_inc(qk_order, 1)
            for i, w in enumerate((W_SQ, W_SK)):
                g.tensor_copy(wx_qk[:, i, :].rearrange("p (d h) -> p d h", d=HD),
                              wx[:, w, :].rearrange(by_dim, d=HD)).then_inc(qk_order, 1)

            def scatter(rows, index, dst, last_row):
                for t in range(T):
                    for k in range(2):
                        g.indirect_dma_start(dst, bass.IndirectOffsetOnAxis(ap=index[:, k, t:t + 1], axis=0), rows[:, t, :],
                                             None, bounds_check=last_row, oob_is_err=False).then_inc(scattered, 16)

            def gather(into, index, src, t):
                for k in range(2):
                    g.indirect_dma_start(into[:, t, k, :], None, src,
                                         bass.IndirectOffsetOnAxis(ap=index[:, k, t:t + 1], axis=0)).then_inc(gathered[t], 16)

            pool.wait_ge(rows_ready, 1)
            pool.wait_ge(zeroed, 32)
            scatter(xn, srow[0], disp0_d, E0 * C0 - 1)
            pool.wait_ge(kc_ready, 1)
            for b in range(B):
                ins = g.tensor_tensor(kbd[:, b], kcT[:, b * J:(b + 1) * J].unsqueeze(1).to_broadcast([P, NH, J]),
                                      head_of[:, :].unsqueeze(2).to_broadcast([P, NH, J]), ALU.mult)
            ins.then_inc(kbd_ready, 1)
            pool.wait_ge(y0_wr, 16 * E0)
            for t in range(T):
                gather(got0, grow[0], y0_d, t)
            for u in range(HG):
                pool.wait_ge(max_neg, u + 1)
                me.link(g.tensor_copy(mparts[:, u, 0, :], mneg[:, :]))
                me.link(g.tensor_tensor(mneg[:, :], mneg[:, :], mparts[:, u, 0, :], ALU.subtract))
                me.link(g.tensor_copy(mparts[:, u, 1, :], mneg[:, :]))
                g.tensor_tensor(mparts[:, u, 2, :], mneg[:, :], mparts[:, u, 1, :], ALU.subtract).then_inc(max_parts, 1)
            me.link(g.iota(slot_iota, [[1, CG]], base=0, channel_multiplier=0, allow_small_or_imprecise_dtypes=True))
            rest = [flat(t2), yparts[:, 2, :, :].rearrange("p t d -> p (t d)")]
            for i, left in enumerate((flat(xn), flat(t2))):
                pool.wait_ge(y_parts, 2 * i + 1)
                g.tensor_tensor(rest[i], left, yparts[:, i, :, :].rearrange("p t d -> p (t d)"),
                                ALU.subtract).then_inc(y_parts, 1)
            pool.wait_ge(rows_ready, 2)
            for r in range(4):
                pool.wait_ge(ring_dma[r], 16 * (E1 // 4))
            for t in range(T + 3):
                if t < T:
                    gather(got1, grow[1], h1_d, t)
                if t >= 3:
                    pool.wait_ge(hid_ready, t - 2)
                    for k in range(2):
                        g.indirect_dma_start(disp2_d, bass.IndirectOffsetOnAxis(ap=srow[1][:, k, t - 3:t - 2], axis=0),
                                             hsum[:, t - 3, :], None, bounds_check=E1 * M1 - 1,
                                             oob_is_err=False).then_inc(scattered, 16)
            pool.wait_ge(y1_wr, 16 * E1)
            for t in range(T):
                gather(got2, grow[1], y1_d, t)

        @block.scalar
        def _(act):
            s = nc.scalar

            def evac_xT(i, v):
                for b in range(B):
                    act.wait_ge(ln_tp, 2 * i + b + 1)
                    dst = xT[:, b * SEQ:(b + 1) * SEQ]
                    if v is None:
                        s.copy(dst, bank(b)).then_inc(xT_ready, 1)
                    else:
                        s.activation(dst, bank(b), ACT.Identity, bias=vcol[:, v + 1:v + 2],
                                     scale=vcol[:, v:v + 1]).then_inc(xT_ready, 1)

            def std_of(i, k=1):
                for b in range(B):
                    half = slice(b * TB, (b + 1) * TB)
                    act.wait_ge(ln_stats, 2 * i + b + 1)
                    s.activation(std[:, 0:k, half], var_eps[:, 0:k, half], ACT.Sqrt).then_inc(ln_std, 1)

            act.wait_ge(ld_gate, 48)
            s.activation(tg[:, 0:4], gates[:, :], ACT.Tanh).then_inc(tanh_ready, 1)
            std_of(0)
            evac_xT(0, None)
            act.wait_ge(sim_sub, 1)
            s.activation(simA, simA, ACT.Exp).then_inc(sim_exp, 1)
            act.wait_ge(batt_sub, 1)
            s.activation(small[:, 16:24], small[:, 8:16], ACT.Exp).then_inc(batt_exp, 1)
            for b in range(B):
                act.wait_ge(simT_tp, b + 1)
                s.copy(simT[:, b * SEQ:(b + 1) * SEQ], ps[0:J, 6 + b, :]).then_inc(simT_ready, 1)
            for b in range(B):
                act.wait_ge(hq_mm, b + 1)
                s.copy(hqT[:, b * SEQ:(b + 1) * SEQ], bank(b)).then_inc(hqT_ready, 1)

            def route_exps(i, E):
                act.wait_ge(route_sub, i + 1)
                s.activation(rtmp[:, 0:T * E], rdl[:, 0:T * E], ACT.Exp)
                s.activation(rs[:, 1, :], rs[:, 0, :], ACT.Exp).then_inc(route_exp, 1)

            std_of(1)
            evac_xT(1, None)
            route_exps(0, E0)
            act.wait_ge(cx_tp, 2)
            s.copy(vcol[:, :], ps[:, 7, 0:NV]).then_inc(vcol_ready, 1)
            act.wait_ge(vcol_ready, 1)
            act.wait_ge(kc_mm, 1)
            s.activation(kcT[:, :], ps[:, 0, 0:B * J], ACT.Identity, bias=vcol[:, V_BCK:V_BCK + 1]).then_inc(kc_ready, 1)

            def evac_slots0(c):
                act.wait_ge(slots0_tp, c + 1)
                s.copy(slots0T[:, 512 * c:512 * c + 512], bank(c % 2)).then_inc(slots0T_ready, 1)

            evac_slots0(0)
            for e in range(E0):
                if e % 2 == 0 and e // 2 + 1 < 4:
                    evac_slots0(e // 2 + 1)
                act.wait_ge(h0_mm, 2 * e + 1)
                if e >= 2:
                    act.wait_ge(y0_mm, e - 1)
                for f in range(2):
                    ins = s.activation(hid0[e % 2][:, f, :], ps[:, 2 + 2 * (e % 2), f * C0:(f + 1) * C0], ACT.Relu,
                                       bias=vcol[:, V_B1 + 4 * e + f:V_B1 + 4 * e + f + 1])
                ins.then_inc(h0_act, 1)

            std_of(2, 2)
            evac_xT(2, V_LN1)
            for mm, full, parts, v, bk in ((2, qf, qparts, V_BSQ, 2), (4, kf, kparts, V_BSK, 4)):
                act.wait_ge(qk_mm, mm)
                src = ps[:, bk:bk + 2, :].rearrange("p b t -> p (b t)")
                s.activation(full, src, ACT.Identity, bias=vcol[:, v:v + 1])
                s.activation(parts[:, 0, :], src, ACT.Identity, bias=vcol[:, v:v + 1]).then_inc(qk_ready, 1)
                act.wait_ge(qk_ready, mm // 2)
                act.dma_start(qk_d[mm // 2 - 1, 0], parts[:, 0, :]).then_inc(part_wr[3 * (mm // 2 - 1)], 16)
            for which, parts in enumerate((qparts, kparts)):
                for i in (1, 2):
                    act.wait_ge(qk_parts, 2 * which + i)
                    act.dma_start(qk_d[which, i], parts[:, i, :]).then_inc(part_wr[3 * which + i], 16)

            def negate_max(u):
                act.wait_ge(max_tp, u + 1)
                if u >= 1:
                    act.wait_ge(max_parts, u)
                s.activation(mneg[:, :], ps[0:MU, 7, 0:P], ACT.Copy, scale=-1.0).then_inc(max_neg, 1)

            negate_max(0)

            def evac_oT(u, produced, count):
                act.wait_ge(produced, count)
                if u >= 2:
                    act.wait_ge(o_tp, u - 1)
                s.copy(oT[u % 2], bank(6)).then_inc(oT_ready, 1)

            for st in range(8 * HG + 1):
                for idx in (2 * st, 2 * st + 1):
                    if st < 8 * HG:
                        act.wait_ge(s2_mm, idx + 1)
                        if idx >= 4:
                            act.wait_ge(pv_mm, (idx - 4) // 2 + 1)
                        s.activation(probs[idx % 4], ps[:, 2 * (idx % 2):2 * (idx % 2) + 2, :].rearrange("p b t -> p (b t)"),
                                     ACT.Exp, scale=QK_SCALE).then_inc(s2_exp, 1)
                    if idx % 2 == 0 and st % 8 == 5 and st // 8 + 1 < HG:
                        negate_max(st // 8 + 1)
                if st >= 4 and st % 4 == 0:
                    evac_oT(st // 4 - 1, pv_mm, st)

            def evac_attnT(i):
                for b in range(B):
                    act.wait_ge(attn_tp, 2 * i + b + 1)
                    s.copy(attnT[:, b * SEQ:(b + 1) * SEQ], bank(b)).then_inc(attnT_ready, 1)

            evac_attnT(0)
            std_of(3)
            evac_xT(3, V_LN2)
            act.wait_ge(qc_mm, 2)
            s.activation(qcT, ps[:, 2:4, :].rearrange("p b t -> p (b t)"), ACT.Identity,
                         bias=vcol[:, V_BCQ:V_BCQ + 1]).then_inc(qc_ready, 1)

            def cross_exp(un):
                act.wait_ge(c_sub, un + 1)
                s.activation(pc[un % 3], pc[un % 3], ACT.Exp, scale=QK_SCALE).then_inc(c_exp, 1)

            cross_exp(0)
            for un in range(2 * T):
                if un + 1 < 2 * T:
                    cross_exp(un + 1)
                t, half = un // 2, un % 2
                for j in range(2):
                    act.wait_ge(c_tp, 2 * un + j + 1)
                    h = 8 * half + 4 * j
                    s.copy(PT[t // TB][:, h:h + 4, (t % TB) * P:(t % TB + 1) * P],
                           ps[0:J, 4 + j, :].rearrange("p (h q) -> p h q", h=4)).then_inc(c_PT, 1)
                if 8 <= un < 8 + HG:
                    evac_oT(2 * HG + un - 8, c_pv, un - 7)
            for hg in range(HG):
                evac_oT(3 * HG + hg, c_pv, HG + hg + 1)
            evac_attnT(1)
            std_of(4)
            evac_xT(4, V_LN3)
            for b in range(B):
                for f in range(4):
                    act.wait_ge(ff_mm, 4 * b + f + 1)
                    s.activation(geluT[:, f, b * SEQ:(b + 1) * SEQ], bank(4 * b + f), ACT.Gelu,
                                 bias=vcol[:, V_BFF1 + f:V_BFF1 + f + 1]).then_inc(ff_gelu, 1)
            std_of(5)
            evac_xT(5, None)
            act.wait_ge(ln_out, 6 * T)
            s.copy(yparts[:, 0, :, :].rearrange("p t d -> p (t d)"), flat(xn)).then_inc(y_parts, 1)
            act.wait_ge(y_parts, 2)
            s.copy(yparts[:, 1, :, :].rearrange("p t d -> p (t d)"), flat(t2)).then_inc(y_parts, 1)
            route_exps(1, E1)
            for gr in range(NG):
                act.wait_ge(disp_mm, B * (gr + 1))
                bk = 6 * (gr % 2)
                s.copy(slots1T.rearrange("p (a e m) -> p a e m", a=2, m=M1)[:, :, :, C1 * gr:C1 * (gr + 1)],
                       ps[:, bk:bk + 2, 0:CG // 2].rearrange("p a (e c) -> p a e c", c=C1)).then_inc(slots1T_ready, 1)
            for e in range(E1):
                if e % 2 == 0:
                    act.wait_ge(h1_mm, e + 1)
                    if e >= 4:
                        act.wait_ge(ring_dma[e % 4], 16 * (e // 4))
                    s.copy(ring[e % 4], ps[0:M1, 2 + e % 4, :]).then_inc(h1_act, 1)
            for b in range(B):
                act.wait_ge(comb_tp, b + 1)
                s.copy(combT[:, b * SEQ:(b + 1) * SEQ], ps[0:E1, b, :]).then_inc(combT_ready, 1)
            for t in range(T):
                act.wait_ge(hvar, t + 1)
                s.activation(tmp8[:, t:t + 1], tmp8b[:, t:t + 1], ACT.Sqrt).then_inc(hstd, 1)
            for e in range(E1 + 1):
                if e < E1 and e % 2 == 0:
                    act.wait_ge(hid1_tp, e + 1)
                    if e >= 4:
                        act.wait_ge(y1_mm, e - 3)
                    s.activation(hid1T[e % 4].rearrange("p f c -> p (f c)"), ps[:, 0, 0:4 * M1],
                                 ACT.Relu).then_inc(hid1_act, 1)
                if e >= 1 and (e - 1) % 2 == 1:
                    act.wait_ge(y1_mm, e)
                    s.copy(yrow1[:, e - 1, :], ps[0:M1, 2 + (e - 1) % 4, 0:D]).then_inc(y1_act, 1)
            for b in range(B):
                half = slice(b * TB, (b + 1) * TB)
                act.wait_ge(ln_stats, 12 + b + 1)
                s.activation(std[:, 0, half], var_eps[:, 0, half], ACT.Sqrt).then_inc(ln_std, 1)

        @block.vector
        def _(dve):
            me = Chain(dve, dve_self)
            v = nc.vector

            def stats(src, i, b, again=False):
                half = slice(b * TB, (b + 1) * TB)
                for t in range(b * TB, (b + 1) * TB):
                    me.step(v.bn_stats(st6[:, t, :], src[:, t, :]))
                me.wait()
                for t in range(b * TB, (b + 1) * TB):
                    me.step(v.bn_aggr(mv[:, t, :], st6[:, t, :]))
                me.wait()
                if again:
                    me.step(v.tensor_scalar(var_eps[:, 1, half], mv[:, half, 1], 0.01 + LN_EPS, LN_EPS * LN_EPS,
                                            ALU.mult, ALU.add))
                v.tensor_scalar(var_eps[:, 0, half], mv[:, half, 1], LN_EPS, None, ALU.add).then_inc(ln_stats, 1)

            def scale_of(src, dst, i, b, again=False):
                half = slice(b * TB, (b + 1) * TB)
                dve.wait_ge(ln_std, 2 * i + b + 1)
                k = 2 if again else 1
                me.link(v.reciprocal(rstds[:, 0:k, half], std[:, 0:k, half]))
                if again:
                    me.link(v.tensor_scalar(rstds[:, :, half], rstds[:, :, half], 0.1, None, ALU.mult))
                for t in range(b * TB, (b + 1) * TB):
                    v.tensor_scalar(dst[:, t, :], src[:, t, :], mv[:, t, 0:1], rstds[:, k - 1, t:t + 1],
                                    ALU.subtract, ALU.mult).then_inc(ln_out, 1)

            def layer_norm(src, dst, i, again=False):
                for b in range(B):
                    stats(src, i, b, again)
                for b in range(B):
                    scale_of(src, dst, i, b, again)

            dve.wait_ge(ld_x, 32)
            layer_norm(x0, xn, 0)
            dve.wait_ge(cx_tp, 1)
            me.step(v.tensor_copy(cxT[:, :], ps[:, 2, 0:B * J]))
            v.tensor_copy(wsim[:, :], ps[:, 2, B * J:B * J + 3]).then_inc(cxT_ready, 1)
            dve.wait_ge(cxT_ready, 1)
            v.tensor_scalar(rT[:, :], cxT[:, :], wsim[:, 2:3], wsim[:, 0:1], ALU.mult, ALU.add).then_inc(rT_ready, 1)
            v.tensor_scalar(imgT[:, :], cxT[:, :], 0.1, None, ALU.mult).then_inc(rT_ready, 1)
            dve.wait_ge(simrow_mm, 1)
            dve.wait_ge(ld_gate, 48)
            v.tensor_scalar(simrow[:, :], ps[0:1, 3, 0:B * J], bsim[:, 0:1], None, ALU.add).then_inc(simrow_ready, 1)
            dve.wait_ge(tanh_ready, 1)
            dve.wait_ge(ld_bias, 16 * N_BIAS)
            me.step(v.tensor_scalar(tg[:, 4:5], tg[:, 1:2], 10.0, None, ALU.mult))
            me.link(v.tensor_scalar(attn[:, 0, :], bias[:, R_QV, :], tg[:, 0:1], None, ALU.mult))
            me.step(v.tensor_tensor(xplus, x0, attn[:, 0:1, :].to_broadcast([P, T, D]), ALU.add))
            dve.wait_ge(sim_mm, 2)
            sim = ps[:, 2:4, 0:TB * J].rearrange("p b (t j) -> p b t j", j=J)
            mx = small[:, 0:T]
            v.tensor_reduce(mx.rearrange("p (b t) -> p b t", b=B), sim, AX.X, ALU.max).then_inc(simmax, 1)
            dve.wait_ge(simmax, 1)
            v.tensor_tensor(simA.rearrange("p (b t) j -> p b t j", b=B), sim,
                            mx.rearrange("p (b t) -> p b t", b=B).unsqueeze(3).to_broadcast([P, B, TB, J]),
                            ALU.subtract).then_inc(sim_sub, 1)
            dve.wait_ge(mrow_tp, 1)
            v.tensor_reduce(rowmax[:, :], ps[0:1, 0:2, :], AX.X, ALU.max).then_inc(mrow_max, 1)
            dve.wait_ge(mrow_mm, 1)
            v.tensor_tensor(small[:, 8:16].rearrange("p (b t) -> p b t", b=B), mx.rearrange("p (b t) -> p b t", b=B),
                            ps[:, 4, 0:B].unsqueeze(2).to_broadcast([P, B, TB]), ALU.subtract).then_inc(batt_sub, 1)
            dve.wait_ge(sim_exp, 1)
            me.link(v.tensor_reduce(small[:, 24:32], simA, AX.X, ALU.add))
            me.link(v.reciprocal(small[:, 32:40], small[:, 24:32]))
            v.tensor_tensor(simA, simA, small[:, 32:40].unsqueeze(2).to_broadcast([P, T, J]), ALU.mult).then_inc(sim_norm, 1)
            dve.wait_ge(batt_mm, 1)
            me.link(v.tensor_reduce(small[:, 40:42], ps[:, 4, 8:16].rearrange("p (b t) -> p b t", b=B), AX.X, ALU.add))
            me.link(v.reciprocal(small[:, 42:44], small[:, 40:42]))
            me.link(v.tensor_tensor(small[:, 44:46], ps[:, 5, 0:B], small[:, 42:44], ALU.mult))
            dve.wait_ge(ld_wqv, 16)
            for b in range(B):
                ins = v.scalar_tensor_tensor(out=w14[:, b, :], in0=wqv[:, 3, :], scalar=small[:, 44 + b:45 + b],
                                             in1=wqv[:, 0, :], op0=ALU.mult, op1=ALU.add)
            ins.then_inc(w14_ready, 1)
            for b in range(B):
                dve.wait_ge(hqT_ready, b + 1)
                half = slice(b * SEQ, (b + 1) * SEQ)
                v.tensor_tensor(prodT[:, half], hqT[:, half], xT[:, half], ALU.mult).then_inc(prodT_ready, 1)
            for b in range(B):
                dve.wait_ge(hcq_mm, b + 1)
                half = slice(b * TB, (b + 1) * TB)
                v.scalar_tensor_tensor(out=x1[:, half, :].rearrange("p t d -> p (t d)"), in0=bank(2 + b), scalar=tg[:, 0:1],
                                       in1=xplus[:, half, :].rearrange("p t d -> p (t d)"), op0=ALU.mult,
                                       op1=ALU.add).then_inc(x1_ready, 1)
                dve.wait_ge(x1_ready, b + 1)
                stats(x1, 1, b)

            col1 = small[:, 32:48].rearrange("p (k t) -> p k t", k=2)

            def one_hot_slots():
                me.wait()
                for gr in range(NG):
                    if gr >= 2:
                        dve.wait_ge(disp_mm, B * (gr - 1))
                    for b in range(B):
                        tile = gr + TB * b
                        me.step(v.tensor_scalar(slot1h[2 * (gr % 2) + b], slot_iota, col1[:, 0, tile:tile + 1], None,
                                                ALU.is_equal))
                    for b in range(B):
                        tile = gr + TB * b
                        me.wait(me.n - 1 + b)
                        v.scalar_tensor_tensor(out=slot1h[2 * (gr % 2) + b], in0=slot_iota, scalar=col1[:, 1, tile:tile + 1],
                                               in1=slot1h[2 * (gr % 2) + b], op0=ALU.is_equal,
                                               op1=ALU.add).then_inc(slot_onehot, 1)

            def route(i, E, C, logits, loc_of):
                def pte(tile):
                    return tile[:, 0:T * E].rearrange("p (t e) -> p t e", e=E)
                def over(x):
                    return x.unsqueeze(2).to_broadcast([P, T, E])
                revb = rev[:, 0:E].unsqueeze(1).to_broadcast([P, T, E])
                m2, e2, m1, km = rs[:, 0, :], rs[:, 1, :], rs[:, 2, :], rs[:, 3:5, :]
                dve.wait_ge(logits_mm, i + 1)
                me.link(v.tensor_reduce(m1, logits, AX.X, ALU.max))
                me.link(v.tensor_tensor(pte(rdl), logits, over(m1), ALU.subtract))
                me.link(v.scalar_tensor_tensor(out=pte(rkey), in0=pte(rdl), scalar=0.0, in1=revb,
                                               op0=ALU.is_equal, op1=ALU.mult))
                me.link(v.tensor_reduce(km[:, 0, :], pte(rkey), AX.X, ALU.max))
                me.link(v.tensor_tensor(pte(oh[0]), pte(rkey), over(km[:, 0, :]), ALU.is_equal))
                me.link(v.scalar_tensor_tensor(out=pte(rkey), in0=pte(oh[0]), scalar=-BIG, in1=pte(rdl),
                                               op0=ALU.mult, op1=ALU.add))
                v.tensor_reduce(m2, pte(rkey), AX.X, ALU.max).then_inc(route_sub, 1)
                dve.wait_ge(route_sub, i + 1)
                me.link(v.tensor_tensor(pte(rkey), pte(rkey), over(m2), ALU.is_equal))
                me.link(v.tensor_tensor(pte(rkey), pte(rkey), revb, ALU.mult))
                me.link(v.tensor_reduce(km[:, 1, :], pte(rkey), AX.X, ALU.max))
                v.tensor_tensor(pte(oh[1]), pte(rkey), over(km[:, 1, :]), ALU.is_equal).then_inc(onehot, 1)
                score, valid, pos, base = rs[:, 5:7, :], rs[:, 7:9, :], rs[:, 9:11, :], rs[:, 11:13, :]
                dve.wait_ge(route_exp, i + 1)
                me.link(v.tensor_reduce(rs[:, 13, :], pte(rtmp), AX.X, ALU.add))
                me.link(v.reciprocal(score[:, 0, :], rs[:, 13, :]))
                me.link(v.tensor_tensor(score[:, 1, :], score[:, 0, :], e2, ALU.mult))
                me.step(v.tensor_scalar(base, km, -float(C if i == 0 else M1), 32.0 * (C if i == 0 else M1), ALU.mult, ALU.add))
                dve.wait_ge(loc_mm, i + 1)
                for k in range(2):
                    me.link(v.tensor_tensor(pte(rkey), loc_of(k), pte(oh[k]), ALU.mult))
                    me.link(v.tensor_reduce(pos[:, k, :], pte(rkey), AX.X, ALU.add))
                me.link(v.tensor_scalar(valid, pos, float(C), None, ALU.is_lt))
                if i == 1:
                    me.link(v.tensor_tensor(base, base, group_row[:, :].unsqueeze(1).to_broadcast([P, 2, T]), ALU.add))
                else:
                    me.wait()
                skip = rs[:, 14:16, :]
                me.step(v.tensor_scalar(skip, valid, -SKIP, SKIP, ALU.mult, ALU.add))
                me.link(v.tensor_tensor(rkey[:, 0:16].rearrange("p (k t) -> p k t", k=2), pos, valid, ALU.mult))
                me.step(v.tensor_tensor(grow[i][:, :, :], rkey[:, 0:16].rearrange("p (k t) -> p k t", k=2), base, ALU.add))
                if i == 1:
                    me.link(v.tensor_scalar(col1, km, -float(C1), 32.0 * C1, ALU.mult, ALU.add))
                    me.link(v.tensor_tensor(col1, col1, skip, ALU.add))
                    me.step(v.tensor_tensor(col1, col1, pos, ALU.add))
                me.link(v.tensor_tensor(pos, pos, base, ALU.add))
                v.tensor_tensor(srow[i][:, :, :], pos, skip, ALU.add).then_inc(rows_ready, 1)
                if i == 1:
                    one_hot_slots()
                g = gate[i][:, :, :]
                if i == 0:
                    me.link(v.tensor_tensor(rs[:, 13, :], score[:, 0, :], score[:, 1, :], ALU.add))
                    me.link(v.tensor_tensor(score, score, valid, ALU.mult))
                else:
                    me.link(v.tensor_tensor(score, score, valid, ALU.mult))
                    me.link(v.tensor_tensor(rs[:, 13, :], score[:, 0, :], score[:, 1, :], ALU.add))
                    me.link(v.tensor_scalar(rs[:, 13, :], rs[:, 13, :], 1e-9, None, ALU.max))
                me.link(v.reciprocal(rs[:, 2, :], rs[:, 13, :]))
                me.link(v.tensor_tensor(g, score, rs[:, 2:3, :].to_broadcast([P, 2, T]), ALU.mult))

            for b in range(B):
                scale_of(x1, xn, 1, b)
            route(0, E0, C0, ps[:, 2, 0:T * E0].rearrange("p (t e) -> p t e", e=E0),
                  lambda k: ps[:, 3 + k, 0:T * E0].rearrange("p (t e) -> p t e", e=E0))
            me.link(v.tensor_scalar(gate[0][:, :, :], gate[0][:, :, :], tg[:, 2:3], None, ALU.mult))
            dve.wait_ge(kc_mm, 2)
            v.tensor_tensor(vcaug[:, :, :, 0:HD], ps[0:J, 1, 0:B * D].rearrange("p (b h d) -> p b h d", b=B, h=NH),
                            bias[0:J, R_CV, :].rearrange("p (h d) -> p h d", h=NH).unsqueeze(1).to_broadcast([J, B, NH, HD]),
                            ALU.add).then_inc(vc_ready, 1)
            dve.wait_ge(vcol_ready, 1)
            for e in range(E0 + 1):
                if e < E0:
                    dve.wait_ge(h0_mm, 2 * e + 2)
                    if e >= 2:
                        dve.wait_ge(y0_mm, e - 1)
                    for f in (2, 3):
                        ins = v.tensor_scalar(hid0[e % 2][:, f, :], ps[:, 3 + 2 * (e % 2), (f - 2) * C0:(f - 1) * C0],
                                              vcol[:, V_B1 + 4 * e + f:V_B1 + 4 * e + f + 1], 0.0, ALU.add, ALU.max)
                    ins.then_inc(h0_dve, 1)
                if e >= 1:
                    dve.wait_ge(y0_mm, e)
                    v.tensor_tensor(yrow0[:, 2 * e - 2:2 * e, :], ps[:, 6 + (e - 1) % 2, 0:2 * D].rearrange("p (a d) -> p a d", a=2),
                                    b2_0[:, e - 1:e, :].to_broadcast([P, 2, D]), ALU.add).then_inc(y0_row, 1)
            for t in range(T):
                dve.wait_ge(gathered[t], 32)
                me.step(v.scalar_tensor_tensor(out=x1[:, t, :], in0=got0[:, t, 0, :], scalar=gate[0][:, 0, t:t + 1],
                                               in1=x1[:, t, :], op0=ALU.mult, op1=ALU.add))
                me.wait()
                v.scalar_tensor_tensor(out=x2[:, t, :], in0=got0[:, t, 1, :], scalar=gate[0][:, 1, t:t + 1],
                                       in1=x1[:, t, :], op0=ALU.mult, op1=ALU.add).then_inc(x2_ready, 1)
                if t % TB == TB - 1:
                    dve.wait_ge(x2_ready, t + 1)
                    stats(x2, 2, t // TB, again=True)

            for b in range(B):
                scale_of(x2, xn, 2, b, again=True)
            for t in range(T):
                me.step(v.tensor_scalar(xres[:, t, :], x2[:, t, :], mv[:, t, 0:1], rstds[:, 0, t:t + 1], ALU.subtract, ALU.mult))
            for n, full, parts in ((1, qf, qparts), (2, kf, kparts)):
                dve.wait_ge(qk_ready, n)
                me.link(v.tensor_tensor(full, full, parts[:, 0, :], ALU.subtract))
                v.tensor_copy(parts[:, 1, :], full).then_inc(qk_parts, 1)
                dve.wait_ge(qk_parts, 2 * n - 1)
                v.tensor_tensor(parts[:, 2, :], full, parts[:, 1, :], ALU.subtract).then_inc(qk_parts, 1)
            for b in range(B):
                dve.wait_ge(v_mm, b + 1)
                v.tensor_tensor(vaug[:, b * TB:(b + 1) * TB, :, 0:HD],
                                bank(6 + b).rearrange("p (t h d) -> p t h d", t=TB, h=NH),
                                bias[:, R_SV, :].rearrange("p (h d) -> p h d", h=NH).unsqueeze(1).to_broadcast([P, TB, NH, HD]),
                                ALU.add).then_inc(v_ready, 1)
            me.step(v.tensor_tensor(xres[:, :, :], xres[:, :, :], bias[:, R_SO:R_SO + 1, :].to_broadcast([P, T, D]), ALU.add))

            def row_max(n):
                hg, r = n // MU, n % MU
                dve.wait_ge(s1_mm, n + 1)
                col = T * (r % 4) + r // 4
                v.tensor_reduce(mcol[:, hg, col:col + 1], bank(4 + n % 2), AX.X, ALU.max).then_inc(s1_max, 1)

            def normalize(u, hg, b):
                dve.wait_ge(o_tp, u + 1)
                o = bank(7).rearrange("p (t h c) -> p t h c", t=TB, h=4)
                me.link(v.reciprocal(rden[:, :].rearrange("p (t h) -> p t h", h=4), o[:, :, :, HD]))
                v.tensor_tensor(attn[:, b * TB:(b + 1) * TB, 32 * hg:32 * hg + 32].rearrange("p t (h d) -> p t h d", h=4),
                                o[:, :, :, 0:HD],
                                rden[:, :].rearrange("p (t h) -> p t h", h=4).unsqueeze(3).to_broadcast([P, TB, 4, HD]),
                                ALU.mult).then_inc(o_norm, 1)

            for n in range(LEAD):
                row_max(n)
            n = LEAD
            for st in range(8 * HG + 1):
                for i in range(4):
                    if i == 3 and st % 4 == 2 and st >= 6:
                        u = (st - 6) // 4
                        normalize(u, u // 2, u % 2)
                    if n < MU * HG:
                        row_max(n)
                        n += 1
            normalize(2 * HG - 1, HG - 1, 1)
            for b in range(B):
                dve.wait_ge(proj_mm, b + 1)
                v.tensor_tensor(xa[:, b * TB:(b + 1) * TB, :].rearrange("p t d -> p (t d)"), bank(2 + b),
                                xres[:, b * TB:(b + 1) * TB, :].rearrange("p t d -> p (t d)"), ALU.add).then_inc(xa_ready, 1)
                dve.wait_ge(xa_ready, b + 1)
                stats(xa, 3, b)

            for b in range(B):
                scale_of(xa, xn, 3, b)
            me.step(v.tensor_tensor(xres[:, :, :], xa[:, :, :], bias[:, R_CO:R_CO + 1, :].to_broadcast([P, T, D]), ALU.add))

            for un in range(2 * T):
                dve.wait_ge(c_mm, un + 1)
                bk = 2 * (un % 2)
                sc = ps[:, bk:bk + 2, 0:4 * J].rearrange("p b (h j) -> p b h j", h=4)
                m = small[:, 0:8].rearrange("p (b h) -> p b h", b=2)
                me.link(v.tensor_reduce(m, sc, AX.X, ALU.max))
                if un >= 3:
                    dve.wait_ge(c_tp, 2 * un - 4)
                v.tensor_tensor(pc[un % 3].rearrange("p (b h) j -> p b h j", b=2), sc,
                                m.unsqueeze(3).to_broadcast([P, 2, 4, J]), ALU.subtract).then_inc(c_sub, 1)
                dve.wait_ge(c_sub, un + 1)
                if 11 <= un < 11 + HG:
                    normalize(2 * HG + un - 11, un - 11, 0)
            for hg in range(HG):
                normalize(3 * HG + hg, hg, 1)
            for b in range(B):
                dve.wait_ge(proj_mm, 2 + b + 1)
                v.tensor_tensor(xa[:, b * TB:(b + 1) * TB, :].rearrange("p t d -> p (t d)"), bank(2 + b),
                                xres[:, b * TB:(b + 1) * TB, :].rearrange("p t d -> p (t d)"), ALU.add).then_inc(xa_ready, 1)
                dve.wait_ge(xa_ready, 2 + b + 1)
                stats(xa, 4, b)

            for b in range(B):
                scale_of(xa, xn, 4, b)
            me.link(v.tensor_tensor(xres[:, :, :], xa[:, :, :], bias[:, R_FF2:R_FF2 + 1, :].to_broadcast([P, T, D]), ALU.add))
            me.link(v.scalar_tensor_tensor(out=flat(t1), in0=flat(xres), scalar=tg[:, 4:5], in1=flat(x2), op0=ALU.mult, op1=ALU.add))
            x4 = t3
            for b in range(B):
                half = slice(b * TB, (b + 1) * TB)
                dve.wait_ge(ff2_mm, b + 1)
                v.scalar_tensor_tensor(out=x4[:, half, :].rearrange("p t d -> p (t d)"), in0=bank(4 * b), scalar=tg[:, 4:5],
                                       in1=t1[:, half, :].rearrange("p t d -> p (t d)"), op0=ALU.mult,
                                       op1=ALU.add).then_inc(x4_ready, 1)
                dve.wait_ge(x4_ready, b + 1)
                stats(x4, 5, b)

            for b in range(B):
                scale_of(x4, xn, 5, b)
            lnw = bias[:, R_LNW, :]
            me.step(v.tensor_scalar(lnw, lnw, tg[:, 3:4], None, ALU.mult))
            me.link(v.tensor_scalar(bias[:, R_LNB, :], bias[:, R_LNB, :], tg[:, 3:4], None, ALU.mult))
            me.step(v.tensor_tensor(t1[:, :, :], x4[:, :, :], bias[:, R_LNB:R_LNB + 1, :].to_broadcast([P, T, D]), ALU.add))
            route(1, E1, C1, ps[:, 2, 0:T * E1].rearrange("p (t e) -> p t e", e=E1),
                  lambda k: ps[:, 3 + k, 0:T * E1].rearrange("p (t e) -> p t e", e=E1))
            ohe = [oh[k][:, :].rearrange("p (t e) -> p t e", e=E1) for k in range(2)]
            g1 = gate[1]
            me.step(v.tensor_tensor(comb[:, :, :], ohe[0], g1[:, 0, :].unsqueeze(2).to_broadcast([P, T, E1]), ALU.mult))
            kk = rkey[:, :].rearrange("p (t e) -> p t e", e=E1)
            me.link(v.tensor_tensor(kk, ohe[1], g1[:, 1, :].unsqueeze(2).to_broadcast([P, T, E1]), ALU.mult))
            v.tensor_tensor(comb[:, :, :], comb[:, :, :], kk, ALU.add).then_inc(comb_ready, 1)
            for e in range(1, E1, 2):
                dve.wait_ge(h1_mm, e + 1)
                if e >= 4:
                    dve.wait_ge(ring_dma[e % 4], 16 * (e // 4))
                v.tensor_copy(ring[e % 4], ps[0:M1, 2 + e % 4, :]).then_inc(h1_dve, 1)
            dve.wait_ge(ld_hid, 64)
            for t in range(T + 1):
                if t < T:
                    dve.wait_ge(gathered[t], 64)
                    dve.wait_ge(hb_mm, t + 1)
                    me.link(v.scalar_tensor_tensor(out=hsum[:, t, :], in0=got1[:, t, 0, :], scalar=g1[:, 0, t:t + 1],
                                                   in1=bank(2 + t % 4), op0=ALU.mult, op1=ALU.add))
                    me.link(v.scalar_tensor_tensor(out=hsum[:, t, :], in0=got1[:, t, 1, :], scalar=g1[:, 1, t:t + 1],
                                                   in1=hsum[:, t, :], op0=ALU.mult, op1=ALU.add))
                    me.link(v.bn_stats(st6[:, t, :], hsum[:, t, :]))
                    me.link(v.bn_aggr(mv[:, t, :], st6[:, t, :]))
                    v.tensor_scalar(tmp8b[:, t:t + 1], mv[:, t, 1:2], MOE_EPS, None, ALU.add).then_inc(hvar, 1)
                if t >= 1:
                    u = t - 1
                    gi = u % TB
                    dve.wait_ge(hstd, u + 1)
                    me.link(v.reciprocal(rstd[:, u:u + 1], tmp8[:, u:u + 1]))
                    me.link(v.scalar_tensor_tensor(out=got1[:, u, 0, :], in0=hsum[:, u, :], scalar=mv[:, u, 0:1],
                                                   in1=lnw_h[:, gi, :], op0=ALU.subtract, op1=ALU.mult))
                    v.scalar_tensor_tensor(out=hsum[:, u, :], in0=got1[:, u, 0, :], scalar=rstd[:, u:u + 1],
                                           in1=lnb_h[:, gi, :], op0=ALU.mult, op1=ALU.add).then_inc(hid_ready, 1)
            for e in range(E1 + 1):
                if e < E1 and e % 2 == 1:
                    dve.wait_ge(hid1_tp, e + 1)
                    if e >= 4:
                        dve.wait_ge(y1_mm, e - 3)
                    v.tensor_scalar(hid1T[e % 4].rearrange("p f c -> p (f c)"), ps[:, 1, 0:4 * M1], 0.0, None,
                                    ALU.max).then_inc(hid1_dve, 1)
                if e >= 1 and (e - 1) % 2 == 0:
                    dve.wait_ge(y1_mm, e)
                    v.tensor_copy(yrow1[:, e - 1, :], ps[0:M1, 2 + (e - 1) % 4, 0:D]).then_inc(y1_dve, 1)
            z = t2
            for t in range(T):
                dve.wait_ge(gathered[t], 96)
                if t % TB == 0:
                    dve.wait_ge(ob_mm, t // TB + 1)
                me.link(v.scalar_tensor_tensor(out=z[:, t, :], in0=got2[:, t, 0, :], scalar=g1[:, 0, t:t + 1],
                                               in1=ps[:, 6 + t // TB, (t % TB) * D:(t % TB + 1) * D], op0=ALU.mult, op1=ALU.add))
                me.link(v.scalar_tensor_tensor(out=z[:, t, :], in0=got2[:, t, 1, :], scalar=g1[:, 1, t:t + 1],
                                               in1=z[:, t, :], op0=ALU.mult, op1=ALU.add))
                me.link(v.tensor_tensor(z[:, t, :], z[:, t, :], xn[:, t, :], ALU.add))
                me.link(v.bn_stats(st6[:, t, :], z[:, t, :]))
                me.link(v.bn_aggr(mv[:, t, :], st6[:, t, :]))
                if t % TB == TB - 1:
                    half = slice(t - TB + 1, t + 1)
                    v.tensor_scalar(var_eps[:, 0, half], mv[:, half, 1], MOE_EPS, None, ALU.add).then_inc(ln_stats, 1)
            for t in range(T):
                if t % TB == 0:
                    dve.wait_ge(ln_std, 12 + t // TB + 1)
                    me.link(v.reciprocal(rstds[:, 0, t:t + TB], std[:, 0, t:t + TB]))
                me.link(v.scalar_tensor_tensor(out=z[:, t, :], in0=z[:, t, :], scalar=mv[:, t, 0:1], in1=lnw,
                                               op0=ALU.subtract, op1=ALU.mult))
                v.scalar_tensor_tensor(out=t3[:, t, :], in0=z[:, t, :], scalar=rstd[:, t:t + 1], in1=t1[:, t, :],
                                       op0=ALU.mult, op1=ALU.add).then_inc(out_ready, 1)

        @block.tensor
        def _(pe):
            m = nc.tensor

            def tp(dst, src, k):
                return m.transpose(dst, src, ident[0:k, 0:k])

            def transpose_tiles(src, ready, first, done):
                for b in range(B):
                    for s in range(TB):
                        if ready is not None:
                            pe.wait_ge(ready, first + b * TB + s + 1)
                        ins = tp(ps[:, b, s * P:(s + 1) * P], src[:, b * TB + s, :], P)
                    ins.then_inc(done, 1)

            pe.wait_ge(consts, 2)
            pe.wait_ge(ld_cx, 32)
            for b in range(B):
                tp(ps[:, 2, b * J:(b + 1) * J], cx[:, b, :], J)
            tp(ps[:, 2, B * J:B * J + 3], wsim_row[:, :], 3).then_inc(cx_tp, 1)
            pe.wait_ge(cxT_ready, 1)
            m.matmul(ps[0:1, 3, 0:B * J], wsim[:, 1:2], cxT[:, :], start=True, stop=True).then_inc(simrow_mm, 1)
            transpose_tiles(xn, ln_out, 0, ln_tp)
            pe.wait_ge(rT_ready, 2)
            pe.wait_ge(simrow_ready, 1)
            for b in range(B):
                pe.wait_ge(xT_ready, b + 1)
                for s in range(TB):
                    o = ps[:, 2 + b, s * J:(s + 1) * J]
                    m.matmul(o, xT[:, (b * TB + s) * P:(b * TB + s + 1) * P], rT[:, b * J:(b + 1) * J], start=True, stop=False)
                    ins = m.matmul(o, ones_f[0:1, :], simrow[0:1, b * J:(b + 1) * J], start=False, stop=True)
                ins.then_inc(sim_mm, 1)
            pe.wait_ge(simmax, 1)
            for t in range(T):
                ins = tp(ps[0:1, t // TB, (t % TB) * P:(t % TB + 1) * P], small[:, t:t + 1], P)
            ins.then_inc(mrow_tp, 1)
            pe.wait_ge(mrow_max, 1)
            m.matmul(ps[:, 4, 0:B], ones_f[0:1, :], rowmax[0:1, :], start=True, stop=True).then_inc(mrow_mm, 1)
            pe.wait_ge(batt_exp, 1)
            m.matmul(ps[:, 4, 8:16], ones_f[:, :], small[:, 16:24], start=True, stop=True)
            for t in range(T):
                ins = m.matmul(ps[:, 5, t // TB:t // TB + 1], xn[:, t, :], small[:, 16 + t:17 + t],
                               start=(t % TB == 0), stop=(t % TB == TB - 1))
            ins.then_inc(batt_mm, 1)
            pe.wait_ge(sim_norm, 1)
            for t in range(T):
                ins = tp(ps[0:J, 6 + t // TB, (t % TB) * P:(t % TB + 1) * P], simA[:, t, :], P)
                if t % TB == TB - 1:
                    ins.then_inc(simT_tp, 1)
            for b in range(B):
                pe.wait_ge(simT_ready, b + 1)
                m.matmul(bank(b), cx[:, b, :], simT[:, b * SEQ:(b + 1) * SEQ], start=True, stop=True).then_inc(hq_mm, 1)
            pe.wait_ge(w14_ready, 1)
            for b in range(B):
                pe.wait_ge(prodT_ready, b + 1)
                for s in range(TB):
                    o = ps[:, 2 + b, s * P:(s + 1) * P]
                    c = slice((b * TB + s) * P, (b * TB + s + 1) * P)
                    m.matmul(o, xT[:, c], w14[:, b, :], start=True, stop=False)
                    m.matmul(o, hqT[:, c], wqv[:, 1, :], start=False, stop=False)
                    ins = m.matmul(o, prodT[:, c], wqv[:, 2, :], start=False, stop=True)
                ins.then_inc(hcq_mm, 1)

            transpose_tiles(xn, ln_out, T, ln_tp)
            pe.wait_ge(ld_wx, 16 * N_WX)
            for t in range(T):
                if t % TB == 0:
                    pe.wait_ge(xT_ready, 2 + t // TB + 1)
                ins = m.matmul(ps[:, 2, t * E0:(t + 1) * E0], xT[:, t * P:(t + 1) * P], wg0[:, :], start=True, stop=True)
            ins.then_inc(logits_mm, 1)
            pe.wait_ge(onehot, 1)
            o0 = [oh[k][:, 0:T * E0].rearrange("p (t e) -> p t e", e=E0) for k in range(2)]
            for k in range(2):
                loc = ps[:, 3 + k, 0:T * E0].rearrange("p (t e) -> p t e", e=E0)
                m.matmul(loc, before[:, :], o0[k], start=True, stop=False)
                for t in range(T - 1):
                    m.matmul(loc[:, t + 1:T, :], ones_b[:, :], o0[k][:, t:t + 1, :].to_broadcast([P, T - 1 - t, E0]),
                             start=False, stop=(k == 0 and t == T - 2))
                if k == 1:
                    for t in range(T):
                        ins = m.matmul(loc, ones_b[:, :], o0[0][:, t:t + 1, :].to_broadcast([P, T, E0]),
                                       start=False, stop=(t == T - 1))
            ins.then_inc(loc_mm, 1)
            pe.wait_ge(ld_vec, 16 * N_VEC)
            pe.wait_ge(qk_order, 3)
            tp(ps[:, 7, 0:NV], vrow[:, :], NV)
            tp(ps[:, 7, V_BSQ:V_BSK + 1], vrow_qk[:, :], 2).then_inc(cx_tp, 1)
            m.matmul(ps[:, 0, 0:B * J], wx[:, W_CK, :], imgT[:, :], start=True, stop=True).then_inc(kc_mm, 1)
            for b in range(B):
                ins = m.matmul(ps[0:J, 1, b * D:(b + 1) * D], imgT[:, b * J:(b + 1) * J], wx[:, W_CV, :], start=True, stop=True)
            ins.then_inc(kc_mm, 1)

            def slots0_transposes(c):
                pe.wait_ge(ld_slots[c], 16)
                if c == 0:
                    pe.wait_ge(kc_ready, 1)
                elif c == 1:
                    pe.wait_ge(vc_ready, 1)
                else:
                    pe.wait_ge(slots0T_ready, c - 1)
                for i in range(4):
                    ins = tp(ps[:, c % 2, i * P:(i + 1) * P], slots0[:, 4 * c + i, :], P)
                ins.then_inc(slots0_tp, 1)

            slots0_transposes(0)
            pe.wait_ge(ld_w0, 32)
            for e in range(E0 + 1):
                if e < E0:
                    if e % 2 == 0 and e // 2 + 1 < 4:
                        slots0_transposes(e // 2 + 1)
                    pe.wait_ge(slots0T_ready, e // 2 + 1)
                    for f in range(4):
                        if e >= 2 and f % 2 == 0:
                            pe.wait_ge(h0_dve if f else h0_act, e - 1)
                        elif e < 2 and f == 0:
                            pe.wait_ge(rows_ready, 1)
                        ins = m.matmul(ps[:, 2 + 2 * (e % 2) + f // 2, (f % 2) * C0:(f % 2 + 1) * C0],
                                       w1_0[:, e, f * P:(f + 1) * P], slots0T[:, e * C0:(e + 1) * C0], start=True, stop=True)
                        if f % 2:
                            ins.then_inc(h0_mm, 1)
                if e >= 1:
                    q = e - 1
                    pe.wait_ge(h0_act, q + 1)
                    pe.wait_ge(h0_dve, q + 1)
                    if q >= 2:
                        pe.wait_ge(y0_row, q - 1)
                    for r in range(2):
                        for f in range(4):
                            ins = m.matmul(ps[:, 6 + q % 2, r * D:(r + 1) * D], hid0[q % 2][:, f, r * P:(r + 1) * P],
                                           w2_0[:, 4 * q + f, :], start=(f == 0), stop=(f == 3))
                    ins.then_inc(y0_mm, 1)

            transpose_tiles(xn, ln_out, 2 * T, ln_tp)
            for w, bk in ((0, 2), (1, 4)):
                for b in range(B):
                    pe.wait_ge(xT_ready, 4 + b + 1)
                    m.matmul(bank(bk + b), wx_qk[:, w, :], xT[:, b * SEQ:(b + 1) * SEQ], start=True, stop=True).then_inc(qk_mm, 1)
            for b in range(B):
                for s in range(TB):
                    ins = m.matmul(ps[:, 6 + b, s * D:(s + 1) * D], xT[:, (b * TB + s) * P:(b * TB + s + 1) * P],
                                   wx[:, W_SV, :], start=True, stop=True)
                ins.then_inc(v_mm, 1)

            def score_row_tile(n):
                hg, r = n // MU, n % MU
                t, h = r // 4, 4 * hg + r % 4
                b = t // TB
                if n == 0:
                    pe.wait_ge(ld_qk[0], 16 * 9)
                elif n == MU:
                    pe.wait_ge(ld_qk[1], 16 * 6)
                if n >= 2:
                    pe.wait_ge(s1_max, n - 1)
                m.matmul(bank(4 + n % 2), Q9[0:KP, h, t * P:(t + 1) * P], K9[0:KP, h, b * SEQ:(b + 1) * SEQ],
                         start=True, stop=True).then_inc(s1_mm, 1)

            def max_transpose(hg, units):
                pe.wait_ge(s1_max, MU * (hg + 1))
                if units > 0:
                    pe.wait_ge(o_norm, units)
                tp(ps[0:MU, 7, 0:P], mcol[:, hg, :], P).then_inc(max_tp, 1)

            def score_pair(idx):
                st, pair = idx // 2, idx % 2
                hg, b, kt = st // 8, st % 8 // 4, st % 4
                if idx >= 2:
                    pe.wait_ge(s2_exp, idx - 1)
                for j in range(2):
                    h = 4 * hg + 2 * pair + j
                    k0 = b * SEQ + kt * P
                    ins = m.matmul(bank(2 * (idx % 2) + j), K9[0:KP, h, k0:k0 + P], Q9[0:KP, h, b * SEQ:(b + 1) * SEQ],
                                   start=True, stop=True)
                ins.then_inc(s2_mm, 1)

            def values(st):
                hg, b, kt, u = st // 8, st % 8 // 4, st % 4, st // 4
                pe.wait_ge(s2_exp, 2 * st + 2)
                if kt == 0 and u >= 1:
                    pe.wait_ge(oT_ready, u)
                for hh in range(4):
                    ins = m.matmul(ps[32 * hh:32 * hh + HD + 1, 6, :], vaug[:, b * TB + kt, 4 * hg + hh, :],
                                   probs[(2 * st + hh // 2) % 4][:, (hh % 2) * SEQ:(hh % 2 + 1) * SEQ],
                                   start=(kt == 0), stop=(kt == TB - 1))
                ins.then_inc(pv_mm, 1)

            def out_transposes(u):
                pe.wait_ge(oT_ready, u + 1)
                if u >= 1:
                    pe.wait_ge(o_norm, u)
                for s in range(TB):
                    ins = tp(ps[:, 7, s * P:(s + 1) * P], oT[u % 2][:, s * P:(s + 1) * P], P)
                ins.then_inc(o_tp, 1)

            pe.wait_ge(qk_ready, 2)
            pe.wait_ge(v_ready, 2)
            for n in range(MU):
                score_row_tile(n)
            max_transpose(0, 0)
            for n in range(MU, LEAD):
                score_row_tile(n)
            def row_tiles(n, count):
                for k in range(n, min(n + count, MU * HG)):
                    score_row_tile(k)

            for st in range(8 * HG + 1):
                n = LEAD + 4 * st
                if st < 8 * HG:
                    if st % 8 == 0:
                        pe.wait_ge(ld_max[st // 8], 16 * 3)
                    score_pair(2 * st)
                row_tiles(n, 1)
                if st % 8 == 5 and st // 8 + 1 < HG:
                    max_transpose(st // 8 + 1, 2 * (st // 8))
                if st < 8 * HG:
                    score_pair(2 * st + 1)
                row_tiles(n + 1, 1)
                if st >= 1:
                    values(st - 1)
                row_tiles(n + 2, 1)
                if st % 4 == 2 and st >= 6:
                    pe.wait_ge(max_neg, min(HG, 1 + (st + 3) // 8))
                    out_transposes(st // 4 - 1)
                row_tiles(n + 3, 1)
            out_transposes(2 * HG - 1)

            def project(i, w):
                pe.wait_ge(o_norm, 2 * HG * (i + 1))
                transpose_tiles(attn, None, 0, attn_tp)
                for b in range(B):
                    pe.wait_ge(attnT_ready, 2 * i + b + 1)
                    for s in range(TB):
                        ins = m.matmul(ps[:, 2 + b, s * D:(s + 1) * D], attnT[:, (b * TB + s) * P:(b * TB + s + 1) * P],
                                       wx[:, w, :], start=True, stop=True)
                    ins.then_inc(proj_mm, 1)

            project(0, W_SO)

            transpose_tiles(xn, ln_out, 3 * T, ln_tp)
            for b in range(B):
                pe.wait_ge(xT_ready, 6 + b + 1)
                m.matmul(bank(2 + b), wx[:, W_CQ, :], xT[:, b * SEQ:(b + 1) * SEQ], start=True, stop=True).then_inc(qc_mm, 1)
            pe.wait_ge(qc_ready, 1)
            pe.wait_ge(kbd_ready, 1)

            def cross_scores(un):
                t, half = un // 2, un % 2
                if un >= 2:
                    pe.wait_ge(c_sub, un - 1)
                for j in range(2):
                    h = 8 * half + 4 * j
                    ins = m.matmul(ps[:, 2 * (un % 2) + j, 0:4 * J], qcT[:, t * P:(t + 1) * P],
                                   kbd[:, t // TB, h:h + 4, :].rearrange("p h j -> p (h j)"), start=True, stop=True)
                ins.then_inc(c_mm, 1)

            def cross_values(b, hg):
                if hg == 0:
                    pe.wait_ge(c_PT, 16 * (b + 1))
                pe.wait_ge(oT_ready, 2 * HG + HG * b + hg)
                for hh in range(4):
                    ins = m.matmul(ps[32 * hh:32 * hh + HD + 1, 6, :], vcaug[:, b, 4 * hg + hh, :], PT[b][:, 4 * hg + hh, :],
                                   start=True, stop=True)
                ins.then_inc(c_pv, 1)

            cross_scores(0)
            cross_scores(1)
            for un in range(2 * T):
                if un + 2 < 2 * T:
                    cross_scores(un + 2)
                if 9 <= un < 9 + HG:
                    out_transposes(2 * HG + un - 9)
                if 8 <= un < 8 + HG:
                    cross_values(0, un - 8)
                pe.wait_ge(c_exp, un + 1)
                for j in range(2):
                    if un >= 1:
                        pe.wait_ge(c_PT, 2 * un - 1 + j)
                    for i in range(4):
                        ins = tp(ps[0:J, 4 + j, i * P:(i + 1) * P], pc[un % 3][:, 4 * j + i, :], P)
                    ins.then_inc(c_tp, 1)
            for hg in range(HG + 1):
                if hg < HG:
                    cross_values(1, hg)
                if hg >= 1:
                    out_transposes(3 * HG + hg - 1)
            project(1, W_CO)

            transpose_tiles(xn, ln_out, 4 * T, ln_tp)
            pe.wait_ge(ld_ff, 32)
            for b in range(B):
                pe.wait_ge(xT_ready, 8 + b + 1)
                for f in range(4):
                    if b == 0 and f == 1:
                        pe.wait_ge(xT_ready, 10)
                    m.matmul(bank(4 * b + f), ff1[:, f * P:(f + 1) * P], xT[:, b * SEQ:(b + 1) * SEQ],
                             start=True, stop=True).then_inc(ff_mm, 1)
            for b in range(B):
                pe.wait_ge(ff_gelu, 4 * (b + 1))
                for s in range(TB):
                    for f in range(4):
                        ins = m.matmul(ps[:, 4 * b, s * D:(s + 1) * D], geluT[:, f, (b * TB + s) * P:(b * TB + s + 1) * P],
                                       ff2[:, f, :], start=(f == 0), stop=(f == 3))
                ins.then_inc(ff2_mm, 1)

            transpose_tiles(xn, ln_out, 5 * T, ln_tp)
            for t in range(T):
                if t % TB == 0:
                    pe.wait_ge(xT_ready, 10 + t // TB + 1)
                ins = m.matmul(ps[:, 2, t * E1:(t + 1) * E1], xT[:, t * P:(t + 1) * P], wg1[:, :], start=True, stop=True)
            ins.then_inc(logits_mm, 1)
            pe.wait_ge(onehot, 2)
            o1 = [oh[k][:, :].rearrange("p (t e) -> p t e", e=E1) for k in range(2)]
            for k in range(2):
                loc = ps[:, 3 + k, 0:T * E1].rearrange("p (t e) -> p t e", e=E1)
                m.matmul(loc, before[:, :], o1[k], start=True, stop=False)
                m.matmul(loc[:, TB:T, :], ones_b[:, :], o1[k][:, 0:TB, :], start=False, stop=(k == 0))
                if k == 1:
                    for dst in (slice(0, TB), slice(TB, T)):
                        for src in (slice(0, TB), slice(TB, T)):
                            ins = m.matmul(loc[:, dst, :], ones_b[:, :], o1[0][:, src, :], start=False,
                                           stop=(dst.start == TB and src.start == TB))
            ins.then_inc(loc_mm, 1)

            pe.wait_ge(y_parts, 4)
            for gr in range(NG):
                if gr >= 2:
                    pe.wait_ge(slots1T_ready, gr - 1)
                for b in range(B):
                    pe.wait_ge(slot_onehot, B * gr + b + 1)
                    for part in range(3):
                        for half in range(2):
                            ins = m.matmul(ps[:, 6 * (gr % 2) + half, 0:CG // 2], yparts[:, part, gr + TB * b, :],
                                           slot1h[2 * (gr % 2) + b][:, half * (CG // 2):(half + 1) * (CG // 2)],
                                           start=(b == 0 and part == 0), stop=(b == B - 1 and part == 2))
                    ins.then_inc(disp_mm, 1)
            pe.wait_ge(slots1T_ready, NG)
            pe.wait_ge(ld_W1, 16)
            for e in range(E1):
                if e >= 4:
                    pe.wait_ge(h1_dve if e % 2 else h1_act, (e - 4) // 2 + 1)
                m.matmul(ps[0:M1, 2 + e % 4, :], slots1T[:, e * M1:(e + 1) * M1], W1[:, e, :],
                         start=True, stop=True).then_inc(h1_mm, 1)
            pe.wait_ge(comb_ready, 1)
            for t in range(T):
                ins = tp(ps[0:E1, t // TB, (t % TB) * P:(t % TB + 1) * P], comb[:, t, :], P)
                if t % TB == TB - 1:
                    ins.then_inc(comb_tp, 1)
            pe.wait_ge(ld_hid, 64)
            pe.wait_ge(h1_act, E1 // 2)
            pe.wait_ge(h1_dve, E1 // 2)
            pe.wait_ge(combT_ready, 2)
            for t in range(T):
                ins = m.matmul(ps[:, 6 + t // TB, (t % TB) * D:(t % TB + 1) * D], combT[:, t * P:(t + 1) * P], b2_1[:, :],
                               start=True, stop=True)
                if t % TB == TB - 1:
                    ins.then_inc(ob_mm, 1)
            for t in range(T):
                if t >= 4:
                    pe.wait_ge(hvar, t - 3)
                m.matmul(bank(2 + t % 4), combT[:, t * P:(t + 1) * P], b1_1[:, :], start=True, stop=True).then_inc(hb_mm, 1)
            pe.wait_ge(hid_ready, T)
            pe.wait_ge(ld_W2, 16)
            for e in range(E1 + 1):
                if e < E1:
                    pe.wait_ge(ring_dma[e % 4], 16 * (E1 // 4 + e // 4 + 1))
                    if e >= 2:
                        pe.wait_ge(hid1_dve if e % 2 else hid1_act, (e - 2) // 2 + 1)
                    for f in range(4):
                        ins = tp(ps[:, e % 2, f * M1:(f + 1) * M1], ring[e % 4][:, f * P:(f + 1) * P], M1)
                    ins.then_inc(hid1_tp, 1)
                if e >= 1:
                    q = e - 1
                    pe.wait_ge(hid1_dve if q % 2 else hid1_act, q // 2 + 1)
                    if q >= 4:
                        pe.wait_ge(y1_act if q % 2 else y1_dve, (q - 4) // 2 + 1)
                    for f in range(4):
                        ins = m.matmul(ps[0:M1, 2 + q % 4, 0:D], hid1T[q % 4][:, f, :], W2[:, 4 * q + f, :],
                                       start=(f == 0), stop=(f == 3))
                    ins.then_inc(y1_mm, 1)


def kernel(**inputs):
    import numpy as _np
    import concourse.bacc as _bacc
    from concourse import mybir as _mybir
    from concourse.bass_utils import run_bass_kernel_spmd as _run

    nc = _bacc.Bacc("TRN2", target_bir_lowering=False, num_devices=1)
    arrays, args = {}, {}
    for name, value in inputs.items():
        v = _np.ascontiguousarray(value)
        arrays[f"in_{name}_dram"] = v
        args[name] = nc.dram_tensor(f"in_{name}_dram", v.shape, _mybir.dt.from_np(v.dtype), kind="ExternalInput").ap()
    out = nc.dram_tensor("out_0_dram", (2, 512, 128), _mybir.dt.float32, kind="ExternalOutput").ap()
    flamingo_kernel(nc, args, out)
    r = _run(nc, [arrays], core_ids=[0])
    return r.results[0]["out_0_dram"]
```

```python
from contextlib import ExitStack

import concourse.bass as bass
from concourse import mybir

F32 = mybir.dt.float32
BF16 = mybir.dt.bfloat16
U32 = mybir.dt.uint32
ALU = mybir.AluOpType
ACT = mybir.ActivationFunctionType
AX = mybir.AxisListType

P = 128
D = 128
B, SEQ = 2, 512
TB = SEQ // P
T = B * TB
N = B * SEQ
J = 77
NH, HD = 16, 8
HG = NH // 4
QK_SCALE = HD ** -0.5
E0, C0 = 8, 256
F0 = 512
E1, NG, C1 = 24, 4, 22
M1 = NG * C1
CG = E1 * C1
F1 = 512
KP = 96
BIG = 1e30
SKIP = 1e6
LN_EPS = 1e-5
MOE_EPS = 1e-6

V_BSQ, V_BSK, V_BCQ, V_BCK, V_BFF1, V_LN1, V_LN2, V_LN3, V_B1 = 0, 1, 2, 3, 4, 8, 10, 12, 14
NV = V_B1 + E0 * F0 // P
(R_QV, R_SV, R_SO, R_CV, R_CO, R_FF2, R_LNW, R_LNB) = range(8)
(W_SQ, W_SK, W_SV, W_SO, W_CQ, W_CK, W_CV, W_CO) = range(8)
MU = 4 * 8
LEAD = 44


class Chain:

    def __init__(self, eng, sem):
        self.eng, self.sem, self.n = eng, sem, 0

    def step(self, ins):
        ins.then_inc(self.sem, 1)
        self.n += 1
        return self.n

    def wait(self, n=None):
        self.eng.wait_ge(self.sem, self.n if n is None else n)

    def link(self, ins):
        self.step(ins)
        self.wait()


def flamingo_kernel(nc, a, out):
    ctx = ExitStack()
    with ctx:
        def sb(name, shape, dt=F32):
            return ctx.enter_context(nc.sbuf_tensor(name, shape, dt))

        def sem(name):
            return ctx.enter_context(nc.semaphore(name))

        def sems(name, n):
            return [sem(f"{name}{i}") for i in range(n)]

        R0 = sb("R0", [P, 8192])
        w1_0 = R0[:, 0:4096].rearrange("p (e h) -> p e h", e=E0)
        w2_0 = R0[:, 4096:8192].rearrange("p (e m) -> p e m", e=E0 * 4)
        lnw_h = R0[:, 0:2048].rearrange("p (g f) -> p g f", g=NG)
        lnb_h = R0[:, 2048:4096].rearrange("p (g f) -> p g f", g=NG)
        geluT = R0[:, 4096:8192].rearrange("p (f t) -> p f t", f=4)
        yparts = R0[:, 4096:5632].bitcast(BF16).rearrange("p (i t d) -> p i t d", i=3, t=T)
        slot1h = [R0[:, 5632 + CG // 2 * i:5632 + CG // 2 * (i + 1)].bitcast(BF16) for i in range(T)]
        yrow1 = R0[0:M1, 4096:4096 + E1 * D].rearrange("p (e d) -> p e d", e=E1)

        R1 = sb("R1", [P, 24576])

        def r1(start, n, parts=P):
            return R1[0:parts, start:start + n]

        x0 = r1(0, 1024).rearrange("p (t d) -> p t d", t=T)
        xplus = r1(1024, 1024).rearrange("p (t d) -> p t d", t=T)
        x1 = r1(2048, 1024).rearrange("p (t d) -> p t d", t=T)
        hqT = r1(3072, 1024)
        prodT = r1(4096, 1024)
        simA = r1(5120, T * J).rearrange("p (t j) -> p t j", t=T)
        simT = r1(6144, 1024, J)
        wqv = r1(7168, 512).rearrange("p (k n) -> p k n", k=4)
        w14 = r1(7680, 256).rearrange("p (b n) -> p b n", b=B)
        b2_0 = r1(8192, 1024).rearrange("p (e d) -> p e d", e=E0)
        slots0 = r1(9216, 2048).rearrange("p (a d) -> p a d", a=16)
        slots0T = r1(11264, 2048)
        hid0 = [r1(13312 + 1024 * i, 1024).rearrange("p (f c) -> p f c", f=4) for i in range(2)]
        yrow0 = r1(15360, 2048).rearrange("p (a d) -> p a d", a=16)
        got0 = r1(17408, 2048).rearrange("p (t k d) -> p t k d", t=T, k=2)
        Q9 = r1(0, 8192).bitcast(BF16).rearrange("p (h t) -> p h t", h=NH)
        K9 = r1(8192, 8192).bitcast(BF16).rearrange("p (h t) -> p h t", h=NH)
        probs = [r1(16384 + 1024 * i, 1024) for i in range(4)]
        qparts = r1(20480, 1536).bitcast(BF16).rearrange("p (i t) -> p i t", i=3)
        kparts = r1(22016, 1536).bitcast(BF16).rearrange("p (i t) -> p i t", i=3)
        qcT = r1(16384 + 2048, 1024)
        PT = [r1(8192 * b, 8192, J).rearrange("p (h t) -> p h t", h=NH) for b in range(B)]
        PC = 8 * J
        pc = [r1(16384 + PC * i, PC).rearrange("p (h j) -> p h j", h=8) for i in range(3)]
        W1 = r1(0, 12288).rearrange("p (e f) -> p e f", e=E1)
        W2 = r1(12288, 12288).rearrange("p (e m) -> p e m", e=E1 * 4)
        got1 = [r1(2 * F1 * i, 2 * F1).rearrange("p (k f) -> p k f", k=2) for i in range(4)]
        HP = 3 * F1 // 2
        hparts = [(R0[:, 4096 + HP * i:4096 + HP * (i + 1)] if i < 2 else r1(10432 + HP * (i - 2), HP))
                  .bitcast(BF16).rearrange("p (i f) -> p i f", i=3) for i in range(4)]
        got2 = r1(0, 2048).rearrange("p (t k d) -> p t k d", t=T, k=2)

        R2 = sb("R2", [P, 2048])
        oT = [R2[:, 512 * i:512 * i + 512] for i in range(2)]
        slot_iota = R2[:, 1024:1024 + CG]
        ring = [R2[0:M1, 512 * i:512 * i + 512] for i in range(4)]

        R3 = sb("R3", [P, B * NH * J])
        kbd = R3[:, :].rearrange("p (b h j) -> p b h j", b=B, h=NH)
        slots1T = R3[:, 0:E1 * M1]
        hid1T = [r1(4096 + E1 * M1 * f, E1 * M1) for f in range(3)] + [R3[:, 0:E1 * M1]]

        t1 = sb("t1", [P, T, D])
        t2 = sb("t2", [P, T, D])
        t3 = sb("t3", [P, T, D])
        xn = sb("xn", [P, T, D])
        xT = sb("xT", [P, N])
        attn = sb("attn", [P, T, D])
        attnT = sb("attnT", [P, N])
        flat = lambda tile: tile[:, :, :].rearrange("p t d -> p (t d)")
        x2, xres, xa = t1, t2, t3
        qf, kf = flat(attn), attnT[:, :]
        combT = attnT[0:E1, :]
        hsum = [flat(tile)[:, F1 * i:F1 * (i + 1)] for tile in (t2, attn) for i in range(2)]

        ident = sb("ident", [P, P])
        ones_f = sb("ones_f", [P, P])
        ones_b = sb("ones_b", [P, P], BF16)
        before = sb("before", [P, P], BF16)
        rev = sb("rev", [P, E1])
        group_row = sb("group_row", [P, T])
        head_of = sb("head_of", [P, NH])
        zeros = sb("zeros", [P, 512])
        wsim_row = sb("wsim_row", [3, P])
        wsim = sb("wsim", [P, 3])
        vrow = sb("vrow", [NV, P])
        vrow_qk = sb("vrow_qk", [2, P])
        wx_qk = sb("wx_qk", [P, 2, P])
        vcol = sb("vcol", [P, NV])
        bias = sb("bias", [P, 8, D])
        gates = sb("gates", [P, 4])
        tg = sb("tg", [P, 6])
        bsim = sb("bsim", [1, 1])
        wx = sb("wx", [P, 8, D])
        wg0 = sb("wg0", [P, E0])
        wg1 = sb("wg1", [P, E1])
        ff1 = sb("ff1", [P, 512])
        ff2 = sb("ff2", [P, 4, D])
        cx = sb("cx", [J, B, D])
        cxT = sb("cxT", [P, B * J])
        imgT = sb("imgT", [P, B * J])
        rT = sb("rT", [P, B * J])
        simrow = sb("simrow", [1, B * J])
        kcT = sb("kcT", [P, B * J])
        vaug = sb("vaug", [P, T, NH, HD + 1])
        vcaug = sb("vcaug", [J, B, NH, HD + 1])
        st6 = sb("st6", [P, T, 6])
        mv = sb("mv", [P, T, 2])
        var_eps = sb("var_eps", [P, 2, T])
        std = sb("std", [P, 2, T])
        rstds = sb("rstds", [P, 2, T])
        rstd, rstd2 = rstds[:, 0, :], rstds[:, 1, :]
        tmp8 = sb("tmp8", [P, T])
        tmp8b = sb("tmp8b", [P, T])
        small = sb("small", [P, 64])
        rowmax = sb("rowmax", [1, B])
        mcol = sb("mcol", [P, HG, MU])
        mneg = sb("mneg", [MU, P])
        mparts = R0[0:MU, 4096:4096 + HG * 3 * P // 2].bitcast(BF16).rearrange("p (g i c) -> p g i c", g=HG, i=3)
        rden = sb("rden", [P, NH])
        rdl = sb("rdl", [P, T * E1])
        rkey = sb("rkey", [P, T * E1])
        rtmp = sb("rtmp", [P, T * E1])
        oh = [sb(f"oh{k}", [P, T * E1], BF16) for k in range(2)]
        rs = sb("rs", [P, 16, T])
        srow0 = sb("srow0", [P, 2, T], U32)
        grow = [sb(f"grow{k}", [P, 2, T], U32) for k in range(2)]
        gate = [sb(f"gate{k}", [P, 2, T]) for k in range(2)]
        b1_1 = xT[0:E1, 0:F1]
        b2_1 = xT[0:E1, F1:F1 + D]
        comb = xT[:, 640:640 + T * E1].rearrange("p (t e) -> p t e", t=T)

        ps = ctx.enter_context(nc.psum_tensor("ps", [P, 8, 512], F32))
        bank = lambda i: ps[:, i, :]

        disp0_d = nc.dram_tensor("disp0_d", (E0 * C0, D), F32).ap()
        y0_d = nc.dram_tensor("y0_d", (E0 * C0, D), F32).ap()
        qk_d = nc.dram_tensor("qk_d", (2, 3, P, N), BF16).ap()
        h1_d = nc.dram_tensor("h1_d", (E1 * M1, F1), F32).ap()
        y1_d = nc.dram_tensor("y1_d", (E1 * M1, D), F32).ap()

        pool_self, dve_self, act_self = sem("pool_self"), sem("dve_self"), sem("act_self")
        consts = sem("consts")
        ld_x, ld_cx, ld_vec, ld_gate = sem("ld_x"), sem("ld_cx"), sem("ld_vec"), sem("ld_gate")
        ld_wqv, ld_bias, ld_wx, ld_w0 = sem("ld_wqv"), sem("ld_bias"), sem("ld_wx"), sem("ld_w0")
        ld_ff, ld_hid, ld_W1, ld_W2 = sem("ld_ff"), sem("ld_hid"), sem("ld_W1"), sem("ld_W2")
        zeroed = sem("zeroed")
        ln_stats, ln_std, ln_out, ln_tp, xT_ready = (
            sem("ln_stats"), sem("ln_std"), sem("ln_out"), sem("ln_tp"), sem("xT_ready"))
        tanh_ready, vcol_ready = sem("tanh_ready"), sem("vcol_ready")
        cx_tp, cxT_ready, rT_ready, simrow_mm, simrow_ready = (
            sem("cx_tp"), sem("cxT_ready"), sem("rT_ready"), sem("simrow_mm"), sem("simrow_ready"))
        sim_mm, simmax, sim_sub, sim_exp, sim_norm = (
            sem("sim_mm"), sem("simmax"), sem("sim_sub"), sem("sim_exp"), sem("sim_norm"))
        mrow_tp, mrow_max, mrow_mm, batt_sub, batt_exp, batt_mm = (
            sem("mrow_tp"), sem("mrow_max"), sem("mrow_mm"), sem("batt_sub"), sem("batt_exp"), sem("batt_mm"))
        simT_tp, simT_ready, hq_mm, hqT_ready, prodT_ready, w14_ready, hcq_mm, x1_ready = (
            sem("simT_tp"), sem("simT_ready"), sem("hq_mm"), sem("hqT_ready"), sem("prodT_ready"),
            sem("w14_ready"), sem("hcq_mm"), sem("x1_ready"))
        logits_mm, route_sub, route_exp, onehot, loc_mm, rows_ready = (
            sem("logits_mm"), sem("route_sub"), sem("route_exp"), sem("onehot"), sem("loc_mm"), sem("rows_ready"))
        kc_mm, kc_ready, kbd_ready, vc_ready = sem("kc_mm"), sem("kc_ready"), sem("kbd_ready"), sem("vc_ready")
        scattered, ld_slots = sem("scattered"), sems("ld_slots", 4)
        slots0_tp, slots0T_ready, h0_mm, h0_act, h0_dve, y0_mm, y0_row, y0_wr = (
            sem("slots0_tp"), sem("slots0T_ready"), sem("h0_mm"), sem("h0_act"), sem("h0_dve"),
            sem("y0_mm"), sem("y0_row"), sem("y0_wr"))
        gathered = sems("gathered", T)
        x2_ready = sem("x2_ready")
        qk_mm, v_mm, qk_ready, qk_parts, v_ready = (
            sem("qk_mm"), sem("v_mm"), sem("qk_ready"), sem("qk_parts"), sem("v_ready"))
        part_wr = sems("part_wr", 4)
        ld_qk, ld_max = sems("ld_qk", 2), sems("ld_max", HG)
        qk_order = sem("qk_order")
        s1_mm, s1_max, max_tp, max_neg, max_parts = (
            sem("s1_mm"), sem("s1_max"), sem("max_tp"), sem("max_neg"), sem("max_parts"))
        s2_mm, s2_exp, pv_mm, oT_ready, o_tp, o_norm = (
            sem("s2_mm"), sem("s2_exp"), sem("pv_mm"), sem("oT_ready"), sem("o_tp"), sem("o_norm"))
        attn_tp, attnT_ready, proj_mm, xa_ready = sem("attn_tp"), sem("attnT_ready"), sem("proj_mm"), sem("xa_ready")
        qc_mm, qc_ready, c_mm, c_sub, c_exp, c_tp, c_PT, c_pv = (
            sem("qc_mm"), sem("qc_ready"), sem("c_mm"), sem("c_sub"), sem("c_exp"), sem("c_tp"), sem("c_PT"), sem("c_pv"))
        ff_mm, ff_gelu, ff2_mm, x4_ready = sem("ff_mm"), sem("ff_gelu"), sem("ff2_mm"), sem("x4_ready")
        y_parts, slot_onehot, disp_mm = sem("y_parts"), sem("slot_onehot"), sem("disp_mm")
        slots1T_ready, h1_mm, h1_act, h1_dve = (
            sem("slots1T_ready"), sem("h1_mm"), sem("h1_act"), sem("h1_dve"))
        ring_dma = sems("ring_dma", 4)
        comb_ready, comb_tp, combT_ready, hb_mm, hvar, hstd, hid_ready = (
            sem("comb_ready"), sem("comb_tp"), sem("combT_ready"), sem("hb_mm"), sem("hvar"), sem("hstd"),
            sem("hid_ready"))
        hid_p1, hid_r1, hid_p2, hid_p3, hdisp_mm, hid1T_ready = (
            sem("hid_p1"), sem("hid_r1"), sem("hid_p2"), sem("hid_p3"), sem("hdisp_mm"), sem("hid1T_ready"))
        hid_last, hid1T_dve = sem("hid_last"), sem("hid1T_dve")
        y1_mm, y1_act, y1_dve, y1_wr = sem("y1_mm"), sem("y1_act"), sem("y1_dve"), sem("y1_wr")
        ob_mm, out_ready, out_done = (
            sem("ob_mm"), sem("out_ready"), sem("out_done"))

        N_VEC, N_BIAS, N_WX = 12, 9, 10
        paired = [gr + TB * b for gr in range(NG) for b in range(B)]
        chunk_bank = lambda c: 6 * (c % 2) if c < 4 * (NG - 1) else (0, 6, 2, 4)[c % 4]
        row = lambda v: v.rearrange("(a d) -> a d", a=1)
        block = ctx.enter_context(nc.Block())

        @block.sync
        def _(sp):
            for b in range(B):
                sp.dma_start(x0[:, b * TB:(b + 1) * TB, :], a["x"][b].rearrange("(s p) d -> p s d", p=P)).then_inc(ld_x, 16)
            sp.dma_start(cx[:, :, :], a["ctx_1024"].rearrange("b j d -> j b d")).then_inc(ld_cx, 16)
            sp.dma_start(wsim_row[:, :], a["L0_xattn_w_sim"].rearrange("(k d) -> k d", k=3)).then_inc(ld_cx, 16)
            sp.dma_start(gates[:, 0:2], row(a["g_xattn"]).to_broadcast([P, 2])).then_inc(ld_gate, 16)
            sp.dma_start(gates[:, 2:4], row(a["g_ffn"]).to_broadcast([P, 2])).then_inc(ld_gate, 16)
            sp.dma_start(bsim[:, :], row(a["L0_xattn_b_sim"])).then_inc(ld_gate, 16)
            sp.dma_start(wqv, a["L0_xattn_W_qv"].rearrange("(k p) n -> p k n", p=P)).then_inc(ld_wqv, 16)
            for r, name in enumerate(("L0_xattn_b_qv", "L1_xattn_b_sv", "L1_xattn_b_so", "L1_xattn_b_cv", "L1_xattn_b_co",
                                      "L1_xattn_b_ff2", "L1_ffn_ln_out_w", "L1_ffn_ln_out_b")):
                sp.dma_start(bias[:, r, :], row(a[name]).to_broadcast([P, D])).then_inc(ld_bias, 16)
            sp.dma_start(b2_0.rearrange("p e d -> p (e d)"),
                         row(a["L0_ffn_b2"].rearrange("e d -> (e d)")).to_broadcast([P, E0 * D])).then_inc(ld_bias, 16)
            sp.dma_start(wg0[:, :], a["L0_ffn_wg"]).then_inc(ld_wx, 16)
            sp.dma_start(wg1[:, :], a["L1_ffn_Wg"]).then_inc(ld_wx, 16)
            for w, name in enumerate(("sq", "sk", "sv", "so", "cq", "ck", "cv", "co")):
                sp.dma_start(wx[:, w, :], a["L1_xattn_W_" + name]).then_inc(ld_wx, 16)
            for name, r in (("b_sq", V_BSQ), ("b_sk", V_BSK), ("b_cq", V_BCQ), ("b_ck", V_BCK),
                            ("g_ln1", V_LN1), ("b_ln1", V_LN1 + 1), ("g_ln2", V_LN2), ("b_ln2", V_LN2 + 1),
                            ("g_ln3", V_LN3), ("b_ln3", V_LN3 + 1)):
                sp.dma_start(vrow[r:r + 1, :], row(a["L1_xattn_" + name])).then_inc(ld_vec, 16)
            sp.dma_start(vrow[V_BFF1:V_BFF1 + 4, :], a["L1_xattn_b_ff1"].rearrange("(k d) -> k d", k=4)).then_inc(ld_vec, 16)
            sp.dma_start(vrow[V_B1:NV, :], a["L0_ffn_b1"].rearrange("e (k f) -> (e k) f", f=P)).then_inc(ld_vec, 16)
            sp.wait_ge(consts, 1)
            sp.dma_start(disp0_d.rearrange("(p a) d -> p (a d)", p=P).rearrange("p (a z) -> p a z", z=512),
                         zeros[:, 0:512].unsqueeze(1).to_broadcast([P, 4, 512])).then_inc(zeroed, 16)
            sp.dma_start(w1_0, a["L0_ffn_w1"].rearrange("e m h -> m e h")).then_inc(ld_w0, 16)
            sp.dma_start(w2_0, a["L0_ffn_w2"].rearrange("e (k f) m -> f (e k) m", f=P)).then_inc(ld_w0, 16)
            sp.dma_start(ff1[:, :], a["L1_xattn_W_ff1"]).then_inc(ld_ff, 16)
            sp.dma_start(ff2[:, :, :], a["L1_xattn_W_ff2"].rearrange("(k f) m -> f k m", f=P)).then_inc(ld_ff, 16)

            sp.wait_ge(scattered, 16 * 2 * T)
            for c in range(4):
                sp.dma_start(slots0[:, 4 * c:4 * c + 4, :],
                             disp0_d[512 * c:512 * c + 512, :].rearrange("(a p) d -> p a d", p=P)).then_inc(ld_slots[c], 16)
            for e in range(E0):
                sp.wait_ge(y0_row, e + 1)
                sp.dma_start(y0_d[C0 * e:C0 * e + C0, :].rearrange("(a p) d -> p a d", p=P),
                             yrow0[:, 2 * e:2 * e + 2, :]).then_inc(y0_wr, 16)

            sp.wait_ge(x2_ready, T)
            ones_src = ones_b[72:75, :].unsqueeze(1)
            zsrc = lambda lo: zeros[lo:KP, 0:512].bitcast(BF16).unsqueeze(1).to_broadcast([KP - lo, NH, N])
            sp.dma_start(Q9[72:KP, :, :], zsrc(72)).then_inc(ld_qk[0], 16)
            sp.dma_start(K9[75:KP, :, :], zsrc(75)).then_inc(ld_qk[0], 16)
            sp.dma_start(K9[72:75, :, :].rearrange("p h (u q) -> p (h u) q", q=P),
                         ones_src.to_broadcast([3, NH * T, P])).then_inc(ld_qk[0], 16)

            def load_packed(which, c, heads, n):
                src = (qk_d[0, c].unsqueeze(0).to_broadcast([3, P, N]) if which == 0 else qk_d[1])
                src = src.rearrange("i (d h) t -> i d h t", d=HD)[:, :, heads, :].rearrange("i d h t -> i d (h t)")
                sp.dma_start((Q9, K9)[which][24 * c:24 * c + 24, heads, :].rearrange("r h t -> r (h t)"), src).then_inc(ld_qk[n], 16)

            for part in range(3):
                sp.wait_ge(part_wr[part], 16)
                load_packed(0, part, slice(0, 4), 0)
            sp.wait_ge(part_wr[3], 3 * 16)
            for part in range(3):
                load_packed(1, part, slice(0, 4), 0)
            for which in range(2):
                for part in range(3):
                    load_packed(which, part, slice(4, NH), 1)
            for hg in range(HG):
                sp.wait_ge(max_parts, hg + 1)
                for i in range(3):
                    sp.dma_start(Q9[72 + i:73 + i, 4 * hg:4 * hg + 4, :].rearrange("p h (t q) -> p (h t) q", q=P),
                                 mparts[:, hg, i, :]).then_inc(ld_max[hg], 16)

            sp.dma_start(lnw_h, a["L1_ffn_ln_hid_w"].rearrange("g f -> (g f)").rearrange("(a d) -> a d", a=1)
                         .to_broadcast([P, NG * F1]).rearrange("p (g f) -> p g f", g=NG)).then_inc(ld_hid, 16)
            sp.dma_start(lnb_h, a["L1_ffn_ln_hid_b"].rearrange("g f -> (g f)").rearrange("(a d) -> a d", a=1)
                         .to_broadcast([P, NG * F1]).rearrange("p (g f) -> p g f", g=NG)).then_inc(ld_hid, 16)

            sp.wait_ge(o_norm, 4 * HG)
            sp.dma_start(W1, a["L1_ffn_W1"].rearrange("e m h -> m e h")).then_inc(ld_W1, 16)
            sp.dma_start(W2, a["L1_ffn_W2"].rearrange("e (k f) m -> f (e k) m", f=P)).then_inc(ld_W2, 16)

            sp.wait_ge(logits_mm, 2)
            sp.dma_start(b1_1, a["L1_ffn_b1"]).then_inc(ld_hid, 16)
            sp.dma_start(b2_1, a["L1_ffn_b2"]).then_inc(ld_hid, 16)

            for e in range(E1):
                sp.wait_ge(h1_dve if e % 2 else h1_act, e // 2 + 1)
                sp.dma_start(h1_d[M1 * e:M1 * (e + 1), :], ring[e % 4]).then_inc(ring_dma[e % 4], 16)
            for e in range(E1):
                sp.wait_ge(y1_act if e % 2 else y1_dve, e // 2 + 1)
                sp.dma_start(y1_d[M1 * e:M1 * (e + 1), :], yrow1[:, e, :]).then_inc(y1_wr, 16)
            for b in range(B):
                sp.wait_ge(out_ready, TB * (b + 1))
                sp.dma_start(out[b].rearrange("(s p) d -> p s d", p=P), t3[:, b * TB:(b + 1) * TB, :]).then_inc(out_done, 16)
            sp.wait_ge(out_done, 16 * B)

        @block.gpsimd
        def _(pool):
            me = Chain(pool, pool_self)
            g = nc.gpsimd
            g.memset(zeros[:, :], 0.0).then_inc(consts, 1)
            me.step(g.memset(ident[:, :], 0.0))
            me.step(g.memset(ones_f[:, :], 1.0))
            me.step(g.memset(ones_b[:, :], 1.0))
            me.step(g.memset(head_of[:, :], 1.0))
            me.link(g.memset(before[:, :], 1.0))
            me.step(g.affine_select(out=ident[:, :], in_=ident[:, :], compare_op=ALU.not_equal, fill=1.0, base=0,
                                    pattern=[[-1, P]], channel_multiplier=1))
            me.step(g.affine_select(out=before[:, :], in_=before[:, :], compare_op=ALU.is_gt, fill=0.0, base=0,
                                    pattern=[[1, P]], channel_multiplier=-1))
            me.link(g.affine_select(out=head_of[:, :], in_=head_of[:, :], compare_op=ALU.is_ge, fill=0.0, base=0,
                                    pattern=[[-HD, NH]], channel_multiplier=1))
            me.step(g.affine_select(out=head_of[:, :], in_=head_of[:, :], compare_op=ALU.is_ge, fill=0.0, base=HD - 1,
                                    pattern=[[HD, NH]], channel_multiplier=-1))
            me.step(g.iota(rev[:, :], [[-1, E1]], base=32, channel_multiplier=0, allow_small_or_imprecise_dtypes=True))
            me.step(g.iota(group_row[:, :].rearrange("p (b s) -> p b s", b=B), [[0, B], [C1, TB]], base=0,
                           channel_multiplier=0, allow_small_or_imprecise_dtypes=True))
            me.step(g.memset(vaug[:, :, :, HD], 1.0))
            g.memset(vcaug[:, :, :, HD], 1.0).then_inc(consts, 1)

            pool.wait_ge(ld_vec, 16 * N_VEC)
            pool.wait_ge(ld_wx, 16 * N_WX)
            by_dim = "p (h d) -> p d h"
            g.tensor_copy(vrow_qk[:, :].rearrange("p (d h) -> p d h", d=HD),
                          vrow[V_BSQ:V_BSK + 1, :].rearrange(by_dim, d=HD)).then_inc(qk_order, 1)
            for i, w in enumerate((W_SQ, W_SK)):
                g.tensor_copy(wx_qk[:, i, :].rearrange("p (d h) -> p d h", d=HD),
                              wx[:, w, :].rearrange(by_dim, d=HD)).then_inc(qk_order, 1)

            def scatter(rows, index, dst, last_row):
                for t in range(T):
                    for k in range(2):
                        g.indirect_dma_start(dst, bass.IndirectOffsetOnAxis(ap=index[:, k, t:t + 1], axis=0), rows[:, t, :],
                                             None, bounds_check=last_row, oob_is_err=False).then_inc(scattered, 16)

            def gather(into, index, src, t):
                for k in range(2):
                    g.indirect_dma_start(into[:, t, k, :], None, src,
                                         bass.IndirectOffsetOnAxis(ap=index[:, k, t:t + 1], axis=0)).then_inc(gathered[t], 16)

            pool.wait_ge(rows_ready, 1)
            pool.wait_ge(zeroed, 16)
            scatter(xn, srow0, disp0_d, E0 * C0 - 1)
            pool.wait_ge(kc_ready, 1)
            for b in range(B):
                ins = g.tensor_tensor(kbd[:, b], kcT[:, b * J:(b + 1) * J].unsqueeze(1).to_broadcast([P, NH, J]),
                                      head_of[:, :].unsqueeze(2).to_broadcast([P, NH, J]), ALU.mult)
            ins.then_inc(kbd_ready, 1)
            pool.wait_ge(y0_wr, 16 * E0)
            for t in range(T):
                gather(got0, grow[0], y0_d, t)
            for u in range(HG):
                pool.wait_ge(max_neg, u + 1)
                me.link(g.tensor_copy(mparts[:, u, 0, :], mneg[:, :]))
                me.link(g.tensor_tensor(mneg[:, :], mneg[:, :], mparts[:, u, 0, :], ALU.subtract))
                me.link(g.tensor_copy(mparts[:, u, 1, :], mneg[:, :]))
                g.tensor_tensor(mparts[:, u, 2, :], mneg[:, :], mparts[:, u, 1, :], ALU.subtract).then_inc(max_parts, 1)
            me.link(g.iota(slot_iota, [[1, CG]], base=0, channel_multiplier=0, allow_small_or_imprecise_dtypes=True))
            rest = [flat(t2), yparts[:, 2, :, :].rearrange("p t d -> p (t d)")]
            for i, left in enumerate((flat(xn), flat(t2))):
                pool.wait_ge(y_parts, 2 * i + 1)
                g.tensor_tensor(rest[i], left, yparts[:, i, :, :].rearrange("p t d -> p (t d)"),
                                ALU.subtract).then_inc(y_parts, 1)
            pool.wait_ge(rows_ready, 2)
            for r in range(4):
                pool.wait_ge(ring_dma[r], 16 * (E1 // 4))
            def gather_hidden(q, k):
                t = paired[q]
                g.indirect_dma_start(got1[q % 4][:, k, :], None, h1_d,
                                     bass.IndirectOffsetOnAxis(ap=grow[1][:, k, t:t + 1], axis=0)).then_inc(gathered[t], 16)

            for q in range(4):
                for k in range(2):
                    gather_hidden(q, k)
            for q in range(T - 1):
                pool.wait_ge(hid_p1, q + 1)
                g.tensor_tensor(hsum[q % 4], hsum[q % 4], hparts[q % 4][:, 0, :], ALU.subtract).then_inc(hid_r1, 1)
                if q + 4 < T:
                    gather_hidden(q + 4, 0)
                pool.wait_ge(hid_p2, q + 1)
                g.tensor_tensor(hparts[q % 4][:, 2, :], hsum[q % 4], hparts[q % 4][:, 1, :], ALU.subtract).then_inc(hid_p3, 1)
                if q + 4 < T:
                    gather_hidden(q + 4, 1)
            pool.wait_ge(y1_wr, 16 * E1)
            for t in range(T):
                gather(got2, grow[1], y1_d, t)

        @block.scalar
        def _(act):
            s = nc.scalar

            def evac_xT(i, v):
                for b in range(B):
                    act.wait_ge(ln_tp, 2 * i + b + 1)
                    dst = xT[:, b * SEQ:(b + 1) * SEQ]
                    if v is None:
                        s.copy(dst, bank(b)).then_inc(xT_ready, 1)
                    else:
                        s.activation(dst, bank(b), ACT.Identity, bias=vcol[:, v + 1:v + 2],
                                     scale=vcol[:, v:v + 1]).then_inc(xT_ready, 1)

            def std_of(i, k=1):
                for b in range(B):
                    half = slice(b * TB, (b + 1) * TB)
                    act.wait_ge(ln_stats, 2 * i + b + 1)
                    s.activation(std[:, 0:k, half], var_eps[:, 0:k, half], ACT.Sqrt).then_inc(ln_std, 1)

            act.wait_ge(ld_gate, 48)
            s.activation(tg[:, 0:4], gates[:, :], ACT.Tanh).then_inc(tanh_ready, 1)
            std_of(0)
            evac_xT(0, None)
            act.wait_ge(sim_sub, 1)
            s.activation(simA, simA, ACT.Exp).then_inc(sim_exp, 1)
            act.wait_ge(batt_sub, 1)
            s.activation(small[:, 16:24], small[:, 8:16], ACT.Exp).then_inc(batt_exp, 1)
            for b in range(B):
                act.wait_ge(simT_tp, b + 1)
                s.copy(simT[:, b * SEQ:(b + 1) * SEQ], ps[0:J, 6 + b, :]).then_inc(simT_ready, 1)
            for b in range(B):
                act.wait_ge(hq_mm, b + 1)
                s.copy(hqT[:, b * SEQ:(b + 1) * SEQ], bank(b)).then_inc(hqT_ready, 1)

            def route_exps(i, E):
                act.wait_ge(route_sub, i + 1)
                s.activation(rtmp[:, 0:T * E], rdl[:, 0:T * E], ACT.Exp)
                s.activation(rs[:, 1, :], rs[:, 0, :], ACT.Exp).then_inc(route_exp, 1)

            std_of(1)
            evac_xT(1, None)
            route_exps(0, E0)
            act.wait_ge(cx_tp, 2)
            s.copy(vcol[:, :], ps[:, 7, 0:NV]).then_inc(vcol_ready, 1)
            act.wait_ge(vcol_ready, 1)
            act.wait_ge(kc_mm, 1)
            s.activation(kcT[:, :], ps[:, 0, 0:B * J], ACT.Identity, bias=vcol[:, V_BCK:V_BCK + 1]).then_inc(kc_ready, 1)

            def evac_slots0(c):
                act.wait_ge(slots0_tp, c + 1)
                s.copy(slots0T[:, 512 * c:512 * c + 512], bank(c % 2)).then_inc(slots0T_ready, 1)

            evac_slots0(0)
            for e in range(E0):
                if e % 2 == 0 and e // 2 + 1 < 4:
                    evac_slots0(e // 2 + 1)
                act.wait_ge(h0_mm, 2 * e + 1)
                if e >= 2:
                    act.wait_ge(y0_mm, e - 1)
                for f in range(2):
                    ins = s.activation(hid0[e % 2][:, f, :], ps[:, 2 + 2 * (e % 2), f * C0:(f + 1) * C0], ACT.Relu,
                                       bias=vcol[:, V_B1 + 4 * e + f:V_B1 + 4 * e + f + 1])
                ins.then_inc(h0_act, 1)

            std_of(2, 2)
            evac_xT(2, V_LN1)
            for mm, full, parts, v, bk in ((2, qf, qparts, V_BSQ, 2), (4, kf, kparts, V_BSK, 4)):
                act.wait_ge(qk_mm, mm)
                src = ps[:, bk:bk + 2, :].rearrange("p b t -> p (b t)")
                s.activation(full, src, ACT.Identity, bias=vcol[:, v:v + 1])
                s.activation(parts[:, 0, :], src, ACT.Identity, bias=vcol[:, v:v + 1]).then_inc(qk_ready, 1)
                act.wait_ge(qk_ready, mm // 2)
                act.dma_start(qk_d[mm // 2 - 1, 0], parts[:, 0, :]).then_inc(part_wr[3 * (mm // 2 - 1)], 16)
            for which, parts in enumerate((qparts, kparts)):
                for i in (1, 2):
                    act.wait_ge(qk_parts, 2 * which + i)
                    act.dma_start(qk_d[which, i], parts[:, i, :]).then_inc(part_wr[3 if which else i], 16)

            def negate_max(u):
                act.wait_ge(max_tp, u + 1)
                if u >= 1:
                    act.wait_ge(max_parts, u)
                s.activation(mneg[:, :], ps[0:MU, 7, 0:P], ACT.Copy, scale=-1.0).then_inc(max_neg, 1)

            negate_max(0)

            def evac_oT(u, produced, count):
                act.wait_ge(produced, count)
                if u >= 2:
                    act.wait_ge(o_tp, u - 1)
                s.copy(oT[u % 2], bank(6)).then_inc(oT_ready, 1)

            for st in range(8 * HG + 1):
                for idx in (2 * st, 2 * st + 1):
                    if st < 8 * HG:
                        act.wait_ge(s2_mm, idx + 1)
                        if idx >= 4:
                            act.wait_ge(pv_mm, (idx - 4) // 2 + 1)
                        s.activation(probs[idx % 4], ps[:, 2 * (idx % 2):2 * (idx % 2) + 2, :].rearrange("p b t -> p (b t)"),
                                     ACT.Exp, scale=QK_SCALE).then_inc(s2_exp, 1)
                    if idx % 2 == 0 and st % 8 == 5 and st // 8 + 1 < HG:
                        negate_max(st // 8 + 1)
                if st >= 4 and st % 4 == 0:
                    evac_oT(st // 4 - 1, pv_mm, st)

            def evac_attnT(i):
                for b in range(B):
                    act.wait_ge(attn_tp, 2 * i + b + 1)
                    s.copy(attnT[:, b * SEQ:(b + 1) * SEQ], bank(b)).then_inc(attnT_ready, 1)

            evac_attnT(0)
            std_of(3)
            evac_xT(3, V_LN2)
            act.wait_ge(qc_mm, 2)
            s.activation(qcT, ps[:, 2:4, :].rearrange("p b t -> p (b t)"), ACT.Identity,
                         bias=vcol[:, V_BCQ:V_BCQ + 1]).then_inc(qc_ready, 1)

            def cross_exp(un):
                act.wait_ge(c_sub, un + 1)
                s.activation(pc[un % 3], pc[un % 3], ACT.Exp, scale=QK_SCALE).then_inc(c_exp, 1)

            cross_exp(0)
            for un in range(2 * T):
                if un + 1 < 2 * T:
                    cross_exp(un + 1)
                t, half = un // 2, un % 2
                for j in range(2):
                    act.wait_ge(c_tp, 2 * un + j + 1)
                    h = 8 * half + 4 * j
                    s.copy(PT[t // TB][:, h:h + 4, (t % TB) * P:(t % TB + 1) * P],
                           ps[0:J, 4 + j, :].rearrange("p (h q) -> p h q", h=4)).then_inc(c_PT, 1)
                if 8 <= un < 8 + HG:
                    evac_oT(2 * HG + un - 8, c_pv, un - 7)
            for hg in range(HG):
                evac_oT(3 * HG + hg, c_pv, HG + hg + 1)
            evac_attnT(1)
            std_of(4)
            evac_xT(4, V_LN3)
            for b in range(B):
                for f in range(4):
                    act.wait_ge(ff_mm, 4 * b + f + 1)
                    s.activation(geluT[:, f, b * SEQ:(b + 1) * SEQ], bank(4 * b + f), ACT.Gelu,
                                 bias=vcol[:, V_BFF1 + f:V_BFF1 + f + 1]).then_inc(ff_gelu, 1)
            std_of(5)
            evac_xT(5, None)
            act.wait_ge(ln_out, 6 * T)
            s.copy(yparts[:, 0, :, :].rearrange("p t d -> p (t d)"), flat(xn)).then_inc(y_parts, 1)
            act.wait_ge(y_parts, 2)
            s.copy(yparts[:, 1, :, :].rearrange("p t d -> p (t d)"), flat(t2)).then_inc(y_parts, 1)
            route_exps(1, E1)
            for gr in range(NG):
                act.wait_ge(disp_mm, B * (gr + 1))
                bk = 6 * (gr % 2)
                s.copy(slots1T.rearrange("p (a e m) -> p a e m", a=2, m=M1)[:, :, :, C1 * gr:C1 * (gr + 1)],
                       ps[:, bk:bk + 2, 0:CG // 2].rearrange("p a (e c) -> p a e c", c=C1)).then_inc(slots1T_ready, 1)
            for e in range(E1):
                if e % 2 == 0:
                    act.wait_ge(h1_mm, e + 1)
                    if e >= 4:
                        act.wait_ge(ring_dma[e % 4], 16 * (e // 4))
                    s.copy(ring[e % 4], ps[0:M1, 2 + e % 4, :]).then_inc(h1_act, 1)
            for b in range(B):
                act.wait_ge(comb_tp, b + 1)
                s.copy(combT[:, b * SEQ:(b + 1) * SEQ], ps[0:E1, b, :]).then_inc(combT_ready, 1)

            def evac_hidden(c):
                gr, f = c // 4, c % 4
                act.wait_ge(hdisp_mm, c + 1)
                bk = chunk_bank(c)
                s.activation(hid1T[f].rearrange("p (a e m) -> p a e m", a=2, m=M1)[:, :, :, C1 * gr:C1 * (gr + 1)],
                             ps[:, bk:bk + 2, 0:CG // 2].rearrange("p a (e c) -> p a e c", c=C1),
                             ACT.Relu).then_inc(hid1T_ready, 1)

            for q in range(T + 1):
                u = q - 1
                if 1 <= q < T:
                    act.wait_ge(hid_ready, u + 1)
                    if u >= 4:
                        act.wait_ge(hdisp_mm, 4 * ((u - 4) // 2 + 1))
                    s.copy(hparts[u % 4][:, 0, :], hsum[u % 4]).then_inc(hid_p1, 1)
                if q < T:
                    act.wait_ge(hvar, q + 1)
                    s.activation(tmp8[:, q:q + 1], tmp8b[:, q:q + 1], ACT.Sqrt).then_inc(hstd, 1)
                if 1 <= q < T:
                    act.wait_ge(hid_r1, u + 1)
                    s.copy(hparts[u % 4][:, 1, :], hsum[u % 4]).then_inc(hid_p2, 1)
                if q >= 3:
                    evac_hidden(2 * (q - 3))
                    evac_hidden(2 * (q - 3) + 1)
            for c in range(2 * (T - 2), 4 * NG - 2):
                evac_hidden(c)
            for e in range(1, E1, 2):
                act.wait_ge(y1_mm, e + 1)
                s.copy(yrow1[:, e, :], ps[0:M1, 2 + e % 4, 0:D]).then_inc(y1_act, 1)
            for b in range(B):
                half = slice(b * TB, (b + 1) * TB)
                act.wait_ge(ln_stats, 12 + b + 1)
                s.activation(std[:, 0, half], var_eps[:, 0, half], ACT.Sqrt).then_inc(ln_std, 1)

        @block.vector
        def _(dve):
            me = Chain(dve, dve_self)
            v = nc.vector

            def stats(src, i, b, again=False):
                half = slice(b * TB, (b + 1) * TB)
                for t in range(b * TB, (b + 1) * TB):
                    me.step(v.bn_stats(st6[:, t, :], src[:, t, :]))
                me.wait()
                for t in range(b * TB, (b + 1) * TB):
                    me.step(v.bn_aggr(mv[:, t, :], st6[:, t, :]))
                me.wait()
                if again:
                    me.step(v.tensor_scalar(var_eps[:, 1, half], mv[:, half, 1], 0.01 + LN_EPS, LN_EPS * LN_EPS,
                                            ALU.mult, ALU.add))
                v.tensor_scalar(var_eps[:, 0, half], mv[:, half, 1], LN_EPS, None, ALU.add).then_inc(ln_stats, 1)

            def scale_of(src, dst, i, b, again=False):
                half = slice(b * TB, (b + 1) * TB)
                dve.wait_ge(ln_std, 2 * i + b + 1)
                k = 2 if again else 1
                me.link(v.reciprocal(rstds[:, 0:k, half], std[:, 0:k, half]))
                if again:
                    me.link(v.tensor_scalar(rstds[:, :, half], rstds[:, :, half], 0.1, None, ALU.mult))
                for t in range(b * TB, (b + 1) * TB):
                    v.tensor_scalar(dst[:, t, :], src[:, t, :], mv[:, t, 0:1], rstds[:, k - 1, t:t + 1],
                                    ALU.subtract, ALU.mult).then_inc(ln_out, 1)

            def layer_norm(src, dst, i, again=False):
                for b in range(B):
                    stats(src, i, b, again)
                for b in range(B):
                    scale_of(src, dst, i, b, again)

            dve.wait_ge(ld_x, 32)
            layer_norm(x0, xn, 0)
            dve.wait_ge(cx_tp, 1)
            me.step(v.tensor_copy(cxT[:, :], ps[:, 2, 0:B * J]))
            v.tensor_copy(wsim[:, :], ps[:, 2, B * J:B * J + 3]).then_inc(cxT_ready, 1)
            dve.wait_ge(cxT_ready, 1)
            v.tensor_scalar(rT[:, :], cxT[:, :], wsim[:, 2:3], wsim[:, 0:1], ALU.mult, ALU.add).then_inc(rT_ready, 1)
            v.tensor_scalar(imgT[:, :], cxT[:, :], 0.1, None, ALU.mult).then_inc(rT_ready, 1)
            dve.wait_ge(simrow_mm, 1)
            dve.wait_ge(ld_gate, 48)
            v.tensor_scalar(simrow[:, :], ps[0:1, 3, 0:B * J], bsim[:, 0:1], None, ALU.add).then_inc(simrow_ready, 1)
            dve.wait_ge(tanh_ready, 1)
            dve.wait_ge(ld_bias, 16 * N_BIAS)
            me.step(v.tensor_scalar(tg[:, 4:5], tg[:, 1:2], 10.0, None, ALU.mult))
            me.link(v.tensor_scalar(attn[:, 0, :], bias[:, R_QV, :], tg[:, 0:1], None, ALU.mult))
            me.step(v.tensor_tensor(xplus, x0, attn[:, 0:1, :].to_broadcast([P, T, D]), ALU.add))
            dve.wait_ge(sim_mm, 2)
            sim = ps[:, 2:4, 0:TB * J].rearrange("p b (t j) -> p b t j", j=J)
            mx = small[:, 0:T]
            v.tensor_reduce(mx.rearrange("p (b t) -> p b t", b=B), sim, AX.X, ALU.max).then_inc(simmax, 1)
            dve.wait_ge(simmax, 1)
            v.tensor_tensor(simA.rearrange("p (b t) j -> p b t j", b=B), sim,
                            mx.rearrange("p (b t) -> p b t", b=B).unsqueeze(3).to_broadcast([P, B, TB, J]),
                            ALU.subtract).then_inc(sim_sub, 1)
            dve.wait_ge(mrow_tp, 1)
            v.tensor_reduce(rowmax[:, :], ps[0:1, 0:2, :], AX.X, ALU.max).then_inc(mrow_max, 1)
            dve.wait_ge(mrow_mm, 1)
            v.tensor_tensor(small[:, 8:16].rearrange("p (b t) -> p b t", b=B), mx.rearrange("p (b t) -> p b t", b=B),
                            ps[:, 4, 0:B].unsqueeze(2).to_broadcast([P, B, TB]), ALU.subtract).then_inc(batt_sub, 1)
            dve.wait_ge(sim_exp, 1)
            me.link(v.tensor_reduce(small[:, 24:32], simA, AX.X, ALU.add))
            me.link(v.reciprocal(small[:, 32:40], small[:, 24:32]))
            v.tensor_tensor(simA, simA, small[:, 32:40].unsqueeze(2).to_broadcast([P, T, J]), ALU.mult).then_inc(sim_norm, 1)
            dve.wait_ge(batt_mm, 1)
            me.link(v.tensor_reduce(small[:, 40:42], ps[:, 4, 8:16].rearrange("p (b t) -> p b t", b=B), AX.X, ALU.add))
            me.link(v.reciprocal(small[:, 42:44], small[:, 40:42]))
            me.link(v.tensor_tensor(small[:, 44:46], ps[:, 5, 0:B], small[:, 42:44], ALU.mult))
            dve.wait_ge(ld_wqv, 16)
            for b in range(B):
                ins = v.scalar_tensor_tensor(out=w14[:, b, :], in0=wqv[:, 3, :], scalar=small[:, 44 + b:45 + b],
                                             in1=wqv[:, 0, :], op0=ALU.mult, op1=ALU.add)
            ins.then_inc(w14_ready, 1)
            for b in range(B):
                dve.wait_ge(hqT_ready, b + 1)
                half = slice(b * SEQ, (b + 1) * SEQ)
                v.tensor_tensor(prodT[:, half], hqT[:, half], xT[:, half], ALU.mult).then_inc(prodT_ready, 1)
            for b in range(B):
                dve.wait_ge(hcq_mm, b + 1)
                half = slice(b * TB, (b + 1) * TB)
                v.scalar_tensor_tensor(out=x1[:, half, :].rearrange("p t d -> p (t d)"), in0=bank(2 + b), scalar=tg[:, 0:1],
                                       in1=xplus[:, half, :].rearrange("p t d -> p (t d)"), op0=ALU.mult,
                                       op1=ALU.add).then_inc(x1_ready, 1)
                dve.wait_ge(x1_ready, b + 1)
                stats(x1, 1, b)

            col1 = small[:, 32:48].rearrange("p (k t) -> p k t", k=2)

            def one_hot_slots():
                for gr in range(NG):
                    for b in range(B):
                        tile = gr + TB * b
                        me.step(v.tensor_scalar(slot1h[gr + TB * b], slot_iota, col1[:, 0, tile:tile + 1], None,
                                                ALU.is_equal))
                    for b in range(B):
                        tile = gr + TB * b
                        me.wait(me.n - 1 + b)
                        v.scalar_tensor_tensor(out=slot1h[gr + TB * b], in0=slot_iota, scalar=col1[:, 1, tile:tile + 1],
                                               in1=slot1h[gr + TB * b], op0=ALU.is_equal,
                                               op1=ALU.add).then_inc(slot_onehot, 1)

            def route(i, E, C, logits, loc_of):
                def pte(tile):
                    return tile[:, 0:T * E].rearrange("p (t e) -> p t e", e=E)
                def over(x):
                    return x.unsqueeze(2).to_broadcast([P, T, E])
                revb = rev[:, 0:E].unsqueeze(1).to_broadcast([P, T, E])
                m2, e2, m1, km = rs[:, 0, :], rs[:, 1, :], rs[:, 2, :], rs[:, 3:5, :]
                dve.wait_ge(logits_mm, i + 1)
                me.link(v.tensor_reduce(m1, logits, AX.X, ALU.max))
                me.link(v.tensor_tensor(pte(rdl), logits, over(m1), ALU.subtract))
                me.link(v.scalar_tensor_tensor(out=pte(rkey), in0=pte(rdl), scalar=0.0, in1=revb,
                                               op0=ALU.is_equal, op1=ALU.mult))
                me.link(v.tensor_reduce(km[:, 0, :], pte(rkey), AX.X, ALU.max))
                me.link(v.tensor_tensor(pte(oh[0]), pte(rkey), over(km[:, 0, :]), ALU.is_equal))
                me.link(v.scalar_tensor_tensor(out=pte(rkey), in0=pte(oh[0]), scalar=-BIG, in1=pte(rdl),
                                               op0=ALU.mult, op1=ALU.add))
                v.tensor_reduce(m2, pte(rkey), AX.X, ALU.max).then_inc(route_sub, 1)
                dve.wait_ge(route_sub, i + 1)
                me.link(v.tensor_tensor(pte(rkey), pte(rkey), over(m2), ALU.is_equal))
                me.link(v.tensor_tensor(pte(rkey), pte(rkey), revb, ALU.mult))
                me.link(v.tensor_reduce(km[:, 1, :], pte(rkey), AX.X, ALU.max))
                v.tensor_tensor(pte(oh[1]), pte(rkey), over(km[:, 1, :]), ALU.is_equal).then_inc(onehot, 1)
                score, valid, pos, base = rs[:, 5:7, :], rs[:, 7:9, :], rs[:, 9:11, :], rs[:, 11:13, :]
                dve.wait_ge(route_exp, i + 1)
                me.link(v.tensor_reduce(rs[:, 13, :], pte(rtmp), AX.X, ALU.add))
                me.link(v.reciprocal(score[:, 0, :], rs[:, 13, :]))
                me.link(v.tensor_tensor(score[:, 1, :], score[:, 0, :], e2, ALU.mult))
                me.step(v.tensor_scalar(base, km, -float(C if i == 0 else M1), 32.0 * (C if i == 0 else M1), ALU.mult, ALU.add))
                dve.wait_ge(loc_mm, i + 1)
                for k in range(2):
                    me.link(v.tensor_tensor(pte(rkey), loc_of(k), pte(oh[k]), ALU.mult))
                    me.link(v.tensor_reduce(pos[:, k, :], pte(rkey), AX.X, ALU.add))
                me.link(v.tensor_scalar(valid, pos, float(C), None, ALU.is_lt))
                if i == 1:
                    me.link(v.tensor_tensor(base, base, group_row[:, :].unsqueeze(1).to_broadcast([P, 2, T]), ALU.add))
                else:
                    me.wait()
                skip = rs[:, 14:16, :]
                me.step(v.tensor_scalar(skip, valid, -SKIP, SKIP, ALU.mult, ALU.add))
                me.link(v.tensor_tensor(rkey[:, 0:16].rearrange("p (k t) -> p k t", k=2), pos, valid, ALU.mult))
                me.step(v.tensor_tensor(grow[i][:, :, :], rkey[:, 0:16].rearrange("p (k t) -> p k t", k=2), base, ALU.add))
                if i == 1:
                    me.link(v.tensor_scalar(col1, km, -float(C1), 32.0 * C1, ALU.mult, ALU.add))
                    me.link(v.tensor_tensor(col1, col1, skip, ALU.add))
                    v.tensor_tensor(col1, col1, pos, ALU.add).then_inc(rows_ready, 1)
                    dve.wait_ge(rows_ready, 2)
                    one_hot_slots()
                else:
                    me.link(v.tensor_tensor(pos, pos, base, ALU.add))
                    v.tensor_tensor(srow0[:, :, :], pos, skip, ALU.add).then_inc(rows_ready, 1)
                g = gate[i][:, :, :]
                if i == 0:
                    me.link(v.tensor_tensor(rs[:, 13, :], score[:, 0, :], score[:, 1, :], ALU.add))
                    me.link(v.tensor_tensor(score, score, valid, ALU.mult))
                else:
                    me.link(v.tensor_tensor(score, score, valid, ALU.mult))
                    me.link(v.tensor_tensor(rs[:, 13, :], score[:, 0, :], score[:, 1, :], ALU.add))
                    me.link(v.tensor_scalar(rs[:, 13, :], rs[:, 13, :], 1e-9, None, ALU.max))
                me.link(v.reciprocal(rs[:, 2, :], rs[:, 13, :]))
                me.link(v.tensor_tensor(g, score, rs[:, 2:3, :].to_broadcast([P, 2, T]), ALU.mult))

            for b in range(B):
                scale_of(x1, xn, 1, b)
            route(0, E0, C0, ps[:, 2, 0:T * E0].rearrange("p (t e) -> p t e", e=E0),
                  lambda k: ps[:, 3 + k, 0:T * E0].rearrange("p (t e) -> p t e", e=E0))
            me.link(v.tensor_scalar(gate[0][:, :, :], gate[0][:, :, :], tg[:, 2:3], None, ALU.mult))
            dve.wait_ge(kc_mm, 2)
            v.tensor_tensor(vcaug[:, :, :, 0:HD], ps[0:J, 1, 0:B * D].rearrange("p (b h d) -> p b h d", b=B, h=NH),
                            bias[0:J, R_CV, :].rearrange("p (h d) -> p h d", h=NH).unsqueeze(1).to_broadcast([J, B, NH, HD]),
                            ALU.add).then_inc(vc_ready, 1)
            dve.wait_ge(vcol_ready, 1)
            for e in range(E0 + 1):
                if e < E0:
                    dve.wait_ge(h0_mm, 2 * e + 2)
                    if e >= 2:
                        dve.wait_ge(y0_mm, e - 1)
                    for f in (2, 3):
                        ins = v.tensor_scalar(hid0[e % 2][:, f, :], ps[:, 3 + 2 * (e % 2), (f - 2) * C0:(f - 1) * C0],
                                              vcol[:, V_B1 + 4 * e + f:V_B1 + 4 * e + f + 1], 0.0, ALU.add, ALU.max)
                    ins.then_inc(h0_dve, 1)
                if e >= 1:
                    dve.wait_ge(y0_mm, e)
                    v.tensor_tensor(yrow0[:, 2 * e - 2:2 * e, :], ps[:, 6 + (e - 1) % 2, 0:2 * D].rearrange("p (a d) -> p a d", a=2),
                                    b2_0[:, e - 1:e, :].to_broadcast([P, 2, D]), ALU.add).then_inc(y0_row, 1)
            for t in range(T):
                dve.wait_ge(gathered[t], 32)
                me.step(v.scalar_tensor_tensor(out=x1[:, t, :], in0=got0[:, t, 0, :], scalar=gate[0][:, 0, t:t + 1],
                                               in1=x1[:, t, :], op0=ALU.mult, op1=ALU.add))
                me.wait()
                v.scalar_tensor_tensor(out=x2[:, t, :], in0=got0[:, t, 1, :], scalar=gate[0][:, 1, t:t + 1],
                                       in1=x1[:, t, :], op0=ALU.mult, op1=ALU.add).then_inc(x2_ready, 1)
                if t % TB == TB - 1:
                    dve.wait_ge(x2_ready, t + 1)
                    stats(x2, 2, t // TB, again=True)

            for b in range(B):
                scale_of(x2, xn, 2, b, again=True)
            for t in range(T):
                me.step(v.tensor_scalar(xres[:, t, :], x2[:, t, :], mv[:, t, 0:1], rstds[:, 0, t:t + 1], ALU.subtract, ALU.mult))
            for n, full, parts in ((1, qf, qparts), (2, kf, kparts)):
                dve.wait_ge(qk_ready, n)
                me.link(v.tensor_tensor(full, full, parts[:, 0, :], ALU.subtract))
                v.tensor_copy(parts[:, 1, :], full).then_inc(qk_parts, 1)
                dve.wait_ge(qk_parts, 2 * n - 1)
                v.tensor_tensor(parts[:, 2, :], full, parts[:, 1, :], ALU.subtract).then_inc(qk_parts, 1)
            for b in range(B):
                dve.wait_ge(v_mm, b + 1)
                v.tensor_tensor(vaug[:, b * TB:(b + 1) * TB, :, 0:HD],
                                bank(6 + b).rearrange("p (t h d) -> p t h d", t=TB, h=NH),
                                bias[:, R_SV, :].rearrange("p (h d) -> p h d", h=NH).unsqueeze(1).to_broadcast([P, TB, NH, HD]),
                                ALU.add).then_inc(v_ready, 1)
            me.step(v.tensor_tensor(xres[:, :, :], xres[:, :, :], bias[:, R_SO:R_SO + 1, :].to_broadcast([P, T, D]), ALU.add))

            def row_max(n):
                hg, r = n // MU, n % MU
                dve.wait_ge(s1_mm, n + 1)
                col = T * (r % 4) + r // 4
                v.tensor_reduce(mcol[:, hg, col:col + 1], bank(4 + n % 2), AX.X, ALU.max).then_inc(s1_max, 1)

            def normalize(u, hg, b):
                dve.wait_ge(o_tp, u + 1)
                o = bank(7).rearrange("p (t h c) -> p t h c", t=TB, h=4)
                me.link(v.reciprocal(rden[:, :].rearrange("p (t h) -> p t h", h=4), o[:, :, :, HD]))
                v.tensor_tensor(attn[:, b * TB:(b + 1) * TB, 32 * hg:32 * hg + 32].rearrange("p t (h d) -> p t h d", h=4),
                                o[:, :, :, 0:HD],
                                rden[:, :].rearrange("p (t h) -> p t h", h=4).unsqueeze(3).to_broadcast([P, TB, 4, HD]),
                                ALU.mult).then_inc(o_norm, 1)

            for n in range(LEAD):
                row_max(n)
            n = LEAD
            for st in range(8 * HG + 1):
                for i in range(4):
                    if i == 3 and st % 4 == 2 and st >= 6:
                        u = (st - 6) // 4
                        normalize(u, u // 2, u % 2)
                    if n < MU * HG:
                        row_max(n)
                        n += 1
            normalize(2 * HG - 1, HG - 1, 1)
            for b in range(B):
                dve.wait_ge(proj_mm, b + 1)
                v.tensor_tensor(xa[:, b * TB:(b + 1) * TB, :].rearrange("p t d -> p (t d)"), bank(2 + b),
                                xres[:, b * TB:(b + 1) * TB, :].rearrange("p t d -> p (t d)"), ALU.add).then_inc(xa_ready, 1)
                dve.wait_ge(xa_ready, b + 1)
                stats(xa, 3, b)

            for b in range(B):
                scale_of(xa, xn, 3, b)
            me.step(v.tensor_tensor(xres[:, :, :], xa[:, :, :], bias[:, R_CO:R_CO + 1, :].to_broadcast([P, T, D]), ALU.add))

            for un in range(2 * T):
                dve.wait_ge(c_mm, un + 1)
                bk = 2 * (un % 2)
                sc = ps[:, bk:bk + 2, 0:4 * J].rearrange("p b (h j) -> p b h j", h=4)
                m = small[:, 0:8].rearrange("p (b h) -> p b h", b=2)
                me.link(v.tensor_reduce(m, sc, AX.X, ALU.max))
                if un >= 3:
                    dve.wait_ge(c_tp, 2 * un - 4)
                v.tensor_tensor(pc[un % 3].rearrange("p (b h) j -> p b h j", b=2), sc,
                                m.unsqueeze(3).to_broadcast([P, 2, 4, J]), ALU.subtract).then_inc(c_sub, 1)
                dve.wait_ge(c_sub, un + 1)
                if 11 <= un < 11 + HG:
                    normalize(2 * HG + un - 11, un - 11, 0)
            for hg in range(HG):
                normalize(3 * HG + hg, hg, 1)
            for b in range(B):
                dve.wait_ge(proj_mm, 2 + b + 1)
                v.tensor_tensor(xa[:, b * TB:(b + 1) * TB, :].rearrange("p t d -> p (t d)"), bank(2 + b),
                                xres[:, b * TB:(b + 1) * TB, :].rearrange("p t d -> p (t d)"), ALU.add).then_inc(xa_ready, 1)
                dve.wait_ge(xa_ready, 2 + b + 1)
                stats(xa, 4, b)

            for b in range(B):
                scale_of(xa, xn, 4, b)
            me.link(v.tensor_tensor(xres[:, :, :], xa[:, :, :], bias[:, R_FF2:R_FF2 + 1, :].to_broadcast([P, T, D]), ALU.add))
            me.link(v.scalar_tensor_tensor(out=flat(t1), in0=flat(xres), scalar=tg[:, 4:5], in1=flat(x2), op0=ALU.mult, op1=ALU.add))
            x4 = t3
            for b in range(B):
                half = slice(b * TB, (b + 1) * TB)
                dve.wait_ge(ff2_mm, b + 1)
                v.scalar_tensor_tensor(out=x4[:, half, :].rearrange("p t d -> p (t d)"), in0=bank(4 * b), scalar=tg[:, 4:5],
                                       in1=t1[:, half, :].rearrange("p t d -> p (t d)"), op0=ALU.mult,
                                       op1=ALU.add).then_inc(x4_ready, 1)
                dve.wait_ge(x4_ready, b + 1)
                stats(x4, 5, b)

            for b in range(B):
                scale_of(x4, xn, 5, b)
            lnw = bias[:, R_LNW, :]
            me.step(v.tensor_scalar(lnw, lnw, tg[:, 3:4], None, ALU.mult))
            me.link(v.tensor_scalar(bias[:, R_LNB, :], bias[:, R_LNB, :], tg[:, 3:4], None, ALU.mult))
            me.step(v.tensor_tensor(t1[:, :, :], x4[:, :, :], bias[:, R_LNB:R_LNB + 1, :].to_broadcast([P, T, D]), ALU.add))
            route(1, E1, C1, ps[:, 2, 0:T * E1].rearrange("p (t e) -> p t e", e=E1),
                  lambda k: ps[:, 3 + k, 0:T * E1].rearrange("p (t e) -> p t e", e=E1))
            ohe = [oh[k][:, :].rearrange("p (t e) -> p t e", e=E1) for k in range(2)]
            g1 = gate[1]
            me.step(v.tensor_tensor(comb[:, :, :], ohe[0], g1[:, 0, :].unsqueeze(2).to_broadcast([P, T, E1]), ALU.mult))
            kk = rkey[:, :].rearrange("p (t e) -> p t e", e=E1)
            me.link(v.tensor_tensor(kk, ohe[1], g1[:, 1, :].unsqueeze(2).to_broadcast([P, T, E1]), ALU.mult))
            v.tensor_tensor(comb[:, :, :], comb[:, :, :], kk, ALU.add).then_inc(comb_ready, 1)
            for e in range(1, E1, 2):
                dve.wait_ge(h1_mm, e + 1)
                if e >= 4:
                    dve.wait_ge(ring_dma[e % 4], 16 * (e // 4))
                v.tensor_copy(ring[e % 4], ps[0:M1, 2 + e % 4, :]).then_inc(h1_dve, 1)
            dve.wait_ge(ld_hid, 64)
            for q in range(T + 1):
                u = q - 1
                if q < T:
                    t = paired[q]
                    dve.wait_ge(gathered[t], 64)
                    dve.wait_ge(hb_mm, q + 1)
                    if q >= 4:
                        dve.wait_ge(hid_p3, q - 3)
                    first = me.step(v.scalar_tensor_tensor(out=hsum[q % 4], in0=got1[q % 4][:, 0, :], scalar=g1[:, 0, t:t + 1],
                                                           in1=bank(2 + q % 4), op0=ALU.mult, op1=ALU.add))
                if q >= 1:
                    dve.wait_ge(hstd, u + 1)
                    inverse = me.step(v.reciprocal(rstd[:, u:u + 1], tmp8[:, u:u + 1]))
                if q < T:
                    me.wait(first)
                    second = me.step(v.scalar_tensor_tensor(out=hsum[q % 4], in0=got1[q % 4][:, 1, :], scalar=g1[:, 1, t:t + 1],
                                                            in1=hsum[q % 4], op0=ALU.mult, op1=ALU.add))
                if q >= 1:
                    gi = paired[u] % TB
                    me.wait(inverse)
                    centred = me.step(v.scalar_tensor_tensor(out=got1[u % 4][:, 0, :], in0=hsum[u % 4], scalar=mv[:, u, 0:1],
                                                             in1=lnw_h[:, gi, :], op0=ALU.subtract, op1=ALU.mult))
                if q < T:
                    me.wait(second)
                    stat = me.step(v.bn_stats(st6[:, q, :], hsum[q % 4]))
                if q >= 1:
                    me.wait(centred)
                    v.scalar_tensor_tensor(out=hsum[u % 4], in0=got1[u % 4][:, 0, :], scalar=rstd[:, u:u + 1],
                                           in1=lnb_h[:, gi, :], op0=ALU.mult, op1=ALU.add).then_inc(hid_ready, 1)
                if q < T:
                    me.wait(stat)
                    me.link(v.bn_aggr(mv[:, q, :], st6[:, q, :]))
                    v.tensor_scalar(tmp8b[:, q:q + 1], mv[:, q, 1:2], MOE_EPS, None, ALU.add).then_inc(hvar, 1)
            last, parts = hsum[(T - 1) % 4], hparts[(T - 1) % 4]
            dve.wait_ge(hid_ready, T)
            dve.wait_ge(hdisp_mm, 4 * (NG - 2))
            me.link(v.tensor_copy(parts[:, 0, :], last))
            me.link(v.tensor_tensor(last, last, parts[:, 0, :], ALU.subtract))
            v.tensor_copy(parts[:, 1, :], last).then_inc(hid_last, 1)
            dve.wait_ge(hid_last, 1)
            v.tensor_tensor(parts[:, 2, :], last, parts[:, 1, :], ALU.subtract).then_inc(hid_last, 1)
            for f in (2, 3):
                c = 4 * (NG - 1) + f
                dve.wait_ge(hdisp_mm, c + 1)
                v.tensor_scalar(hid1T[f].rearrange("p (a e m) -> p a e m", a=2, m=M1)[:, :, :, C1 * (NG - 1):M1],
                                ps[:, chunk_bank(c):chunk_bank(c) + 2, 0:CG // 2].rearrange("p a (e c) -> p a e c", c=C1),
                                0.0, None, ALU.max).then_inc(hid1T_dve, 1)
            for e in range(0, E1, 2):
                dve.wait_ge(y1_mm, e + 1)
                v.tensor_copy(yrow1[:, e, :], ps[0:M1, 2 + e % 4, 0:D]).then_inc(y1_dve, 1)
            z = t2
            for b in range(B):
                half = slice(b * TB, (b + 1) * TB)
                dve.wait_ge(ob_mm, b + 1)
                me.link(v.tensor_tensor(z[:, half, :].rearrange("p t d -> p (t d)"), bank(6 + b),
                                        xn[:, half, :].rearrange("p t d -> p (t d)"), ALU.add))
            for b in range(B):
                half = slice(b * TB, (b + 1) * TB)
                for t in range(b * TB, (b + 1) * TB):
                    dve.wait_ge(gathered[t], 96)
                    me.link(v.scalar_tensor_tensor(out=z[:, t, :], in0=got2[:, t, 0, :], scalar=g1[:, 0, t:t + 1],
                                                   in1=z[:, t, :], op0=ALU.mult, op1=ALU.add))
                    me.link(v.scalar_tensor_tensor(out=z[:, t, :], in0=got2[:, t, 1, :], scalar=g1[:, 1, t:t + 1],
                                                   in1=z[:, t, :], op0=ALU.mult, op1=ALU.add))
                    me.link(v.bn_stats(st6[:, t, :], z[:, t, :]))
                    me.link(v.bn_aggr(mv[:, t, :], st6[:, t, :]))
                v.tensor_scalar(var_eps[:, 0, half], mv[:, half, 1], MOE_EPS, None, ALU.add).then_inc(ln_stats, 1)
                for t in range(b * TB, (b + 1) * TB):
                    me.step(v.scalar_tensor_tensor(out=z[:, t, :], in0=z[:, t, :], scalar=mv[:, t, 0:1], in1=lnw,
                                                   op0=ALU.subtract, op1=ALU.mult))
                dve.wait_ge(ln_std, 12 + b + 1)
                me.link(v.reciprocal(rstds[:, 0, half], std[:, 0, half]))
                for t in range(b * TB, (b + 1) * TB):
                    v.scalar_tensor_tensor(out=t3[:, t, :], in0=z[:, t, :], scalar=rstd[:, t:t + 1], in1=t1[:, t, :],
                                           op0=ALU.mult, op1=ALU.add).then_inc(out_ready, 1)

        @block.tensor
        def _(pe):
            m = nc.tensor

            def tp(dst, src, k):
                return m.transpose(dst, src, ident[0:k, 0:k])

            def transpose_tiles(src, ready, first, done):
                for b in range(B):
                    for s in range(TB):
                        if ready is not None:
                            pe.wait_ge(ready, first + b * TB + s + 1)
                        ins = tp(ps[:, b, s * P:(s + 1) * P], src[:, b * TB + s, :], P)
                    ins.then_inc(done, 1)

            pe.wait_ge(consts, 2)
            pe.wait_ge(ld_cx, 32)
            for b in range(B):
                tp(ps[:, 2, b * J:(b + 1) * J], cx[:, b, :], J)
            tp(ps[:, 2, B * J:B * J + 3], wsim_row[:, :], 3).then_inc(cx_tp, 1)
            pe.wait_ge(cxT_ready, 1)
            m.matmul(ps[0:1, 3, 0:B * J], wsim[:, 1:2], cxT[:, :], start=True, stop=True).then_inc(simrow_mm, 1)
            transpose_tiles(xn, ln_out, 0, ln_tp)
            pe.wait_ge(rT_ready, 2)
            pe.wait_ge(simrow_ready, 1)
            for b in range(B):
                pe.wait_ge(xT_ready, b + 1)
                for s in range(TB):
                    o = ps[:, 2 + b, s * J:(s + 1) * J]
                    m.matmul(o, xT[:, (b * TB + s) * P:(b * TB + s + 1) * P], rT[:, b * J:(b + 1) * J], start=True, stop=False)
                    ins = m.matmul(o, ones_f[0:1, :], simrow[0:1, b * J:(b + 1) * J], start=False, stop=True)
                ins.then_inc(sim_mm, 1)
            pe.wait_ge(simmax, 1)
            for t in range(T):
                ins = tp(ps[0:1, t // TB, (t % TB) * P:(t % TB + 1) * P], small[:, t:t + 1], P)
            ins.then_inc(mrow_tp, 1)
            pe.wait_ge(mrow_max, 1)
            m.matmul(ps[:, 4, 0:B], ones_f[0:1, :], rowmax[0:1, :], start=True, stop=True).then_inc(mrow_mm, 1)
            pe.wait_ge(batt_exp, 1)
            m.matmul(ps[:, 4, 8:16], ones_f[:, :], small[:, 16:24], start=True, stop=True)
            for t in range(T):
                ins = m.matmul(ps[:, 5, t // TB:t // TB + 1], xn[:, t, :], small[:, 16 + t:17 + t],
                               start=(t % TB == 0), stop=(t % TB == TB - 1))
            ins.then_inc(batt_mm, 1)
            pe.wait_ge(sim_norm, 1)
            for t in range(T):
                ins = tp(ps[0:J, 6 + t // TB, (t % TB) * P:(t % TB + 1) * P], simA[:, t, :], P)
                if t % TB == TB - 1:
                    ins.then_inc(simT_tp, 1)
            for b in range(B):
                pe.wait_ge(simT_ready, b + 1)
                m.matmul(bank(b), cx[:, b, :], simT[:, b * SEQ:(b + 1) * SEQ], start=True, stop=True).then_inc(hq_mm, 1)
            pe.wait_ge(w14_ready, 1)
            for b in range(B):
                pe.wait_ge(prodT_ready, b + 1)
                for s in range(TB):
                    o = ps[:, 2 + b, s * P:(s + 1) * P]
                    c = slice((b * TB + s) * P, (b * TB + s + 1) * P)
                    m.matmul(o, xT[:, c], w14[:, b, :], start=True, stop=False)
                    m.matmul(o, hqT[:, c], wqv[:, 1, :], start=False, stop=False)
                    ins = m.matmul(o, prodT[:, c], wqv[:, 2, :], start=False, stop=True)
                ins.then_inc(hcq_mm, 1)

            transpose_tiles(xn, ln_out, T, ln_tp)
            pe.wait_ge(ld_wx, 16 * N_WX)
            for t in range(T):
                if t % TB == 0:
                    pe.wait_ge(xT_ready, 2 + t // TB + 1)
                ins = m.matmul(ps[:, 2, t * E0:(t + 1) * E0], xT[:, t * P:(t + 1) * P], wg0[:, :], start=True, stop=True)
            ins.then_inc(logits_mm, 1)
            pe.wait_ge(onehot, 1)
            o0 = [oh[k][:, 0:T * E0].rearrange("p (t e) -> p t e", e=E0) for k in range(2)]
            for k in range(2):
                loc = ps[:, 3 + k, 0:T * E0].rearrange("p (t e) -> p t e", e=E0)
                m.matmul(loc, before[:, :], o0[k], start=True, stop=False)
                for t in range(T - 1):
                    m.matmul(loc[:, t + 1:T, :], ones_b[:, :], o0[k][:, t:t + 1, :].to_broadcast([P, T - 1 - t, E0]),
                             start=False, stop=(k == 0 and t == T - 2))
                if k == 1:
                    for t in range(T):
                        ins = m.matmul(loc, ones_b[:, :], o0[0][:, t:t + 1, :].to_broadcast([P, T, E0]),
                                       start=False, stop=(t == T - 1))
            ins.then_inc(loc_mm, 1)
            pe.wait_ge(ld_vec, 16 * N_VEC)
            pe.wait_ge(qk_order, 3)
            tp(ps[:, 7, 0:NV], vrow[:, :], NV)
            tp(ps[:, 7, V_BSQ:V_BSK + 1], vrow_qk[:, :], 2).then_inc(cx_tp, 1)
            m.matmul(ps[:, 0, 0:B * J], wx[:, W_CK, :], imgT[:, :], start=True, stop=True).then_inc(kc_mm, 1)
            for b in range(B):
                ins = m.matmul(ps[0:J, 1, b * D:(b + 1) * D], imgT[:, b * J:(b + 1) * J], wx[:, W_CV, :], start=True, stop=True)
            ins.then_inc(kc_mm, 1)

            def slots0_transposes(c):
                pe.wait_ge(ld_slots[c], 16)
                if c == 0:
                    pe.wait_ge(kc_ready, 1)
                elif c == 1:
                    pe.wait_ge(vc_ready, 1)
                else:
                    pe.wait_ge(slots0T_ready, c - 1)
                for i in range(4):
                    ins = tp(ps[:, c % 2, i * P:(i + 1) * P], slots0[:, 4 * c + i, :], P)
                ins.then_inc(slots0_tp, 1)

            slots0_transposes(0)
            pe.wait_ge(ld_w0, 32)
            for e in range(E0 + 1):
                if e < E0:
                    if e % 2 == 0 and e // 2 + 1 < 4:
                        slots0_transposes(e // 2 + 1)
                    pe.wait_ge(slots0T_ready, e // 2 + 1)
                    for f in range(4):
                        if e >= 2 and f % 2 == 0:
                            pe.wait_ge(h0_dve if f else h0_act, e - 1)
                        elif e < 2 and f == 0:
                            pe.wait_ge(rows_ready, 1)
                        ins = m.matmul(ps[:, 2 + 2 * (e % 2) + f // 2, (f % 2) * C0:(f % 2 + 1) * C0],
                                       w1_0[:, e, f * P:(f + 1) * P], slots0T[:, e * C0:(e + 1) * C0], start=True, stop=True)
                        if f % 2:
                            ins.then_inc(h0_mm, 1)
                if e >= 1:
                    q = e - 1
                    pe.wait_ge(h0_act, q + 1)
                    pe.wait_ge(h0_dve, q + 1)
                    if q >= 2:
                        pe.wait_ge(y0_row, q - 1)
                    for r in range(2):
                        for f in range(4):
                            ins = m.matmul(ps[:, 6 + q % 2, r * D:(r + 1) * D], hid0[q % 2][:, f, r * P:(r + 1) * P],
                                           w2_0[:, 4 * q + f, :], start=(f == 0), stop=(f == 3))
                    ins.then_inc(y0_mm, 1)

            transpose_tiles(xn, ln_out, 2 * T, ln_tp)
            for w, bk in ((0, 2), (1, 4)):
                for b in range(B):
                    pe.wait_ge(xT_ready, 4 + b + 1)
                    m.matmul(bank(bk + b), wx_qk[:, w, :], xT[:, b * SEQ:(b + 1) * SEQ], start=True, stop=True).then_inc(qk_mm, 1)
            for b in range(B):
                for s in range(TB):
                    ins = m.matmul(ps[:, 6 + b, s * D:(s + 1) * D], xT[:, (b * TB + s) * P:(b * TB + s + 1) * P],
                                   wx[:, W_SV, :], start=True, stop=True)
                ins.then_inc(v_mm, 1)

            def score_row_tile(n):
                hg, r = n // MU, n % MU
                t, h = r // 4, 4 * hg + r % 4
                b = t // TB
                if n == 0:
                    pe.wait_ge(ld_qk[0], 16 * 9)
                elif n == MU:
                    pe.wait_ge(ld_qk[1], 16 * 6)
                if n >= 2:
                    pe.wait_ge(s1_max, n - 1)
                m.matmul(bank(4 + n % 2), Q9[0:KP, h, t * P:(t + 1) * P], K9[0:KP, h, b * SEQ:(b + 1) * SEQ],
                         start=True, stop=True).then_inc(s1_mm, 1)

            def max_transpose(hg, units):
                pe.wait_ge(s1_max, MU * (hg + 1))
                if units > 0:
                    pe.wait_ge(o_norm, units)
                tp(ps[0:MU, 7, 0:P], mcol[:, hg, :], P).then_inc(max_tp, 1)

            def score_pair(idx):
                st, pair = idx // 2, idx % 2
                hg, b, kt = st // 8, st % 8 // 4, st % 4
                if idx >= 2:
                    pe.wait_ge(s2_exp, idx - 1)
                for j in range(2):
                    h = 4 * hg + 2 * pair + j
                    k0 = b * SEQ + kt * P
                    ins = m.matmul(bank(2 * (idx % 2) + j), K9[0:KP, h, k0:k0 + P], Q9[0:KP, h, b * SEQ:(b + 1) * SEQ],
                                   start=True, stop=True)
                ins.then_inc(s2_mm, 1)

            def values(st):
                hg, b, kt, u = st // 8, st % 8 // 4, st % 4, st // 4
                pe.wait_ge(s2_exp, 2 * st + 2)
                if kt == 0 and u >= 1:
                    pe.wait_ge(oT_ready, u)
                for hh in range(4):
                    ins = m.matmul(ps[32 * hh:32 * hh + HD + 1, 6, :], vaug[:, b * TB + kt, 4 * hg + hh, :],
                                   probs[(2 * st + hh // 2) % 4][:, (hh % 2) * SEQ:(hh % 2 + 1) * SEQ],
                                   start=(kt == 0), stop=(kt == TB - 1))
                ins.then_inc(pv_mm, 1)

            def out_transposes(u):
                pe.wait_ge(oT_ready, u + 1)
                if u >= 1:
                    pe.wait_ge(o_norm, u)
                for s in range(TB):
                    ins = tp(ps[:, 7, s * P:(s + 1) * P], oT[u % 2][:, s * P:(s + 1) * P], P)
                ins.then_inc(o_tp, 1)

            pe.wait_ge(qk_ready, 2)
            pe.wait_ge(v_ready, 2)
            for n in range(MU):
                score_row_tile(n)
            max_transpose(0, 0)
            for n in range(MU, LEAD):
                score_row_tile(n)
            def row_tiles(n, count):
                for k in range(n, min(n + count, MU * HG)):
                    score_row_tile(k)

            for st in range(8 * HG + 1):
                n = LEAD + 4 * st
                if st < 8 * HG:
                    if st % 8 == 0:
                        pe.wait_ge(ld_max[st // 8], 16 * 3)
                    score_pair(2 * st)
                row_tiles(n, 1)
                if st % 8 == 5 and st // 8 + 1 < HG:
                    max_transpose(st // 8 + 1, 2 * (st // 8))
                if st < 8 * HG:
                    score_pair(2 * st + 1)
                row_tiles(n + 1, 1)
                if st >= 1:
                    values(st - 1)
                row_tiles(n + 2, 1)
                if st % 4 == 2 and st >= 6:
                    pe.wait_ge(max_neg, min(HG, 1 + (st + 3) // 8))
                    out_transposes(st // 4 - 1)
                row_tiles(n + 3, 1)
            out_transposes(2 * HG - 1)

            def project(i, w):
                pe.wait_ge(o_norm, 2 * HG * (i + 1))
                transpose_tiles(attn, None, 0, attn_tp)
                for b in range(B):
                    pe.wait_ge(attnT_ready, 2 * i + b + 1)
                    for s in range(TB):
                        ins = m.matmul(ps[:, 2 + b, s * D:(s + 1) * D], attnT[:, (b * TB + s) * P:(b * TB + s + 1) * P],
                                       wx[:, w, :], start=True, stop=True)
                    ins.then_inc(proj_mm, 1)

            project(0, W_SO)

            transpose_tiles(xn, ln_out, 3 * T, ln_tp)
            for b in range(B):
                pe.wait_ge(xT_ready, 6 + b + 1)
                m.matmul(bank(2 + b), wx[:, W_CQ, :], xT[:, b * SEQ:(b + 1) * SEQ], start=True, stop=True).then_inc(qc_mm, 1)
            pe.wait_ge(qc_ready, 1)
            pe.wait_ge(kbd_ready, 1)

            def cross_scores(un):
                t, half = un // 2, un % 2
                if un >= 2:
                    pe.wait_ge(c_sub, un - 1)
                for j in range(2):
                    h = 8 * half + 4 * j
                    ins = m.matmul(ps[:, 2 * (un % 2) + j, 0:4 * J], qcT[:, t * P:(t + 1) * P],
                                   kbd[:, t // TB, h:h + 4, :].rearrange("p h j -> p (h j)"), start=True, stop=True)
                ins.then_inc(c_mm, 1)

            def cross_values(b, hg):
                if hg == 0:
                    pe.wait_ge(c_PT, 16 * (b + 1))
                pe.wait_ge(oT_ready, 2 * HG + HG * b + hg)
                for hh in range(4):
                    ins = m.matmul(ps[32 * hh:32 * hh + HD + 1, 6, :], vcaug[:, b, 4 * hg + hh, :], PT[b][:, 4 * hg + hh, :],
                                   start=True, stop=True)
                ins.then_inc(c_pv, 1)

            cross_scores(0)
            cross_scores(1)
            for un in range(2 * T):
                if un + 2 < 2 * T:
                    cross_scores(un + 2)
                if 9 <= un < 9 + HG:
                    out_transposes(2 * HG + un - 9)
                if 8 <= un < 8 + HG:
                    cross_values(0, un - 8)
                pe.wait_ge(c_exp, un + 1)
                for j in range(2):
                    if un >= 1:
                        pe.wait_ge(c_PT, 2 * un - 1 + j)
                    for i in range(4):
                        ins = tp(ps[0:J, 4 + j, i * P:(i + 1) * P], pc[un % 3][:, 4 * j + i, :], P)
                    ins.then_inc(c_tp, 1)
            for hg in range(HG + 1):
                if hg < HG:
                    cross_values(1, hg)
                if hg >= 1:
                    out_transposes(3 * HG + hg - 1)
            project(1, W_CO)

            transpose_tiles(xn, ln_out, 4 * T, ln_tp)
            pe.wait_ge(ld_ff, 32)
            for b in range(B):
                pe.wait_ge(xT_ready, 8 + b + 1)
                for f in range(4):
                    if b == 0 and f == 1:
                        pe.wait_ge(xT_ready, 10)
                    m.matmul(bank(4 * b + f), ff1[:, f * P:(f + 1) * P], xT[:, b * SEQ:(b + 1) * SEQ],
                             start=True, stop=True).then_inc(ff_mm, 1)
            for b in range(B):
                pe.wait_ge(ff_gelu, 4 * (b + 1))
                for s in range(TB):
                    for f in range(4):
                        ins = m.matmul(ps[:, 4 * b, s * D:(s + 1) * D], geluT[:, f, (b * TB + s) * P:(b * TB + s + 1) * P],
                                       ff2[:, f, :], start=(f == 0), stop=(f == 3))
                ins.then_inc(ff2_mm, 1)

            transpose_tiles(xn, ln_out, 5 * T, ln_tp)
            for t in range(T):
                if t % TB == 0:
                    pe.wait_ge(xT_ready, 10 + t // TB + 1)
                ins = m.matmul(ps[:, 2, t * E1:(t + 1) * E1], xT[:, t * P:(t + 1) * P], wg1[:, :], start=True, stop=True)
            ins.then_inc(logits_mm, 1)
            pe.wait_ge(onehot, 2)
            o1 = [oh[k][:, :].rearrange("p (t e) -> p t e", e=E1) for k in range(2)]
            for k in range(2):
                loc = ps[:, 3 + k, 0:T * E1].rearrange("p (t e) -> p t e", e=E1)
                m.matmul(loc, before[:, :], o1[k], start=True, stop=False)
                m.matmul(loc[:, TB:T, :], ones_b[:, :], o1[k][:, 0:TB, :], start=False, stop=(k == 0))
                if k == 1:
                    for dst in (slice(0, TB), slice(TB, T)):
                        for src in (slice(0, TB), slice(TB, T)):
                            ins = m.matmul(loc[:, dst, :], ones_b[:, :], o1[0][:, src, :], start=False,
                                           stop=(dst.start == TB and src.start == TB))
            ins.then_inc(loc_mm, 1)

            pe.wait_ge(y_parts, 4)
            for gr in range(NG):
                if gr >= 2:
                    pe.wait_ge(slots1T_ready, gr - 1)
                for b in range(B):
                    pe.wait_ge(slot_onehot, B * gr + b + 1)
                    for part in range(3):
                        for half in range(2):
                            ins = m.matmul(ps[:, 6 * (gr % 2) + half, 0:CG // 2], yparts[:, part, gr + TB * b, :],
                                           slot1h[gr + TB * b][:, half * (CG // 2):(half + 1) * (CG // 2)],
                                           start=(b == 0 and part == 0), stop=(b == B - 1 and part == 2))
                    ins.then_inc(disp_mm, 1)
            pe.wait_ge(slots1T_ready, NG)
            pe.wait_ge(ld_W1, 16)
            for e in range(E1):
                if e >= 4:
                    pe.wait_ge(h1_dve if e % 2 else h1_act, (e - 4) // 2 + 1)
                m.matmul(ps[0:M1, 2 + e % 4, :], slots1T[:, e * M1:(e + 1) * M1], W1[:, e, :],
                         start=True, stop=True).then_inc(h1_mm, 1)
            pe.wait_ge(comb_ready, 1)
            for t in range(T):
                ins = tp(ps[0:E1, t // TB, (t % TB) * P:(t % TB + 1) * P], comb[:, t, :], P)
                if t % TB == TB - 1:
                    ins.then_inc(comb_tp, 1)
            pe.wait_ge(ld_hid, 64)
            pe.wait_ge(h1_act, E1 // 2)
            pe.wait_ge(h1_dve, E1 // 2)
            pe.wait_ge(combT_ready, 2)

            def hidden_bias(q):
                t = paired[q]
                if q >= 4:
                    pe.wait_ge(hvar, q - 3)
                m.matmul(bank(2 + q % 4), combT[:, t * P:(t + 1) * P], b1_1[:, :], start=True, stop=True).then_inc(hb_mm, 1)

            for q in range(4):
                hidden_bias(q)
            def dispatch_hidden(gr, f, b, part):
                for half in range(2):
                    ins = m.matmul(ps[:, chunk_bank(4 * gr + f) + half, 0:CG // 2],
                                   hparts[(2 * gr + b) % 4][:, part, f * P:(f + 1) * P],
                                   slot1h[gr + TB * b][:, half * (CG // 2):(half + 1) * (CG // 2)],
                                   start=(b == 0 and part == 0), stop=(b == B - 1 and part == 2))
                return ins

            for gr in range(NG - 1):
                if gr + 2 < NG:
                    hidden_bias(2 * gr + 4)
                    hidden_bias(2 * gr + 5)
                pe.wait_ge(hid_p2, 2 * gr + 2)
                pe.wait_ge(hid_p3, 2 * gr + 2)
                for f in range(4):
                    c = 4 * gr + f
                    if c >= 2:
                        pe.wait_ge(hid1T_ready, c - 1)
                    for b in range(B):
                        for part in range(3):
                            ins = dispatch_hidden(gr, f, b, part)
                    ins.then_inc(hdisp_mm, 1)
            gr = NG - 1
            pe.wait_ge(hid1T_ready, 4 * gr)
            pe.wait_ge(hvar, T)
            pe.wait_ge(hid_p2, T - 1)
            pe.wait_ge(hid_p3, T - 1)
            for part in range(3):
                for f in range(4):
                    dispatch_hidden(gr, f, 0, part)
            pe.wait_ge(hid_last, 1)
            for part in range(2):
                for f in range(4):
                    dispatch_hidden(gr, f, 1, part)
            pe.wait_ge(hid_last, 2)
            for f in range(4):
                dispatch_hidden(gr, f, 1, 2).then_inc(hdisp_mm, 1)
            pe.wait_ge(hid1T_ready, 4 * NG - 2)
            pe.wait_ge(hid1T_dve, 2)
            pe.wait_ge(ld_W2, 16)
            for e in range(E1):
                if e >= 4:
                    pe.wait_ge(y1_act if e % 2 else y1_dve, (e - 4) // 2 + 1)
                for f in range(4):
                    ins = m.matmul(ps[0:M1, 2 + e % 4, 0:D], hid1T[f][:, e * M1:(e + 1) * M1], W2[:, 4 * e + f, :],
                                   start=(f == 0), stop=(f == 3))
                ins.then_inc(y1_mm, 1)
            for t in range(T):
                ins = m.matmul(ps[:, 6 + t // TB, (t % TB) * D:(t % TB + 1) * D], combT[:, t * P:(t + 1) * P], b2_1[:, :],
                               start=True, stop=True)
                if t % TB == TB - 1:
                    ins.then_inc(ob_mm, 1)


def kernel(**inputs):
    import numpy as _np
    import concourse.bacc as _bacc
    from concourse import mybir as _mybir
    from concourse.bass_utils import run_bass_kernel_spmd as _run

    nc = _bacc.Bacc("TRN2", target_bir_lowering=False, num_devices=1)
    arrays, args = {}, {}
    for name, value in inputs.items():
        v = _np.ascontiguousarray(value)
        arrays[f"in_{name}_dram"] = v
        args[name] = nc.dram_tensor(f"in_{name}_dram", v.shape, _mybir.dt.from_np(v.dtype), kind="ExternalInput").ap()
    out = nc.dram_tensor("out_0_dram", (2, 512, 128), _mybir.dt.float32, kind="ExternalOutput").ap()
    flamingo_kernel(nc, args, out)
    r = _run(nc, [arrays], core_ids=[0])
    return r.results[0]["out_0_dram"]
```
